# Optimizing a Trainium2 kernel written in Bass

```python
import numpy as np
import jax
import jax.numpy as jnp

def _softmax(x, axis=-1):
    return jax.nn.softmax(x, axis=axis)

def _gelu(x):
    return jax.nn.gelu(x, approximate=True)

def _silu(x):
    return jax.nn.silu(x)

def _sigmoid(x):
    return jax.nn.sigmoid(x)

def _layernorm(x, axis=-1, eps=1e-05):
    m = jnp.mean(x, axis=axis, keepdims=True)
    v = jnp.var(x, axis=axis, keepdims=True)
    return (x - m) / jnp.sqrt(v + eps)

def _scatter_add(tgt, idx, src, axis=0):
    return tgt.at[idx].add(src)

def _segment_sum(src, seg, n):
    return jax.ops.segment_sum(src, seg, n)
kernel_name = 'mk_hybrid_d1_jaxref_r8_268060'

def setup_inputs(seed: int=0):
    np.random.seed(seed)
    _w = jnp.asarray

    def _L0_attn_a_setup():
        import jax, jax.numpy as jnp
        import numpy as np
        B, S = (2, 256)
        HIDDEN, MLP = (128, 256)
        N_STATE, DT_RANK, CONV_K = (16, 64, 4)

        def _causal_depthwise_conv(u, conv_w, conv_b):
            u_pad = jnp.pad(u, ((0, 0), (CONV_K - 1, 0), (0, 0)))
            seq = u.shape[1]
            y = sum((u_pad[:, k:k + seq, :] * conv_w[:, k] for k in range(CONV_K)))
            return y + conv_b

        def _selective_scan(u, A_log, x_proj_w, dt_proj_w, dt_proj_b, D_skip):
            xp = u @ x_proj_w
            delta = jax.nn.softplus(xp[..., :DT_RANK] @ dt_proj_w + dt_proj_b)
            Bm = xp[..., DT_RANK:DT_RANK + N_STATE]
            Cm = xp[..., DT_RANK + N_STATE:]
            A = -jnp.exp(A_log)
            dA = jnp.exp(delta[..., None] * A)
            dBu = delta[..., None] * Bm[:, :, None, :] * u[..., None]

            def step(h, inp):
                dA_t, dBu_t, C_t = inp
                h = dA_t * h + dBu_t
                y = jnp.einsum('bdn,bn->bd', h, C_t)
                return (h, y)
            h0 = jnp.zeros((u.shape[0], u.shape[2], N_STATE), u.dtype)
            _, ys = jax.lax.scan(step, h0, (dA.transpose(1, 0, 2, 3), dBu.transpose(1, 0, 2, 3), Cm.transpose(1, 0, 2)))
            return ys.transpose(1, 0, 2) + u * D_skip
        key = jax.random.key(seed)
        ks = jax.random.split(key, 14)
        s = 0.02
        return {'x': jax.random.normal(ks[0], (B, S, HIDDEN), jnp.float32), 'W1': jax.random.normal(ks[1], (HIDDEN, MLP), jnp.float32) * s, 'b1': jnp.zeros((MLP,), jnp.float32), 'W2': jax.random.normal(ks[2], (HIDDEN, MLP), jnp.float32) * s, 'b2': jnp.zeros((MLP,), jnp.float32), 'conv_w': jax.random.normal(ks[3], (MLP, CONV_K), jnp.float32) * s, 'conv_b': jnp.zeros((MLP,), jnp.float32), 'A_log': jnp.log(jnp.broadcast_to(jnp.arange(1, N_STATE + 1, dtype=jnp.float32), (MLP, N_STATE))), 'x_proj_w': jax.random.normal(ks[4], (MLP, DT_RANK + 2 * N_STATE), jnp.float32) * s, 'dt_proj_w': jax.random.normal(ks[5], (DT_RANK, MLP), jnp.float32) * s, 'dt_proj_b': jnp.full((MLP,), -4.0, jnp.float32), 'D_skip': jnp.ones((MLP,), jnp.float32), 'Wo': jax.random.normal(ks[6], (MLP, HIDDEN), jnp.float32) * s, 'bo': jnp.zeros((HIDDEN,), jnp.float32)}
    _L0_attn_a_in = _L0_attn_a_setup()

    def _L0_attn_b_setup():
        import jax, jax.numpy as jnp
        import numpy as np
        HID = 128
        NH = 16
        HD = HID // NH
        RD = int(HD * 0.25)
        B = 2
        S = 256
        ROPE_BASE = 10000.0

        def _rotary_tables(seq_len):
            inv_freq = 1.0 / ROPE_BASE ** (jnp.arange(0, RD, 2, dtype=jnp.float32) / RD)
            t = jnp.arange(seq_len, dtype=jnp.float32)
            freqs = jnp.outer(t, inv_freq)
            emb = jnp.concatenate([freqs, freqs], axis=-1)
            return (jnp.cos(emb)[None, None], jnp.sin(emb)[None, None])

        def _rotate_half(x):
            x1, x2 = jnp.split(x, 2, axis=-1)
            return jnp.concatenate([-x2, x1], axis=-1)
        key = jax.random.key(seed)
        ks = jax.random.split(key, 4)
        hidden_states = jax.random.normal(ks[0], (B, S, HID), jnp.float32)
        Wqkv = jax.random.normal(ks[1], (3 * HID, HID), jnp.float32) * HID ** (-0.5)
        bqkv = jnp.zeros((3 * HID,), jnp.float32)
        Wd = jax.random.normal(ks[2], (HID, HID), jnp.float32) * HID ** (-0.5)
        bd = jnp.zeros((HID,), jnp.float32)
        return {'hidden_states': hidden_states, 'Wqkv': Wqkv, 'bqkv': bqkv, 'Wd': Wd, 'bd': bd}
    _L0_attn_b_in = _L0_attn_b_setup()

    def _L0_ffn_setup():
        import jax, jax.numpy as jnp
        import numpy as np
        B, S, H, NH, E, F = (4, 128, 128, 16, 8, 512)
        D = H // NH
        EPS = 1e-05

        def _layernorm(x, g, b):
            mu = jnp.mean(x, axis=-1, keepdims=True)
            var = jnp.var(x, axis=-1, keepdims=True)
            return (x - mu) * jax.lax.rsqrt(var + EPS) * g + b
        key = jax.random.key(seed)
        ks = jax.random.split(key, 16)
        s = 0.02
        return {'x': jax.random.normal(ks[0], (B, S, H), jnp.float32), 'ln1_g': jnp.ones((H,), jnp.float32), 'ln1_b': jnp.zeros((H,), jnp.float32), 'ln2_g': jnp.ones((H,), jnp.float32), 'ln2_b': jnp.zeros((H,), jnp.float32), 'wq': jax.random.normal(ks[1], (H, H), jnp.float32) * s, 'bq': jnp.zeros((H,), jnp.float32), 'wk': jax.random.normal(ks[2], (H, H), jnp.float32) * s, 'bk': jnp.zeros((H,), jnp.float32), 'wv': jax.random.normal(ks[3], (H, H), jnp.float32) * s, 'bv': jnp.zeros((H,), jnp.float32), 'wo': jax.random.normal(ks[4], (H, H), jnp.float32) * s, 'bo': jnp.zeros((H,), jnp.float32), 'gate_w': jax.random.normal(ks[5], (H, E), jnp.float32) * s, 'gate_b': jnp.zeros((E,), jnp.float32), 'w1': jax.random.normal(ks[6], (E, H, F), jnp.float32) * s, 'b1': jnp.zeros((E, F), jnp.float32), 'w2': jax.random.normal(ks[7], (E, F, H), jnp.float32) * s, 'b2': jnp.zeros((E, H), jnp.float32)}
    _L0_ffn_in = _L0_ffn_setup()
    _d = {'L0_attn_a_x': _L0_attn_a_in['x'], 'L0_attn_a_W1': _L0_attn_a_in['W1'], 'L0_attn_a_b1': _L0_attn_a_in['b1'], 'L0_attn_a_W2': _L0_attn_a_in['W2'], 'L0_attn_a_b2': _L0_attn_a_in['b2'], 'L0_attn_a_conv_w': _L0_attn_a_in['conv_w'], 'L0_attn_a_conv_b': _L0_attn_a_in['conv_b'], 'L0_attn_a_A_log': _L0_attn_a_in['A_log'], 'L0_attn_a_x_proj_w': _L0_attn_a_in['x_proj_w'], 'L0_attn_a_dt_proj_w': _L0_attn_a_in['dt_proj_w'], 'L0_attn_a_dt_proj_b': _L0_attn_a_in['dt_proj_b'], 'L0_attn_a_D_skip': _L0_attn_a_in['D_skip'], 'L0_attn_a_Wo': _L0_attn_a_in['Wo'], 'L0_attn_a_bo': _L0_attn_a_in['bo'], 'L0_attn_b_Wqkv': _L0_attn_b_in['Wqkv'], 'L0_attn_b_bqkv': _L0_attn_b_in['bqkv'], 'L0_attn_b_Wd': _L0_attn_b_in['Wd'], 'L0_attn_b_bd': _L0_attn_b_in['bd'], 'L0_ffn_ln1_g': _L0_ffn_in['ln1_g'], 'L0_ffn_ln1_b': _L0_ffn_in['ln1_b'], 'L0_ffn_ln2_g': _L0_ffn_in['ln2_g'], 'L0_ffn_ln2_b': _L0_ffn_in['ln2_b'], 'L0_ffn_wq': _L0_ffn_in['wq'], 'L0_ffn_bq': _L0_ffn_in['bq'], 'L0_ffn_wk': _L0_ffn_in['wk'], 'L0_ffn_bk': _L0_ffn_in['bk'], 'L0_ffn_wv': _L0_ffn_in['wv'], 'L0_ffn_bv': _L0_ffn_in['bv'], 'L0_ffn_wo': _L0_ffn_in['wo'], 'L0_ffn_bo': _L0_ffn_in['bo'], 'L0_ffn_gate_w': _L0_ffn_in['gate_w'], 'L0_ffn_gate_b': _L0_ffn_in['gate_b'], 'L0_ffn_w1': _L0_ffn_in['w1'], 'L0_ffn_b1': _L0_ffn_in['b1'], 'L0_ffn_w2': _L0_ffn_in['w2'], 'L0_ffn_b2': _L0_ffn_in['b2']}
    _x0 = _d['L0_attn_a_x']
    _d['L0_attn_a_x'] = jax.random.normal(jax.random.fold_in(jax.random.key(seed), 1), (4, 512, 128), dtype=_x0.dtype)
    del _x0
    return _d

def reference(L0_attn_a_x, L0_attn_a_W1, L0_attn_a_b1, L0_attn_a_W2, L0_attn_a_b2, L0_attn_a_conv_w, L0_attn_a_conv_b, L0_attn_a_A_log, L0_attn_a_x_proj_w, L0_attn_a_dt_proj_w, L0_attn_a_dt_proj_b, L0_attn_a_D_skip, L0_attn_a_Wo, L0_attn_a_bo, L0_attn_b_Wqkv, L0_attn_b_bqkv, L0_attn_b_Wd, L0_attn_b_bd, L0_ffn_ln1_g, L0_ffn_ln1_b, L0_ffn_ln2_g, L0_ffn_ln2_b, L0_ffn_wq, L0_ffn_bq, L0_ffn_wk, L0_ffn_bk, L0_ffn_wv, L0_ffn_bv, L0_ffn_wo, L0_ffn_bo, L0_ffn_gate_w, L0_ffn_gate_b, L0_ffn_w1, L0_ffn_b1, L0_ffn_w2, L0_ffn_b2):

    def _L0_attn_a_ref(x, W1, b1, W2, b2, conv_w, conv_b, A_log, x_proj_w, dt_proj_w, dt_proj_b, D_skip, Wo, bo):
        import jax, jax.numpy as jnp
        import numpy as np
        B, S = (2, 256)
        HIDDEN, MLP = (128, 256)
        N_STATE, DT_RANK, CONV_K = (16, 64, 4)

        def _causal_depthwise_conv(u, conv_w, conv_b):
            u_pad = jnp.pad(u, ((0, 0), (CONV_K - 1, 0), (0, 0)))
            seq = u.shape[1]
            y = sum((u_pad[:, k:k + seq, :] * conv_w[:, k] for k in range(CONV_K)))
            return y + conv_b

        def _selective_scan(u, A_log, x_proj_w, dt_proj_w, dt_proj_b, D_skip):
            xp = u @ x_proj_w
            delta = jax.nn.softplus(xp[..., :DT_RANK] @ dt_proj_w + dt_proj_b)
            Bm = xp[..., DT_RANK:DT_RANK + N_STATE]
            Cm = xp[..., DT_RANK + N_STATE:]
            A = -jnp.exp(A_log)
            dA = jnp.exp(delta[..., None] * A)
            dBu = delta[..., None] * Bm[:, :, None, :] * u[..., None]

            def step(h, inp):
                dA_t, dBu_t, C_t = inp
                h = dA_t * h + dBu_t
                y = jnp.einsum('bdn,bn->bd', h, C_t)
                return (h, y)
            h0 = jnp.zeros((u.shape[0], u.shape[2], N_STATE), u.dtype)
            _, ys = jax.lax.scan(step, h0, (dA.transpose(1, 0, 2, 3), dBu.transpose(1, 0, 2, 3), Cm.transpose(1, 0, 2)))
            return ys.transpose(1, 0, 2) + u * D_skip
        gate = jax.nn.sigmoid(x @ W2 + b2)
        u = x @ W1 + b1
        u = jax.nn.sigmoid(_causal_depthwise_conv(u, conv_w, conv_b))
        y = _selective_scan(u, A_log, x_proj_w, dt_proj_w, dt_proj_b, D_skip)
        return y * gate @ Wo + bo

    def _L0_attn_b_ref(hidden_states, Wqkv, bqkv, Wd, bd):
        import jax, jax.numpy as jnp
        import numpy as np
        HID = 128
        NH = 16
        HD = HID // NH
        RD = int(HD * 0.25)
        B = 2
        S = 256
        ROPE_BASE = 10000.0

        def _rotary_tables(seq_len):
            inv_freq = 1.0 / ROPE_BASE ** (jnp.arange(0, RD, 2, dtype=jnp.float32) / RD)
            t = jnp.arange(seq_len, dtype=jnp.float32)
            freqs = jnp.outer(t, inv_freq)
            emb = jnp.concatenate([freqs, freqs], axis=-1)
            return (jnp.cos(emb)[None, None], jnp.sin(emb)[None, None])

        def _rotate_half(x):
            x1, x2 = jnp.split(x, 2, axis=-1)
            return jnp.concatenate([-x2, x1], axis=-1)
        b, s, _ = hidden_states.shape
        qkv = hidden_states @ Wqkv.T + bqkv
        qkv = qkv.reshape(b, s, 3, NH, HD).transpose(2, 0, 3, 1, 4)
        q, k, v = (qkv[0], qkv[1], qkv[2])
        cos, sin = _rotary_tables(s)
        q_rot, q_pass = (q[..., :RD], q[..., RD:])
        k_rot, k_pass = (k[..., :RD], k[..., RD:])
        q_rot = q_rot * cos + _rotate_half(q_rot) * sin
        k_rot = k_rot * cos + _rotate_half(k_rot) * sin
        q = jnp.concatenate([q_rot, q_pass], axis=-1)
        k = jnp.concatenate([k_rot, k_pass], axis=-1)
        scale = HD ** (-0.5)
        logits = jnp.einsum('bhqd,bhkd->bhqk', q, k) * scale
        causal_mask = jnp.triu(jnp.full((s, s), -jnp.inf, dtype=logits.dtype), 1)
        probs = jax.nn.softmax(logits + causal_mask, axis=-1)
        L = jnp.eye(s, dtype=probs.dtype) - jnp.tril(probs, -1)
        rhs = jnp.diagonal(probs, axis1=-2, axis2=-1)[..., None] * v
        A = jax.scipy.linalg.solve_triangular(L, rhs, lower=True)
        attn_output = A.transpose(0, 2, 1, 3).reshape(b, s, HID)
        return attn_output @ Wd.T + bd

    def _L0_ffn_ref(x, ln1_g, ln1_b, ln2_g, ln2_b, wq, bq, wk, bk, wv, bv, wo, bo, gate_w, gate_b, w1, b1, w2, b2):
        import jax, jax.numpy as jnp
        import numpy as np
        B, S, H, NH, E, F = (4, 128, 128, 16, 8, 512)
        D = H // NH
        EPS = 1e-05

        def _layernorm(x, g, b):
            mu = jnp.mean(x, axis=-1, keepdims=True)
            var = jnp.var(x, axis=-1, keepdims=True)
            return (x - mu) * jax.lax.rsqrt(var + EPS) * g + b
        b, s, h = x.shape
        hn = _layernorm(x, ln1_g, ln1_b)
        q = (hn @ wq + bq).reshape(b, s, NH, D).transpose(0, 2, 1, 3)
        k = (hn @ wk + bk).reshape(b, s, NH, D).transpose(0, 2, 1, 3)
        v = (hn @ wv + bv).reshape(b, s, NH, D).transpose(0, 2, 1, 3)
        scores = jnp.einsum('bhqd,bhkd->bhqk', q, k) / jnp.sqrt(jnp.float32(D))
        attn = jax.nn.softmax(scores, axis=-1)
        o = jnp.einsum('bhqk,bhkd->bhqd', attn, v)
        o = o.transpose(0, 2, 1, 3).reshape(b, s, h)
        x = x + (o @ wo + bo)
        hn2 = _layernorm(x, ln2_g, ln2_b).reshape(-1, h)
        logits = hn2 @ gate_w + gate_b
        idx = jnp.argmax(logits, axis=-1)
        mid = jax.nn.relu(jnp.einsum('th,ehf->etf', hn2, w1) + b1[:, None, :])
        y = jnp.einsum('etf,efh->eth', mid, w2) + b2[:, None, :]
        moe = y[idx, jnp.arange(hn2.shape[0])]
        return x + moe.reshape(b, s, h)
    x = L0_attn_a_x
    x = x + _L0_attn_a_ref(_layernorm(x, axis=-1), L0_attn_a_W1, L0_attn_a_b1, L0_attn_a_W2, L0_attn_a_b2, L0_attn_a_conv_w, L0_attn_a_conv_b, L0_attn_a_A_log, L0_attn_a_x_proj_w, L0_attn_a_dt_proj_w, L0_attn_a_dt_proj_b, L0_attn_a_D_skip, L0_attn_a_Wo, L0_attn_a_bo)
    x = x + _L0_ffn_ref(_layernorm(x, axis=-1), L0_ffn_ln1_g, L0_ffn_ln1_b, L0_ffn_ln2_g, L0_ffn_ln2_b, L0_ffn_wq, L0_ffn_bq, L0_ffn_wk, L0_ffn_bk, L0_ffn_wv, L0_ffn_bv, L0_ffn_wo, L0_ffn_bo, L0_ffn_gate_w, L0_ffn_gate_b, L0_ffn_w1, L0_ffn_b1, L0_ffn_w2, L0_ffn_b2)
    x = x + _L0_attn_b_ref(_layernorm(x, axis=-1), L0_attn_b_Wqkv, L0_attn_b_bqkv, L0_attn_b_Wd, L0_attn_b_bd)
    x = x + _L0_ffn_ref(_layernorm(x, axis=-1), L0_ffn_ln1_g, L0_ffn_ln1_b, L0_ffn_ln2_g, L0_ffn_ln2_b, L0_ffn_wq, L0_ffn_bq, L0_ffn_wk, L0_ffn_bk, L0_ffn_wv, L0_ffn_bv, L0_ffn_wo, L0_ffn_bo, L0_ffn_gate_w, L0_ffn_gate_b, L0_ffn_w1, L0_ffn_b1, L0_ffn_w2, L0_ffn_b2)
    return x

_drawn_inputs = setup_inputs


def setup_inputs(seed=0):
    import zlib

    import numpy as np

    out = dict(_drawn_inputs(seed))
    spreads = {'L0_attn_a_b1': (0.0, 0.8),
     'L0_attn_a_b2': (0.0, 0.8),
     'L0_attn_a_conv_b': (0.0, 0.8),
     'L0_attn_a_dt_proj_b': (-4.0, 0.6),
     'L0_attn_a_D_skip': (1.0, 0.6),
     'L0_attn_a_bo': (0.0, 0.1),
     'L0_attn_b_bqkv': (0.0, 0.1),
     'L0_attn_b_bd': (0.0, 0.1),
     'L0_ffn_ln1_g': (1.0, 0.6),
     'L0_ffn_ln1_b': (0.0, 0.8),
     'L0_ffn_ln2_g': (1.0, 0.2),
     'L0_ffn_ln2_b': (0.0, 0.307),
     'L0_ffn_bq': (0.0, 0.8),
     'L0_ffn_bk': (0.0, 0.8),
     'L0_ffn_bv': (0.0, 0.329),
     'L0_ffn_bo': (0.0, 0.1),
     'L0_ffn_gate_b': (0.0, 0.1),
     'L0_ffn_b1': (0.0, 0.325),
     'L0_ffn_b2': (0.0, 0.1)}
    factors = {'L0_attn_a_W1': 8.0,
     'L0_attn_a_W2': 4.566,
     'L0_attn_a_conv_w': 8.0,
     'L0_attn_a_A_log': 5.707,
     'L0_attn_a_x_proj_w': 6.351,
     'L0_attn_a_dt_proj_w': 8.0,
     'L0_ffn_wq': 8.0,
     'L0_ffn_wk': 8.0,
     'L0_ffn_wv': 4.43}
    for name, (base, spread) in spreads.items():
        noise = np.random.default_rng([zlib.crc32(name.encode()), seed]).standard_normal(out[name].shape)
        drawn = base * np.exp(spread * noise) if base else spread * noise
        out[name] = jnp.asarray(drawn.astype(out[name].dtype))
    for name, factor in factors.items():
        out[name] = (out[name] * factor).astype(out[name].dtype)
    return out
```

```python
from contextlib import ExitStack, contextmanager

import numpy as np

import concourse.bass as bass
import concourse.mybir as mybir

F32 = mybir.dt.float32
BF16 = mybir.dt.bfloat16
ALU = mybir.AluOpType
ACT = mybir.ActivationFunctionType
AX = mybir.AxisListType

P = 128
B, S, H = 4, 512, 128
T = B * S
TPB = S // P
TILES = T // P
EPS = 1e-5

MLP, N_STATE, DT_RANK, CONV_K = 256, 16, 64, 4
HALVES = MLP // P
NH, HD = 16, 8
E, F = 8, 512
FT = F // P
SCALE = float(HD) ** -0.5

VEC = {}
for _name, _n in (("b1", HALVES), ("b2", HALVES), ("conv_w", HALVES * CONV_K), ("conv_b", HALVES),
                  ("A_log", HALVES * N_STATE), ("dt_b", HALVES), ("D", HALVES),
                  ("ln1_g", 1), ("ln1_b", 1), ("ln2_g", 1), ("ln2_b", 1), ("bq", 1), ("bk", 1),
                  ("moe_b1", E * FT), ("dbq", 1), ("dbk", 1)):
    VEC[_name] = (sum(n for _, n in VEC.values()), _n)
NVEC = sum(n for _, n in VEC.values())
ROW = {}
for _name, _n in (("m_bo", H), ("f_bv", H), ("f_bo", H), ("gate_b", E), ("d_bv", H), ("d_bd", H)):
    ROW[_name] = (sum(n for _, n in ROW.values()), _n)
NROW = sum(n for _, n in ROW.values())


def lay_out(inputs):
    g = {k: np.asarray(v) for k, v in inputs.items()}

    def a(n):
        return g["L0_attn_a_" + n]

    def f(n):
        return g["L0_ffn_" + n]

    def d(n):
        return g["L0_attn_b_" + n]

    def halves(v):
        return v.reshape(HALVES, P, -1).transpose(1, 0, 2).reshape(P, -1)

    def padded_heads(m):
        wide = np.zeros((GROUPS, GROUP, HEAD_COLS, H), np.float32)
        wide[:, :, :HD] = m.reshape(GROUPS, GROUP, HD, H)
        return wide.reshape(GROUPS, P, H).transpose(1, 0, 2)

    def rotary(fn, other):
        angle = np.tile(np.arange(S, dtype=np.float32), (P, 1))
        return np.where((np.arange(P) % HD < 2)[:, None], fn(angle), np.float32(other)).astype(np.float32)

    bf16 = mybir.dt.np(BF16)
    cols = {"b1": halves(a("b1")), "b2": halves(a("b2")), "conv_w": halves(a("conv_w")),
            "conv_b": halves(a("conv_b")), "A_log": halves(a("A_log")), "dt_b": halves(a("dt_proj_b")),
            "D": halves(a("D_skip")), "ln1_g": f("ln1_g")[:, None], "ln1_b": f("ln1_b")[:, None],
            "ln2_g": f("ln2_g")[:, None], "ln2_b": f("ln2_b")[:, None], "bq": f("bq")[:, None],
            "bk": f("bk")[:, None], "moe_b1": f("b1").reshape(E * FT, P).T,
            "dbq": d("bqkv")[0:H, None], "dbk": d("bqkv")[H:2 * H, None]}
    rows = {"m_bo": a("bo"), "f_bv": f("bv"), "f_bo": f("bo"), "gate_b": f("gate_b"),
            "d_bv": d("bqkv")[2 * H:], "d_bd": d("bd")}
    arrays = {
        "in_L0_attn_a_x": g["L0_attn_a_x"],
        "vec": np.concatenate([cols[n] for n in VEC], axis=1),
        "rows": np.broadcast_to(np.concatenate([rows[n] for n in ROW])[None, :], (P, NROW)),
        "m_W1": a("W1"), "m_W2": a("W2"),
        "m_xp": a("x_proj_w").reshape(HALVES, P, -1).transpose(1, 0, 2),
        "m_dt": a("dt_proj_w"),
        "m_Wo": a("Wo").reshape(HALVES, P, H).transpose(1, 0, 2),
        "f_wq": f("wq"), "f_wk": f("wk"), "f_wv": f("wv"), "f_wo": f("wo"), "gate_w": f("gate_w"),
        "f_w1": f("w1").transpose(1, 0, 2), "f_w2": f("w2").reshape(E, FT, P, H).transpose(2, 0, 1, 3),
        "f_b2": f("b2"), "countdown": np.tile(E - np.arange(E, dtype=np.float32), (P, 1)),
        "d_wqkv": d("Wqkv").T, "d_wd": padded_heads(d("Wd").T),
        "cos": rotary(np.cos, 1.0), "sin": rotary(np.sin, 0.0) * np.where(np.arange(P) % HD == 0, -1, 1)[:, None].astype(np.float32),
        "head_sum": np.kron(np.eye(NH), np.ones((HD, 1))).astype(np.float32),
        "off_blocks": 1 - np.kron(np.eye(P // 16), np.ones((16, 16))).astype(np.float32),
        "ident_b": np.eye(P).astype(bf16), "mask_up": (np.triu(np.ones((P, P)), 1) * -1e30).astype(bf16),
        "mask_diag4": np.tile(np.triu(np.ones((P, P)), 0) * -1e30, (1, TPB)).astype(bf16),
        "ones_f": np.ones((P, HEAD_COLS), np.float32), "ones": np.ones((PARTS, NH * S), bf16),
        "ident": np.eye(P, dtype=np.float32),
        "pick": np.tile(np.eye(2 * N_STATE), (3, 1)).astype(mybir.dt.np(BF16)),
    }
    return {k: np.ascontiguousarray(v) for k, v in arrays.items()}


class Core:
    pass


def vec(core, name, k=0, n=1):
    c = VEC[name][0] + k
    return core.vec[:, c:c + n]


def row(core, name):
    c, n = ROW[name]
    return core.rows[:, c:c + n]


def load_phase(core, nc):
    loaded = core.sem("x_and_weights_loaded")
    with nc.Block() as block:
        @block.sync
        def _(sp):
            n = 0
            x_tiles = core.dram["in_L0_attn_a_x"].rearrange("b (n p) h -> p (b n) h", p=P)
            for dst, src in [(core.x[:, :, :], x_tiles)] + [(core.w[k], core.dram[k]) for k in core.w]:
                sp.dma_start(dst, src).then_inc(loaded, 16)
                n += 16
            sp.wait_ge(loaded, n)

        @block.vector
        def _(dve):
            nc.vector.memset(core.minus_half[:, :], -0.5)


def mamba_phase(core, nc):
    sem, x_sb = core.sem, core.x
    with ExitStack() as ctx:
        def sb(name, shape, dt=F32):
            return ctx.enter_context(nc.sbuf_tensor("m_" + name, shape, dt))

        ps = ctx.enter_context(nc.psum_tensor("m_ps", [P, 8, 512], F32))
        XT, U_IN, G_IN, XP, DT = 0, 1, 3, 5, 6
        DECAY, B_BANK, C_BANK, Y = 0, 4, 5, 6
        stats = sb("stats", [P, TPB, 6])
        mv = sb("mv", [P, TPB, 2])
        var_eps = sb("var_eps", [P, TPB])
        rstd = sb("rstd", [P, TPB])
        xn = sb("xn", [P, TPB, H])
        xnT = sb("xnT", [P, S])
        u_pad = sb("u_pad", [P, HALVES, S + CONV_K - 1])
        conv = sb("conv", [P, HALVES, S])
        gate = sb("gate", [P, HALVES, T])
        u = sb("u", [P, HALVES, T])
        delta = sb("delta", [P, HALVES, T])
        du = sb("du", [P, HALVES, T])
        dt_in = sb("dt_in", [DT_RANK, S])
        bc = sb("bc", [3 * 32, T], BF16)
        part = sb("part", [32, S], BF16)
        rest = sb("rest", [32, 2, S])
        z_neg = sb("z_neg", [P, HALVES, S])
        e_abs = sb("e_abs", [P, HALVES, S])
        one_e = sb("one_e", [P, HALVES, S])
        den = sb("den", [P, HALVES, S])
        ratio = sb("ratio", [P, HALVES, S])
        log_e = sb("log_e", [P, HALVES, S])
        A = sb("A", [P, HALVES, N_STATE])
        b_row = sb("b_row", [P, 2, S])
        drive = sb("drive", [P, 2, HALVES, S])
        h = sb("h", [P, 2, HALVES, S])
        hC = sb("hC", [P, 2, HALVES, S])
        yD = sb("yD", [P, HALVES, S])
        yg = sb("yg", [P, HALVES, S])

        names = ("passed pad_zeroed a_exp a_ready ln_stats ln_mv ln_var ln_rstd ln_done xT_ps xT_sb proj_ps u_in gate_out "
                 "conv_step conv_out u_out xp_ps dt_sb split dt_ps z_out z_abs e_out one_e_out den_out rden_out "
                 "log_out quot_out log1p_out delta_out du_out b_ps b_sb decay_out drive_out c_ps scan_out hC_out "
                 "y_ps yD_out yg_out o_ps o_added x_out")
        s = {n: sem("m_" + n) for n in names.split()}
        W1, W2, Wx, Wdt, Wo = (core.w[n] for n in ("m_W1", "m_W2", "m_xp", "m_dt", "m_Wo"))
        FREE = {"b_sb": 1, "decay": 2, "drive": 2, "hC_out": 1, "y_ps": 2, "x_out": 1}

        with nc.Block() as block:
            @block.gpsimd
            def _(pool):
                with pool.Fori(0, B) as b:
                    pool.wait_ge(s["ln_var"], b + 1)
                    nc.gpsimd.tensor_tensor(rstd[:, :], var_eps[:, :], core.minus_half[:, 0:TPB],
                                            ALU.pow).then_inc(s["ln_rstd"], 1)
                pool.sem_inc(s["drive_out"], FREE["drive"])
                with pool.Fori(0, B) as b:
                    now = bass.ds(b * S, S)
                    pool.wait_ge(s["du_out"], b + 1)
                    for n in range(N_STATE):
                        step = b * N_STATE + n
                        pool.wait_ge(s["b_sb"], step + 1 + FREE["b_sb"])
                        pool.wait_ge(s["scan_out"], step + 1)
                        pool.sem_inc(s["passed"], 1)
                        nc.gpsimd.tensor_tensor(drive[:, n % 2, :, :], du[:, :, now],
                                                b_row[:, n % 2, :].unsqueeze(1).to_broadcast([P, HALVES, S]),
                                                ALU.mult).then_inc(s["drive_out"], 1)

            @block.scalar
            def _(act):
                nc.scalar.activation(A[:, :, :], vec(core, "A_log", 0, HALVES * N_STATE).rearrange(
                    "p (a n) -> p a n", a=HALVES), ACT.Exp).then_inc(s["a_exp"], 1)
                act.wait_ge(s["pad_zeroed"], 1)
                with act.Fori(0, B) as b:
                    now = bass.ds(b * S, S)
                    act.wait_ge(s["xT_ps"], b + 1)
                    nc.scalar.copy(xnT[:, :], ps[:, XT, :]).then_inc(s["xT_sb"], 1)
                    act.wait_ge(s["proj_ps"], b + 1)
                    for k in range(HALVES):
                        nc.scalar.activation(u_pad[:, k, CONV_K - 1:], ps[:, U_IN + k, :], ACT.Identity,
                                             bias=vec(core, "b1", k)).then_inc(s["u_in"], 1)
                    for k in range(HALVES):
                        nc.scalar.activation(gate[:, k, now], ps[:, G_IN + k, :], ACT.Sigmoid,
                                             bias=vec(core, "b2", k)).then_inc(s["gate_out"], 1)
                    act.wait_ge(s["conv_out"], b + 1)
                    act.sem_inc(s["passed"], 1)
                    nc.scalar.activation(u[:, :, now], conv[:, :, :], ACT.Sigmoid).then_inc(s["u_out"], 1)
                with act.Fori(0, B) as b:
                    act.wait_ge(s["z_abs"], b + 1)
                    nc.scalar.activation(e_abs[:, :, :], z_neg[:, :, :], ACT.Exp).then_inc(s["e_out"], 1)
                    act.wait_ge(s["one_e_out"], b + 1)
                    nc.scalar.activation(log_e[:, :, :], one_e[:, :, :], ACT.Ln).then_inc(s["log_out"], 1)
                act.wait_ge(s["a_ready"], 1)
                act.sem_inc(s["b_sb"], FREE["b_sb"])
                with act.Fori(0, B) as b:
                    now = bass.ds(b * S, S)
                    act.wait_ge(s["delta_out"], b + 1)
                    for n in range(N_STATE):
                        step = b * N_STATE + n
                        act.wait_ge(s["b_ps"], step + 1)
                        act.wait_ge(s["drive_out"], step + 1)
                        nc.scalar.copy(b_row[:, n % 2, :], ps[:, B_BANK, :]).then_inc(s["b_sb"], 1)
                        act.wait_ge(s["scan_out"], step + 1)
                        act.sem_inc(s["passed"], 1)
                        for k in range(HALVES):
                            last = nc.scalar.activation(ps[:, DECAY + HALVES * (n % 2) + k, :], delta[:, k, now],
                                                        ACT.Exp, scale=A[:, k, n:n + 1])
                        last.then_inc(s["decay_out"], 1)

            @block.vector
            def _(dve):
                nc.vector.memset(u_pad[:, :, 0:CONV_K - 1], 0.0).then_inc(s["pad_zeroed"], 1)
                dve.wait_ge(s["a_exp"], 1)
                nc.vector.tensor_scalar(A[:, :, :], A[:, :, :], -1.0, None, ALU.mult).then_inc(s["a_ready"], 1)
                with dve.Fori(0, B) as b:
                    for t in range(TPB):
                        last = nc.vector.bn_stats(stats[:, t, :], x_sb[:, b * TPB + t, :])
                    last.then_inc(s["ln_stats"], 1)
                    dve.wait_ge(s["ln_stats"], b + 1)
                    dve.sem_inc(s["passed"], 1)
                    for t in range(TPB):
                        last = nc.vector.bn_aggr(mv[:, t, :], stats[:, t, :])
                    last.then_inc(s["ln_mv"], 1)
                    dve.wait_ge(s["ln_mv"], b + 1)
                    nc.vector.tensor_scalar(var_eps[:, :], mv[:, :, 1], EPS, None, ALU.add).then_inc(s["ln_var"], 1)
                    dve.wait_ge(s["ln_rstd"], b + 1)
                    for t in range(TPB):
                        last = nc.vector.tensor_scalar(xn[:, t, :], x_sb[:, b * TPB + t, :], mv[:, t, 0:1],
                                                       rstd[:, t:t + 1], ALU.subtract, ALU.mult)
                    last.then_inc(s["ln_done"], 1)
                    dve.wait_ge(s["u_in"], HALVES * (b + 1))
                    for k in range(HALVES):
                        last = nc.vector.tensor_scalar(conv[:, k, :], u_pad[:, k, 0:S], vec(core, "conv_w", k * CONV_K),
                                                       vec(core, "conv_b", k), ALU.mult, ALU.add)
                    last.then_inc(s["conv_step"], 1)
                    for j in range(1, CONV_K):
                        dve.wait_ge(s["conv_step"], b * (CONV_K - 1) + j)
                        for k in range(HALVES):
                            last = nc.vector.scalar_tensor_tensor(
                                out=conv[:, k, :], in0=u_pad[:, k, j:j + S], scalar=vec(core, "conv_w", k * CONV_K + j),
                                in1=conv[:, k, :], op0=ALU.mult, op1=ALU.add)
                        last.then_inc(s["conv_step"] if j < CONV_K - 1 else s["conv_out"], 1)
                with dve.Fori(0, B) as b:
                    now = bass.ds(b * S, S)
                    dve.wait_ge(s["xp_ps"], b + 1)
                    nc.vector.tensor_copy(dt_in[:, :], ps[0:DT_RANK, XP, :]).then_inc(s["dt_sb"], 1)
                    src = ps[DT_RANK:DT_RANK + 2 * N_STATE, XP, :]
                    nc.vector.tensor_copy(part[:, :], src).then_inc(s["split"], 1)
                    dve.wait_ge(s["split"], 6 * b + 1)
                    nc.vector.tensor_copy(bc[0:32, now], part[:, :])
                    nc.vector.tensor_tensor(rest[:, 0, :], src, part[:, :], ALU.subtract).then_inc(s["split"], 1)
                    dve.wait_ge(s["split"], 6 * b + 2)
                    nc.vector.tensor_copy(part[:, :], rest[:, 0, :]).then_inc(s["split"], 1)
                    dve.wait_ge(s["split"], 6 * b + 3)
                    nc.vector.tensor_copy(bc[32:64, now], part[:, :]).then_inc(s["split"], 1)
                    nc.vector.tensor_tensor(rest[:, 1, :], rest[:, 0, :], part[:, :],
                                            ALU.subtract).then_inc(s["split"], 1)
                    dve.wait_ge(s["split"], 6 * b + 5)
                    nc.vector.tensor_copy(bc[64:96, now], rest[:, 1, :]).then_inc(s["split"], 1)
                    dve.wait_ge(s["dt_ps"], b + 1)
                    for k in range(HALVES):
                        last = nc.vector.tensor_scalar(delta[:, k, now], ps[:, DT + k, :], vec(core, "dt_b", k), None,
                                                       ALU.add)
                    last.then_inc(s["z_out"], 1)
                    dve.wait_ge(s["z_out"], b + 1)
                    nc.vector.scalar_tensor_tensor(out=z_neg[:, :, :], in0=delta[:, :, now], scalar=-1.0,
                                                   in1=delta[:, :, now], op0=ALU.mult,
                                                   op1=ALU.min).then_inc(s["z_abs"], 1)
                    dve.wait_ge(s["e_out"], b + 1)
                    nc.vector.tensor_scalar(one_e[:, :, :], e_abs[:, :, :], 1.0, None,
                                            ALU.add).then_inc(s["one_e_out"], 1)
                    dve.wait_ge(s["one_e_out"], b + 1)
                    nc.vector.tensor_scalar(den[:, :, :], one_e[:, :, :], -1.0, 2.0 ** -24, ALU.add,
                                            ALU.max).then_inc(s["den_out"], 1)
                    dve.wait_ge(s["den_out"], b + 1)
                    nc.vector.reciprocal(ratio[:, :, :], den[:, :, :]).then_inc(s["rden_out"], 1)
                    dve.wait_ge(s["rden_out"], b + 1)
                    dve.wait_ge(s["log_out"], b + 1)
                    nc.vector.scalar_tensor_tensor(out=den[:, :, :], in0=log_e[:, :, :], scalar=2.0 ** -24,
                                                   in1=ratio[:, :, :], op0=ALU.max,
                                                   op1=ALU.mult).then_inc(s["quot_out"], 1)
                    dve.wait_ge(s["quot_out"], b + 1)
                    nc.vector.tensor_tensor(ratio[:, :, :], den[:, :, :], e_abs[:, :, :],
                                            ALU.mult).then_inc(s["log1p_out"], 1)
                    dve.wait_ge(s["log1p_out"], b + 1)
                    nc.vector.scalar_tensor_tensor(out=delta[:, :, now], in0=delta[:, :, now], scalar=0.0,
                                                   in1=ratio[:, :, :], op0=ALU.max,
                                                   op1=ALU.add).then_inc(s["delta_out"], 1)
                    dve.wait_ge(s["delta_out"], b + 1)
                    nc.vector.tensor_tensor(du[:, :, now], delta[:, :, now], u[:, :, now],
                                            ALU.mult).then_inc(s["du_out"], 1)
                dve.sem_inc(s["scan_out"], FREE["decay"])
                dve.sem_inc(s["hC_out"], FREE["hC_out"])
                dve.sem_inc(s["x_out"], FREE["x_out"])
                with dve.Fori(0, B) as b:
                    now = bass.ds(b * S, S)
                    tiles = bass.ds(b * TPB, TPB)
                    for n in range(N_STATE):
                        step = b * N_STATE + n
                        dve.wait_ge(s["decay_out"], step + 1)
                        dve.wait_ge(s["drive_out"], step + 1 + FREE["drive"])
                        for k in range(HALVES):
                            last = nc.vector.tensor_tensor_scan(h[:, n % 2, k, :],
                                                                ps[:, DECAY + HALVES * (n % 2) + k, :],
                                                                drive[:, n % 2, k, :], 0.0, ALU.mult, ALU.add)
                        last.then_inc(s["scan_out"], 1)
                        dve.wait_ge(s["scan_out"], step + 1 + FREE["decay"])
                        dve.wait_ge(s["c_ps"], step + 1)
                        dve.wait_ge(s["y_ps"], step + 1)
                        nc.vector.tensor_tensor(hC[:, n % 2, :, :], h[:, n % 2, :, :],
                                                ps[:, C_BANK, :].unsqueeze(1).to_broadcast([P, HALVES, S]),
                                                ALU.mult).then_inc(s["hC_out"], 1)
                    dve.wait_ge(s["y_ps"], b * N_STATE + N_STATE + FREE["y_ps"])
                    for k in range(HALVES):
                        last = nc.vector.scalar_tensor_tensor(out=yD[:, k, :], in0=u[:, k, now],
                                                              scalar=vec(core, "D", k), in1=ps[:, Y + k, :],
                                                              op0=ALU.mult, op1=ALU.add)
                    last.then_inc(s["yD_out"], 1)
                    dve.wait_ge(s["yD_out"], b + 1)
                    nc.vector.tensor_tensor(yg[:, :, :], yD[:, :, :], gate[:, :, now], ALU.mult).then_inc(s["yg_out"], 1)
                    dve.wait_ge(s["o_ps"], b + 1)
                    nc.vector.tensor_tensor(x_sb[:, tiles, :], x_sb[:, tiles, :],
                                            ps[:, C_BANK, :].rearrange("p (t h) -> p t h", t=TPB),
                                            ALU.add).then_inc(s["o_added"], 1)
                    dve.wait_ge(s["o_added"], b + 1)
                    nc.vector.tensor_tensor(x_sb[:, tiles, :], x_sb[:, tiles, :],
                                            row(core, "m_bo").unsqueeze(1).to_broadcast([P, TPB, H]),
                                            ALU.add).then_inc(s["x_out"], 1)

            @block.tensor
            def _(pe):
                with pe.Fori(0, B) as b:
                    pe.wait_ge(s["ln_done"], b + 1)
                    for t in range(TPB):
                        last = nc.tensor.transpose(ps[:, XT, t * P:(t + 1) * P], xn[:, t, :], core.ident[:, :])
                    last.then_inc(s["xT_ps"], 1)
                    pe.wait_ge(s["xT_sb"], b + 1)
                    for k in range(HALVES):
                        nc.tensor.matmul(ps[:, U_IN + k, :], W1[:, k * P:(k + 1) * P], xnT[:, :], start=True, stop=True)
                    for k in range(HALVES):
                        last = nc.tensor.matmul(ps[:, G_IN + k, :], W2[:, k * P:(k + 1) * P], xnT[:, :],
                                                start=True, stop=True)
                    last.then_inc(s["proj_ps"], 1)
                with pe.Fori(0, B) as b:
                    now = bass.ds(b * S, S)
                    pe.wait_ge(s["u_out"], b + 1)
                    for k in range(HALVES):
                        last = nc.tensor.matmul(ps[0:DT_RANK + 2 * N_STATE, XP, :], Wx[:, k, :], u[:, k, now],
                                                start=(k == 0), stop=(k == HALVES - 1))
                    last.then_inc(s["xp_ps"], 1)
                    pe.wait_ge(s["dt_sb"], b + 1)
                    for k in range(HALVES):
                        last = nc.tensor.matmul(ps[:, DT + k, :], Wdt[:, k * P:(k + 1) * P], dt_in[:, :],
                                                start=True, stop=True)
                    last.then_inc(s["dt_ps"], 1)
                    pe.wait_ge(s["split"], 6 * b + 6)
                    pe.wait_ge(s["z_out"], b + 1)
                pe.sem_inc(s["y_ps"], FREE["y_ps"])
                with pe.Fori(0, B) as b:
                    now = bass.ds(b * S, S)

                    def spread(bank, r):
                        return nc.tensor.matmul(ps[:, bank, :], core.pick[:, r:r + 1].to_broadcast([96, P]),
                                                bc[:, now], start=True, stop=True)

                    for n in range(N_STATE):
                        step = b * N_STATE + n
                        if n == 0:
                            pe.wait_ge(s["du_out"], b + 1)
                            pe.wait_ge(s["b_sb"], step + FREE["b_sb"])
                            spread(B_BANK, n).then_inc(s["b_ps"], 1)
                            pe.wait_ge(s["x_out"], b + FREE["x_out"])
                            spread(C_BANK, N_STATE + n).then_inc(s["c_ps"], 1)
                        if n + 1 < N_STATE:
                            pe.wait_ge(s["b_sb"], step + 1 + FREE["b_sb"])
                            spread(B_BANK, n + 1).then_inc(s["b_ps"], 1)
                        pe.wait_ge(s["hC_out"], step + 1 + FREE["hC_out"])
                        if n + 1 < N_STATE:
                            spread(C_BANK, N_STATE + n + 1).then_inc(s["c_ps"], 1)
                        for k in range(HALVES):
                            last = nc.tensor.matmul(ps[:, Y + k, :], core.ident[:, :], hC[:, n % 2, k, :],
                                                    start=(n == 0), stop=(n == N_STATE - 1))
                        last.then_inc(s["y_ps"], 1)
                    pe.wait_ge(s["yg_out"], b + 1)
                    for t in range(TPB):
                        for k in range(HALVES):
                            last = nc.tensor.matmul(ps[:, C_BANK, t * H:(t + 1) * H], yg[:, k, t * P:(t + 1) * P],
                                                    Wo[:, k, :], start=(k == 0), stop=(k == HALVES - 1))
                    last.then_inc(s["o_ps"], 1)


def layer_norm_stats(nc, dve, pool_rstd, src, tiles, buf, s, pre, i):
    for t in range(tiles):
        last = nc.vector.bn_stats(buf["stats"][:, t, :], src(t))
    last.then_inc(s[pre + "_stats"], 1)
    dve.wait_ge(s[pre + "_stats"], i)
    dve.sem_inc(s["passed"], 1)
    for t in range(tiles):
        last = nc.vector.bn_aggr(buf["mv"][:, t, :], buf["stats"][:, t, :])
    last.then_inc(s[pre + "_mv"], 1)
    dve.wait_ge(s[pre + "_mv"], i)
    nc.vector.tensor_scalar(buf["var_eps"][:, :], buf["mv"][:, :, 1], EPS, None, ALU.add).then_inc(s[pre + "_var"], 1)
    dve.wait_ge(s[pre + "_rstd"], i)
    for t in range(tiles):
        last = nc.vector.tensor_scalar(buf["out"][:, t, :], src(t), buf["mv"][:, t, 0:1], buf["rstd"][:, t:t + 1],
                                       ALU.subtract, ALU.mult)
    last.then_inc(s[pre + "_done"], 1)


def layer_norm_rstd(nc, pool, core, buf, s, pre, i):
    pool.wait_ge(s[pre + "_var"], i)
    nc.gpsimd.tensor_tensor(buf["rstd"][:, :], buf["var_eps"][:, :], core.minus_half[:, 0:TPB],
                            ALU.pow).then_inc(s[pre + "_rstd"], 1)


LN_NAMES = ("stats", "mv", "var", "rstd", "done")
PARTS = 3
QK_ROWS = PARTS * PARTS * HD
SHIFT_ROWS = QK_ROWS + PARTS
HEAD_COLS = 32
GROUP = P // HEAD_COLS
GROUPS = NH // GROUP


def ffn_phase(core, nc, tag):
    x_sb = core.x
    with ExitStack() as ctx:
        def sb(name, shape, dt=F32):
            return ctx.enter_context(nc.sbuf_tensor(tag + name, shape, dt))

        ps = ctx.enter_context(nc.psum_tensor(tag + "ps", [P, 8, 512], F32))
        MAXQ, SCORE, O_BANK, MISC, MOE2 = (0, 1), (2, 3), 4, 5, (6, 7)
        ln = {}
        for n in ("ln0", "ln1", "ln2"):
            ln[n] = {"stats": sb(n + "stats", [P, TPB, 6]), "mv": sb(n + "mv", [P, TPB, 2]),
                     "var_eps": sb(n + "var", [P, TPB]), "rstd": sb(n + "rstd", [P, TPB]),
                     "out": sb(n + "out", [P, TPB, H])}
        hnT = sb("hnT", [P, S])
        qk = sb("qk", [P, 2, S])
        part = sb("part", [P, 2, PARTS, S], BF16)
        rest = sb("rest", [P, 2, 2, S])
        q_op = sb("q_op", [96, NH, S], BF16)
        k_op = sb("k_op", [96, NH, S], BF16)
        v_op = sb("v_op", [P, TPB, NH, HEAD_COLS])
        row_max = sb("row_max", [P, NH, TPB])
        max_part = sb("max_part", [NH * TPB, PARTS, P], BF16)
        max_rest = sb("max_rest", [NH * TPB, 2, P])
        e_sb = sb("e", [P, 2, GROUP, S])
        o_raw = sb("o_raw", [P, S])
        z_inv = sb("z_inv", [P, TPB, GROUP])
        o_nat = sb("o_nat", [P, TPB, NH, HD])
        oT = sb("oT", [P, S])
        x2 = sb("x2", [P, TPB, H])
        h2T = sb("h2T", [P, S])
        lg = sb("lg", [P, TPB, E])
        top = sb("top", [P, TPB])
        first = sb("first", [P, TPB])
        onehot = sb("onehot", [P, TPB, E])
        onehotT = sb("onehotT", [E, S])
        mid = sb("mid", [P, 2, FT, S])
        acc = sb("acc", [P, TPB, H])
        w1 = sb("w1", [P, E, F])
        w2 = sb("w2", [P, E, FT, H])

        names = ("passed weights_in ones_set v_zeroed hT_ps hT_sb qk_ps qk_sb split v_ps v_sb parts_stored q_loaded k_loaded "
                 "max_ps max_out mT_ps m_split m_stored m_loaded s_ps e_out pv_ps o_raw_out oT_ps z_out o_out "
                 "on_ps on_sb wo_ps x2_step x2_out h2_ps h2_sb lg_ps lg_out top_out tie_out rank_out pick_out hot_out "
                 "hotT_ps hotT_sb b2_ps acc_out up_ps mid_out down_ps x_out")
        s = {n: core.sem(tag + n) for n in names.split()}
        s.update({"ln_" + m: core.sem(tag + "ln_" + m) for m in LN_NAMES})
        w = core.w
        q_scr, k_scr, m_scr = core.q_scr, core.k_scr, core.m_scr
        HEADS_Q = NH * TPB
        STEPS = GROUPS * TPB

        with nc.Block() as block:
            @block.gpsimd
            def _(pool):
                with pool.Fori(0, B) as b:
                    layer_norm_rstd(nc, pool, core, ln["ln0"], s, "ln", 3 * b + 1)
                    layer_norm_rstd(nc, pool, core, ln["ln1"], s, "ln", 3 * b + 2)
                    pool.wait_ge(s["qk_sb"], 2 * b + 2)
                    for j in range(PARTS):
                        src = qk[:, :, :] if j == 0 else rest[:, :, j - 1, :]
                        pool.sem_inc(s["passed"], 1)
                        nc.gpsimd.tensor_copy(part[:, :, j, :], src).then_inc(s["split"], 1)
                        pool.wait_ge(s["split"], b * (2 * PARTS - 1) + 2 * j + 1)
                        if j < PARTS - 1:
                            nc.gpsimd.tensor_tensor(rest[:, :, j, :], src, part[:, :, j, :],
                                                    ALU.subtract).then_inc(s["split"], 1)
                            pool.wait_ge(s["split"], b * (2 * PARTS - 1) + 2 * j + 2)
                    layer_norm_rstd(nc, pool, core, ln["ln2"], s, "ln", 3 * b + 3)

            @block.sync
            def _(sp):
                sp.dma_start(w1[:, :, :], core.dram["f_w1"]).then_inc(s["weights_in"], 16)
                sp.dma_start(w2[:, :, :, :], core.dram["f_w2"]).then_inc(s["weights_in"], 16)
                with sp.Fori(0, B) as b:
                    sp.wait_ge(s["split"], (b + 1) * (2 * PARTS - 1))
                    for i, scr in enumerate((q_scr, k_scr)):
                        sp.dma_start(scr[b].rearrange("j r s -> r j s"), part[:, i, :, :]).then_inc(s["parts_stored"], 16)
                    sp.wait_ge(s["parts_stored"], 32 * (b + 1))
                    sp.wait_ge(s["ones_set"], 1)
                    for i in range(PARTS):
                        for j in range(PARTS):
                            r = (i * PARTS + j) * HD
                            sp.dma_start(q_op[r:r + HD, :, :],
                                         q_scr[b, i].rearrange("(h d) s -> d h s", d=HD)).then_inc(s["q_loaded"], 16)
                            sp.dma_start(k_op[r:r + HD, :, :],
                                         k_scr[b, j].rearrange("(h d) s -> d h s", d=HD)).then_inc(s["k_loaded"], 16)
                    sp.wait_ge(s["m_split"], 5 * (b + 1))
                    sp.dma_start(m_scr[b].rearrange("j r s -> r j s"), max_part[:, :, :]).then_inc(s["m_stored"], 16)
                    sp.wait_ge(s["m_stored"], 16 * (b + 1))
                    sp.dma_start(q_op[QK_ROWS:SHIFT_ROWS, :, :],
                                 m_scr[b].rearrange("j (h t) s -> j h (t s)", t=TPB)).then_inc(s["m_loaded"], 16)
                    sp.wait_ge(s["s_ps"], (b + 1) * STEPS * GROUP)
                    sp.sem_inc(s["passed"], 1)

            @block.scalar
            def _(act):
                act.sem_inc(s["e_out"], 2)
                act.sem_inc(s["o_raw_out"], 1)
                with act.Fori(0, B) as b:
                    act.wait_ge(s["qk_ps"], b + 1)
                    for i, n in enumerate(("bq", "bk")):
                        nc.scalar.activation(qk[:, i, :], ps[:, MOE2[i], :], ACT.Identity,
                                             bias=vec(core, n)).then_inc(s["qk_sb"], 1)

                    def leave(g):
                        act.wait_ge(s["pv_ps"], b * STEPS + g * TPB + TPB + 2)
                        act.wait_ge(s["oT_ps"], b * GROUPS + g + 1)
                        nc.scalar.copy(o_raw[:, :], ps[:, O_BANK, :]).then_inc(s["o_raw_out"], 1)

                    for q in range(STEPS):
                        act.wait_ge(s["pv_ps"], b * STEPS + q + 1)
                        for hh in range(GROUP):
                            i = q * GROUP + hh
                            act.wait_ge(s["s_ps"], b * STEPS * GROUP + i + 1)
                            nc.scalar.activation(e_sb[:, q % 2, hh, :], ps[:, SCORE[i % 2], :], ACT.Exp,
                                                 scale=SCALE).then_inc(s["e_out"], 1)
                        if q % TPB == 1 and q > TPB:
                            leave(q // TPB - 1)
                    leave(GROUPS - 1)
                    act.wait_ge(s["on_ps"], b + 1)
                    nc.scalar.copy(oT[:, :], ps[:, MISC, :]).then_inc(s["on_sb"], 1)
                    for e in range(E):
                        for f in range(FT):
                            i = e * FT + f
                            act.wait_ge(s["up_ps"], b * E * FT + i + 1)
                            if f == 0:
                                act.wait_ge(s["down_ps"], b * E + e + 1)
                            nc.scalar.activation(mid[:, e % 2, f, :], ps[:, MAXQ[i % 2], :], ACT.Relu,
                                                 bias=vec(core, "moe_b1", i)).then_inc(s["mid_out"], 1)
                        if e == 0:
                            act.wait_ge(s["hotT_ps"], b + 1)
                            nc.scalar.copy(onehotT[:, :], ps[0:E, MISC, :]).then_inc(s["hotT_sb"], 1)

            @block.vector
            def _(dve):
                nc.vector.memset(k_op[64:96, :, :], 1.0).then_inc(s["ones_set"], 1)
                nc.vector.memset(v_op[:, :, :, :], 0.0).then_inc(s["v_zeroed"], 1)
                dve.wait_ge(s["v_zeroed"], 1)
                nc.vector.memset(v_op[:, :, :, HD:HD + 1], 1.0).then_inc(s["v_zeroed"], 1)
                dve.sem_inc(s["max_out"], 2)
                dve.sem_inc(s["acc_out"], 2)
                with dve.Fori(0, B) as b:
                    layer_norm_stats(nc, dve, None, lambda t: x_sb[:, b * TPB + t, :], TPB, ln["ln0"], s, "ln", 3 * b + 1)
                    dve.wait_ge(s["ln_done"], 3 * b + 1)
                    layer_norm_stats(nc, dve, None, lambda t: ln["ln0"]["out"][:, t, :], TPB, ln["ln1"], s, "ln", 3 * b + 2)
                    dve.wait_ge(s["hT_ps"], b + 1)
                    nc.vector.tensor_scalar(hnT[:, :], ps[:, MISC, :], vec(core, "ln1_g"), vec(core, "ln1_b"),
                                            ALU.mult, ALU.add).then_inc(s["hT_sb"], 1)
                    dve.wait_ge(s["v_ps"], b + 1)
                    nc.vector.tensor_tensor(v_op[:, :, :, 0:HD],
                                            ps[:, MISC, :].rearrange("p (t h d) -> p t h d", t=TPB, d=HD),
                                            row(core, "f_bv").rearrange("p (h d) -> p h d", d=HD).unsqueeze(1)
                                            .to_broadcast([P, TPB, NH, HD]), ALU.add).then_inc(s["v_sb"], 1)
                    for i in range(HEADS_Q):
                        dve.wait_ge(s["max_ps"], b * HEADS_Q + i + 1)
                        nc.vector.tensor_reduce(row_max[:, i // TPB, i % TPB:i % TPB + 1], ps[:, MAXQ[i % 2], :], AX.X,
                                                ALU.max).then_inc(s["max_out"], 1)
                    dve.wait_ge(s["mT_ps"], b + 1)
                    minus = ps[0:HEADS_Q, MISC, 0:P]
                    nc.vector.tensor_scalar(max_part[:, 0, :], minus, -1.0, None, ALU.mult).then_inc(s["m_split"], 1)
                    dve.wait_ge(s["m_split"], 5 * b + 1)
                    nc.vector.scalar_tensor_tensor(out=max_rest[:, 0, :], in0=minus, scalar=-1.0, in1=max_part[:, 0, :],
                                                   op0=ALU.mult, op1=ALU.subtract).then_inc(s["m_split"], 1)
                    dve.wait_ge(s["m_split"], 5 * b + 2)
                    nc.vector.tensor_copy(max_part[:, 1, :], max_rest[:, 0, :]).then_inc(s["m_split"], 1)
                    dve.wait_ge(s["m_split"], 5 * b + 3)
                    nc.vector.tensor_tensor(max_rest[:, 1, :], max_rest[:, 0, :], max_part[:, 1, :],
                                            ALU.subtract).then_inc(s["m_split"], 1)
                    dve.wait_ge(s["m_split"], 5 * b + 4)
                    nc.vector.tensor_copy(max_part[:, 2, :], max_rest[:, 1, :]).then_inc(s["m_split"], 1)
                    for g in range(GROUPS):
                        dve.wait_ge(s["oT_ps"], b * GROUPS + g + 2)
                        o_ps = ps[:, MISC, :].rearrange("p (t h c) -> p t h c", t=TPB, c=HEAD_COLS)
                        nc.vector.reciprocal(z_inv[:, :, :], o_ps[:, :, :, HD]).then_inc(s["z_out"], 1)
                        dve.wait_ge(s["z_out"], b * GROUPS + g + 1)
                        nc.vector.tensor_tensor(o_nat[:, :, g * GROUP:(g + 1) * GROUP, :], o_ps[:, :, :, 0:HD],
                                                z_inv[:, :, :].unsqueeze(3).to_broadcast([P, TPB, GROUP, HD]),
                                                ALU.mult).then_inc(s["o_out"], 1)
                    dve.wait_ge(s["wo_ps"], b + 1)
                    nc.vector.tensor_tensor(x2[:, :, :], ps[:, MISC, :].rearrange("p (t h) -> p t h", t=TPB),
                                            ln["ln0"]["out"][:, :, :], ALU.add).then_inc(s["x2_step"], 1)
                    dve.wait_ge(s["x2_step"], b + 1)
                    nc.vector.tensor_tensor(x2[:, :, :], x2[:, :, :],
                                            row(core, "f_bo").unsqueeze(1).to_broadcast([P, TPB, H]),
                                            ALU.add).then_inc(s["x2_out"], 1)
                    dve.wait_ge(s["x2_out"], b + 1)
                    layer_norm_stats(nc, dve, None, lambda t: x2[:, t, :], TPB, ln["ln2"], s, "ln", 3 * b + 3)
                    dve.wait_ge(s["h2_ps"], b + 1)
                    nc.vector.tensor_scalar(h2T[:, :], ps[:, MISC, :], vec(core, "ln2_g"), vec(core, "ln2_b"),
                                            ALU.mult, ALU.add).then_inc(s["h2_sb"], 1)
                    dve.wait_ge(s["lg_ps"], b + 1)
                    nc.vector.tensor_tensor(lg[:, :, :], ps[:, MISC, 0:TPB * E].rearrange("p (t e) -> p t e", t=TPB),
                                            row(core, "gate_b").unsqueeze(1).to_broadcast([P, TPB, E]),
                                            ALU.add).then_inc(s["lg_out"], 1)
                    dve.wait_ge(s["lg_out"], b + 1)
                    nc.vector.tensor_reduce(top[:, :], lg[:, :, :], AX.X, ALU.max).then_inc(s["top_out"], 1)
                    dve.wait_ge(s["top_out"], b + 1)
                    nc.vector.tensor_tensor(lg[:, :, :], lg[:, :, :], top[:, :].unsqueeze(2).to_broadcast([P, TPB, E]),
                                            ALU.is_equal).then_inc(s["tie_out"], 1)
                    dve.wait_ge(s["tie_out"], b + 1)
                    down_count = w["countdown"].unsqueeze(1).to_broadcast([P, TPB, E])
                    nc.vector.tensor_tensor(lg[:, :, :], lg[:, :, :], down_count, ALU.mult).then_inc(s["rank_out"], 1)
                    dve.wait_ge(s["rank_out"], b + 1)
                    nc.vector.tensor_reduce(first[:, :], lg[:, :, :], AX.X, ALU.max).then_inc(s["pick_out"], 1)
                    dve.wait_ge(s["pick_out"], b + 1)
                    nc.vector.tensor_tensor(onehot[:, :, :], down_count,
                                            first[:, :].unsqueeze(2).to_broadcast([P, TPB, E]),
                                            ALU.is_equal).then_inc(s["hot_out"], 1)
                    dve.wait_ge(s["b2_ps"], b + 1)
                    nc.vector.tensor_tensor(acc[:, :, :], ps[:, MISC, :].rearrange("p (t h) -> p t h", t=TPB),
                                            x2[:, :, :], ALU.add).then_inc(s["acc_out"], 1)
                    for e in range(E):
                        dve.wait_ge(s["down_ps"], b * E + e + 1 + 2)
                        dve.wait_ge(s["acc_out"], b * (E + 1) + e + 1 + 2)
                        for t in range(TPB):
                            last = nc.vector.scalar_tensor_tensor(
                                out=acc[:, t, :], in0=ps[:, MOE2[e % 2], t * H:(t + 1) * H], scalar=onehot[:, t, e:e + 1],
                                in1=acc[:, t, :], op0=ALU.mult, op1=ALU.add)
                        last.then_inc(s["acc_out"], 1)
                    dve.wait_ge(s["acc_out"], (b + 1) * (E + 1) + 2)
                    tiles = bass.ds(b * TPB, TPB)
                    nc.vector.tensor_tensor(x_sb[:, tiles, :], x_sb[:, tiles, :], acc[:, :, :],
                                            ALU.add).then_inc(s["x_out"], 1)

            @block.tensor
            def _(pe):
                pe.wait_ge(s["v_zeroed"], 2)
                pe.wait_ge(s["ones_set"], 1)
                pe.sem_inc(s["pv_ps"], 2)
                pe.sem_inc(s["oT_ps"], 1)
                pe.sem_inc(s["down_ps"], 2)
                with pe.Fori(0, B) as b:
                    def turn(src, done):
                        for t in range(TPB):
                            last = nc.tensor.transpose(ps[:, MISC, t * P:(t + 1) * P], src(t), core.ident[:, :])
                        last.then_inc(done, 1)

                    pe.wait_ge(s["ln_done"], 3 * b + 2)
                    turn(lambda t: ln["ln1"]["out"][:, t, :], s["hT_ps"])
                    pe.wait_ge(s["hT_sb"], b + 1)
                    for i, n in enumerate(("f_wq", "f_wk")):
                        last = nc.tensor.matmul(ps[:, MOE2[i], :], w[n], hnT[:, :], start=True, stop=True)
                    last.then_inc(s["qk_ps"], 1)
                    for t in range(TPB):
                        last = nc.tensor.matmul(ps[:, MISC, t * H:(t + 1) * H], hnT[:, t * P:(t + 1) * P], w["f_wv"],
                                                start=True, stop=True)
                    last.then_inc(s["v_ps"], 1)
                    pe.wait_ge(s["q_loaded"], 16 * PARTS * PARTS * (b + 1))
                    pe.wait_ge(s["k_loaded"], 16 * PARTS * PARTS * (b + 1))
                    for i in range(HEADS_Q):
                        hd, t = i // TPB, i % TPB
                        pe.wait_ge(s["max_out"], b * HEADS_Q + i + 1)
                        nc.tensor.matmul(ps[:, MAXQ[i % 2], :], q_op[0:QK_ROWS, hd, t * P:(t + 1) * P],
                                         k_op[0:QK_ROWS, hd, :], start=True, stop=True).then_inc(s["max_ps"], 1)
                    pe.wait_ge(s["max_out"], (b + 1) * HEADS_Q + 2)
                    pe.sem_inc(s["passed"], 1)
                    nc.tensor.transpose(ps[0:HEADS_Q, MISC, 0:P], row_max[:, :, :].rearrange("p h t -> p (h t)"),
                                        core.ident[:, :]).then_inc(s["mT_ps"], 1)
                    pe.wait_ge(s["m_loaded"], 16 * (b + 1))

                    def scores(q):
                        g, t = q // TPB, q % TPB
                        for hh in range(GROUP):
                            hd, i = g * GROUP + hh, q * GROUP + hh
                            pe.wait_ge(s["e_out"], b * STEPS * GROUP + i + 1)
                            nc.tensor.matmul(ps[:, SCORE[i % 2], :], k_op[0:SHIFT_ROWS, hd, t * P:(t + 1) * P],
                                             q_op[0:SHIFT_ROWS, hd, :], start=True, stop=True).then_inc(s["s_ps"], 1)

                    def values(q):
                        g, t = q // TPB, q % TPB
                        pe.wait_ge(s["e_out"], b * STEPS * GROUP + (q + 1) * GROUP + 2)
                        if t == 0:
                            pe.wait_ge(s["o_raw_out"], b * GROUPS + g + 1)
                        for hh in range(GROUP):
                            last = nc.tensor.matmul(ps[hh * HEAD_COLS:(hh + 1) * HEAD_COLS, O_BANK, :],
                                                    v_op[:, t, g * GROUP + hh, :], e_sb[:, q % 2, hh, :],
                                                    start=(t == 0), stop=(t == TPB - 1))
                        last.then_inc(s["pv_ps"], 1)

                    def turn_group(g):
                        pe.wait_ge(s["o_raw_out"], b * GROUPS + g + 2)
                        if g > 0:
                            pe.wait_ge(s["o_out"], b * GROUPS + g)
                        turn(lambda t: o_raw[:, t * P:(t + 1) * P], s["oT_ps"])

                    for q in range(STEPS + 1):
                        if q < STEPS:
                            scores(q)
                        if q >= 1:
                            values(q - 1)
                        if q % TPB == 2 and q > TPB:
                            turn_group(q // TPB - 1)
                    turn_group(GROUPS - 1)
                    pe.wait_ge(s["o_out"], (b + 1) * GROUPS)
                    turn(lambda t: o_nat[:, t, :, :].rearrange("p h d -> p (h d)"), s["on_ps"])
                    pe.wait_ge(s["on_sb"], b + 1)
                    for t in range(TPB):
                        last = nc.tensor.matmul(ps[:, MISC, t * H:(t + 1) * H], oT[:, t * P:(t + 1) * P], w["f_wo"],
                                                start=True, stop=True)
                    last.then_inc(s["wo_ps"], 1)
                    pe.wait_ge(s["ln_done"], 3 * b + 3)
                    turn(lambda t: ln["ln2"]["out"][:, t, :], s["h2_ps"])
                    pe.wait_ge(s["h2_sb"], b + 1)
                    for t in range(TPB):
                        last = nc.tensor.matmul(ps[:, MISC, t * E:(t + 1) * E], h2T[:, t * P:(t + 1) * P], w["gate_w"],
                                                start=True, stop=True)
                    last.then_inc(s["lg_ps"], 1)

                    def up(e):
                        for f in range(FT):
                            i = e * FT + f
                            if i >= 2:
                                pe.wait_ge(s["mid_out"], b * E * FT + i - 1)
                            nc.tensor.matmul(ps[:, MAXQ[i % 2], :], w1[:, e, f * P:(f + 1) * P], h2T[:, :],
                                             start=True, stop=True).then_inc(s["up_ps"], 1)

                    def down(e):
                        pe.wait_ge(s["mid_out"], b * E * FT + (e + 1) * FT)
                        if e >= 2:
                            pe.wait_ge(s["acc_out"], b * (E + 1) + e + 2)
                        for t in range(TPB):
                            for f in range(FT):
                                last = nc.tensor.matmul(ps[:, MOE2[e % 2], t * H:(t + 1) * H],
                                                        mid[:, e % 2, f, t * P:(t + 1) * P], w2[:, e, f, :],
                                                        start=(f == 0), stop=(f == FT - 1))
                        last.then_inc(s["down_ps"], 1)

                    pe.wait_ge(s["weights_in"], 32)
                    up(0)
                    pe.wait_ge(s["hot_out"], b + 1)
                    for t in range(TPB):
                        last = nc.tensor.transpose(ps[0:E, MISC, t * P:(t + 1) * P], onehot[:, t, :], core.ident[:, :])
                    last.then_inc(s["hotT_ps"], 1)
                    pe.wait_ge(s["hotT_sb"], b + 1)
                    for t in range(TPB):
                        last = nc.tensor.matmul(ps[:, MISC, t * H:(t + 1) * H], onehotT[:, t * P:(t + 1) * P], w["f_b2"],
                                                start=True, stop=True)
                    last.then_inc(s["b2_ps"], 1)
                    for e in range(E):
                        if e + 1 < E:
                            up(e + 1)
                        down(e)
                    pe.wait_ge(s["x_out"], b + 1)


BLK = 16
BLKS = P // BLK
TURNS = BLKS - 1
OFF = [0, 3 * P, 5 * P]
OFF_COLS = 6 * P


def delta_phase(core, nc):
    x_sb = core.x
    with ExitStack() as ctx:
        def sb(name, shape, dt=F32):
            return ctx.enter_context(nc.sbuf_tensor("d_" + name, shape, dt))

        ps = ctx.enter_context(nc.psum_tensor("d_ps", [P, 8, 512], F32))
        MAXQ, SCORE, STEP, MISC, WIDE = (0, 1), (2, 3), 4, 5, (6, 7)
        ln = {"stats": sb("stats", [P, TPB, 6]), "mv": sb("mv", [P, TPB, 2]), "var_eps": sb("var", [P, TPB]),
              "rstd": sb("rstd", [P, TPB]), "out": sb("xh", [P, TPB, H])}
        hT = sb("hT", [P, S])
        early = sb("early", [P, 9 * S])
        qk, swap, rest = (early[:, i * S:(i + 2) * S].rearrange("p (i s) -> p i s", i=2) for i in (0, 2, 7))
        part = early[:, 4 * S:7 * S].bitcast(BF16).rearrange("p (i j s) -> p i j s", i=2, j=PARTS)
        e_blk, m_blk, prod, xz_blk = (early[:, i * S:(i + 2) * S].rearrange("p (t i j) -> p t i j", t=TPB, i=BLK)
                                      for i in (0, 2, 4, 6))
        shared = sb("shared", [P, NH * TPB * P])
        q_op = shared[0:96, 0:NH * S // 2].bitcast(BF16).rearrange("p (h s) -> p h s", h=NH)
        k_op = shared[0:96, NH * S // 2:NH * S].bitcast(BF16).rearrange("p (h s) -> p h s", h=NH)
        mT = shared[:, :].rearrange("p (h t i) -> p h t i", h=NH, t=TPB)
        vn = sb("vn", [P, TPB, NH, HD])
        row_max = sb("row_max", [P, NH, TPB])
        max_part = sb("max_part", [NH * TPB, PARTS, P], BF16)
        max_rest = sb("max_rest", [NH * TPB, 2, P])
        sii = sb("sii", [P, TPB, NH])
        eii = sb("eii", [P, TPB, NH])
        z_col = sb("z_col", [P, TPB, NH])
        zT = sb("zT", [TPB * NH, P])
        z_off = sb("z_off", [P, 3 * P])
        e_off = sb("e_off", [P, NH, OFF_COLS])
        e_nat = sb("e_nat", [P, NH, TPB, P])
        z_blk = sb("z_blk", [P, TPB, BLK])
        zi_blk = sb("zi_blk", [P, TPB, BLK])
        xT_blk = sb("xT_blk", [P, TPB, BLK, BLK])
        xT = sb("xT", [P, NH, TPB, P])
        g_nat = sb("g_nat", [P, NH, HEAD_COLS])
        late = e_nat[:, :, :, :].rearrange("p h t j -> p (h t j)")
        gT, xg, aT = (late[:, i * S:(i + 1) * S].rearrange("p (g i) -> p g i", g=GROUPS) for i in range(3))
        a_nat = late[:, 3 * S:4 * S].rearrange("p (h c) -> p h c", h=NH)
        a_all = late[:, 4 * S:(4 + TPB) * S].rearrange("p (t h c) -> p t h c", t=TPB, h=NH)

        names = ("passed set hT_ps hT_sb qk_ps qk_sb swapped rot1 rot2 rot3 split parts_stored q_loaded k_loaded v_ps v_sb "
                 "prod_out sii_ps sii_sb max_ps max_out mT_ps m_split m_stored m_loaded diff_out eii_out v_out "
                 "s_ps e_out sums_out zo_ps zo_sb zoT_ps z_out zT_ps zT_sb e_stored z_stored e_loaded z_loaded "
                 "zi_out blk_step x_stored x_loaded masked mt_ps mt_sb g_ps gT_sb gn_ps gn_sb at_ps at_sb an_ps an_sb "
                 "o_ps o_step x_out").split()
        s = {n: core.sem("d_" + n) for n in names}
        for m in LN_NAMES:
            s["ln_" + m] = core.sem("d_ln_" + m)
        w = core.w
        q_scr, k_scr, m_scr = core.q_scr, core.k_scr, core.m_scr
        e_scr, z_scr, x_scr = core.e_scr, core.z_scr, core.x_scr
        HEADS_Q = NH * TPB
        SCORE_GROUPS = GROUPS + 3 * GROUPS
        SCORES = SCORE_GROUPS * GROUP
        BLK_STEPS = 2 * (BLK - 1)

        def rows_first(t):
            return t.rearrange("p h t c -> p (h t) c")

        with nc.Block() as block:
            @block.gpsimd
            def _(pool):
                nc.gpsimd.memset(xT[:, :, :, :], 0.0).then_inc(s["set"], 1)
                with pool.Fori(0, B) as b:
                    layer_norm_rstd(nc, pool, core, ln, s, "ln", b + 1)
                    pool.wait_ge(s["rot3"], b + 1)
                    for j in range(PARTS):
                        src = qk[:, :, :] if j == 0 else rest[:, :, :]
                        pool.sem_inc(s["passed"], 1)
                        nc.gpsimd.tensor_copy(part[:, :, j, :], src).then_inc(s["split"], 1)
                        pool.wait_ge(s["split"], b * (2 * PARTS - 1) + 2 * j + 1)
                        if j < PARTS - 1:
                            nc.gpsimd.tensor_tensor(rest[:, :, :], src, part[:, :, j, :],
                                                    ALU.subtract).then_inc(s["split"], 1)
                            pool.wait_ge(s["split"], b * (2 * PARTS - 1) + 2 * j + 2)
                    pool.wait_ge(s["e_stored"], 16 * BLKS * (b + 1))
                    pool.wait_ge(s["sums_out"], NH * (b + 1))
                    for hd in range(NH):
                        nc.gpsimd.tensor_tensor(e_nat[:, hd, :, :], e_nat[:, hd, :, :],
                                                w["off_blocks"].unsqueeze(1).to_broadcast([P, TPB, P]),
                                                ALU.mult).then_inc(s["masked"], 1)

            @block.sync
            def _(sp):
                with sp.Fori(0, B) as b:
                    sp.wait_ge(s["split"], (b + 1) * (2 * PARTS - 1))
                    for i, scr in enumerate((q_scr, k_scr)):
                        sp.dma_start(scr[b].rearrange("j r s -> r j s"), part[:, i, :, :]).then_inc(s["parts_stored"], 16)
                    sp.wait_ge(s["parts_stored"], 32 * (b + 1))
                    for i in range(PARTS):
                        for j in range(PARTS):
                            r = (i * PARTS + j) * HD
                            sp.dma_start(q_op[r:r + HD, :, :],
                                         q_scr[b, i].rearrange("(h d) s -> d h s", d=HD)).then_inc(s["q_loaded"], 16)
                            sp.dma_start(k_op[r:r + HD, :, :],
                                         k_scr[b, j].rearrange("(h d) s -> d h s", d=HD)).then_inc(s["k_loaded"], 16)
                    sp.dma_start(k_op[QK_ROWS:SHIFT_ROWS, :, :],
                                 core.dram["ones"].rearrange("j (h s) -> j h s", h=NH)).then_inc(s["k_loaded"], 16)
                    sp.wait_ge(s["m_split"], 5 * (b + 1))
                    sp.dma_start(m_scr[b].rearrange("j r s -> r j s"), max_part[:, :, :]).then_inc(s["m_stored"], 16)
                    sp.wait_ge(s["m_stored"], 16 * (b + 1))
                    sp.dma_start(q_op[QK_ROWS:SHIFT_ROWS, :, :],
                                 m_scr[b].rearrange("j (h t) s -> j h (t s)", t=TPB)).then_inc(s["m_loaded"], 16)
                    sp.wait_ge(s["e_out"], b * SCORE_GROUPS * GROUP + NH + 2)
                    for k in range(BLKS):
                        own = slice(k * BLK, (k + 1) * BLK)
                        sp.dma_start(e_scr[b, k].rearrange("h t i j -> i (h t) j"),
                                     rows_first(e_nat[own, :, :, own])).then_inc(s["e_stored"], 16)
                    sp.wait_ge(s["e_stored"], 16 * BLKS * (b + 1))
                    sp.dma_start(e_blk[:, :, :, :], e_scr[b].rearrange("k h t i j -> (k h) t i j")).then_inc(s["e_loaded"], 16)
                    sp.wait_ge(s["zT_sb"], b + 1)
                    for t in range(TPB):
                        sp.dma_start(z_scr[b, :, :, t, :].rearrange("k h i -> h k i"),
                                     zT[t * NH:(t + 1) * NH, :].rearrange("h (k i) -> h k i", i=BLK)).then_inc(s["z_stored"], 16)
                    sp.wait_ge(s["z_stored"], 16 * TPB * (b + 1))
                    sp.dma_start(z_blk[:, :, :], z_scr[b].rearrange("k h t i -> (k h) t i")).then_inc(s["z_loaded"], 16)
                    sp.wait_ge(s["blk_step"], (b + 1) * (BLK_STEPS + 2))
                    sp.dma_start(x_scr[b].rearrange("k h t c i -> (k h) t c i"), xz_blk[:, :, :, :]).then_inc(s["x_stored"], 16)
                    sp.wait_ge(s["x_stored"], 16 * (b + 1))
                    for k in range(BLKS):
                        own = slice(k * BLK, (k + 1) * BLK)
                        sp.dma_start(rows_first(xT[own, :, :, own]),
                                     x_scr[b, k].rearrange("h t c i -> c (h t) i")).then_inc(s["x_loaded"], 16)
                    sp.wait_ge(s["x_out"], TPB * (b + 1))
                    sp.sem_inc(s["passed"], 1)

            @block.scalar
            def _(act):
                act.sem_inc(s["e_out"], 2)
                with act.Fori(0, B) as b:
                    act.wait_ge(s["hT_ps"], b + 1)
                    nc.scalar.copy(hT[:, :], ps[:, MISC, :]).then_inc(s["hT_sb"], 1)
                    act.wait_ge(s["qk_ps"], b + 1)
                    for i, n in enumerate(("dbq", "dbk")):
                        nc.scalar.activation(qk[:, i, :], ps[:, WIDE[i], :], ACT.Identity,
                                             bias=vec(core, n)).then_inc(s["qk_sb"], 1)
                    act.wait_ge(s["diff_out"], b + 1)
                    nc.scalar.activation(eii[:, :, :], sii[:, :, :], ACT.Exp, scale=SCALE).then_inc(s["eii_out"], 1)
                    for i in range(SCORES):
                        act.wait_ge(s["s_ps"], b * SCORE_GROUPS * GROUP + i + 1)
                        if i < NH:
                            out, n = e_nat[:, i, :, :].rearrange("p t j -> p (t j)"), S
                        else:
                            g, j, hh = (i - NH) // (3 * GROUP), (i - NH) // GROUP % 3, (i - NH) % GROUP
                            n = (3 - j) * P
                            out = e_off[:, g * GROUP + hh, OFF[j]:OFF[j] + n]
                        nc.scalar.activation(out, ps[:, SCORE[i % 2], 0:n], ACT.Exp, scale=SCALE).then_inc(s["e_out"], 1)
                    for g in range(GROUPS):
                        act.wait_ge(s["zo_ps"], b * GROUPS + g + 1)
                        nc.scalar.copy(z_off[:, :], ps[:, STEP, 0:3 * P]).then_inc(s["zo_sb"], 1)
                    act.wait_ge(s["zT_ps"], b + 1)
                    nc.scalar.copy(zT[:, :], ps[0:TPB * NH, MISC, 0:P]).then_inc(s["zT_sb"], 1)
                    for hd in range(NH):
                        act.wait_ge(s["mt_ps"], b * NH + hd + 1)
                        nc.scalar.copy(mT[:, hd, :, :].rearrange("p t i -> p (t i)"),
                                       ps[:, MAXQ[hd % 2], :]).then_inc(s["mt_sb"], 1)
                    for t in range(TPB):
                        first = (b * TPB + t) * BLKS
                        with act.Fori(0, TURNS) as k:
                            act.wait_ge(s["an_ps"], first + k + 1)
                            nc.scalar.copy(a_nat[:, :, :].rearrange("p h c -> p (h c)"),
                                           ps[:, MISC, :]).then_inc(s["an_sb"], 1)
                        act.wait_ge(s["an_ps"], first + BLKS)
                        nc.scalar.copy(a_all[:, t, :, :].rearrange("p h c -> p (h c)"),
                                       ps[:, MISC, :]).then_inc(s["an_sb"], 1)

            @block.vector
            def _(dve):
                nc.vector.memset(xT_blk[:, :, :, :], 0.0).then_inc(s["set"], 1)
                nc.vector.memset(g_nat[:, :, :], 0.0).then_inc(s["set"], 1)
                dve.wait_ge(s["set"], 3)
                for c in range(BLK):
                    last = nc.vector.memset(xT_blk[:, :, c, c:c + 1], 1.0)
                last.then_inc(s["set"], 1)
                dve.wait_ge(s["set"], 4)
                dve.sem_inc(s["max_out"], 2)
                swap_pairs = [i ^ 1 if i % HD < 2 else i for i in range(32)]
                with dve.Fori(0, B) as b:
                    layer_norm_stats(nc, dve, None, lambda t: x_sb[:, b * TPB + t, :], TPB, ln, s, "ln", b + 1)
                    dve.wait_ge(s["qk_sb"], 2 * b + 2)
                    dve.sem_inc(s["passed"], 1)
                    nc.vector.stream_shuffle(swap[:, :, :], qk[:, :, :], swap_pairs).then_inc(s["swapped"], 1)
                    dve.wait_ge(s["swapped"], b + 1)
                    nc.vector.tensor_tensor(qk[:, :, :], qk[:, :, :], w["cos"].unsqueeze(1).to_broadcast([P, 2, S]),
                                            ALU.mult).then_inc(s["rot1"], 1)
                    nc.vector.tensor_tensor(swap[:, :, :], swap[:, :, :], w["sin"].unsqueeze(1).to_broadcast([P, 2, S]),
                                            ALU.mult).then_inc(s["rot2"], 1)
                    dve.wait_ge(s["rot1"], b + 1)
                    dve.wait_ge(s["rot2"], b + 1)
                    nc.vector.tensor_tensor(qk[:, :, :], qk[:, :, :], swap[:, :, :], ALU.add).then_inc(s["rot3"], 1)
                    dve.wait_ge(s["rot3"], b + 1)
                    nc.vector.tensor_tensor(swap[:, 0, :], qk[:, 0, :], qk[:, 1, :], ALU.mult).then_inc(s["prod_out"], 1)
                    dve.wait_ge(s["v_ps"], b + 1)
                    nc.vector.tensor_tensor(vn[:, :, :, :],
                                            ps[:, MISC, :].rearrange("p (t h d) -> p t h d", t=TPB, d=HD),
                                            row(core, "d_bv").rearrange("p (h d) -> p h d", d=HD).unsqueeze(1)
                                            .to_broadcast([P, TPB, NH, HD]), ALU.add).then_inc(s["v_sb"], 1)
                    dve.wait_ge(s["sii_ps"], b + 1)
                    nc.vector.tensor_copy(sii[:, :, :], ps[:, MISC, 0:TPB * NH].rearrange("p (t h) -> p t h", t=TPB)).then_inc(
                        s["sii_sb"], 1)
                    for i in range(HEADS_Q):
                        n = (i % TPB + 1) * P
                        dve.wait_ge(s["max_ps"], b * HEADS_Q + i + 1)
                        nc.vector.tensor_reduce(row_max[:, i // TPB, i % TPB:i % TPB + 1], ps[:, MAXQ[i % 2], 0:n], AX.X,
                                                ALU.max).then_inc(s["max_out"], 1)
                    dve.wait_ge(s["max_out"], (b + 1) * HEADS_Q + 2)
                    dve.wait_ge(s["sii_sb"], b + 1)
                    nc.vector.tensor_tensor(sii[:, :, :], sii[:, :, :], row_max[:, :, :].rearrange("p h t -> p t h"),
                                            ALU.subtract).then_inc(s["diff_out"], 1)
                    dve.wait_ge(s["mT_ps"], b + 1)
                    minus = ps[0:HEADS_Q, MISC, 0:P]
                    nc.vector.tensor_scalar(max_part[:, 0, :], minus, -1.0, None, ALU.mult).then_inc(s["m_split"], 1)
                    dve.wait_ge(s["m_split"], 5 * b + 1)
                    nc.vector.scalar_tensor_tensor(out=max_rest[:, 0, :], in0=minus, scalar=-1.0, in1=max_part[:, 0, :],
                                                   op0=ALU.mult, op1=ALU.subtract).then_inc(s["m_split"], 1)
                    dve.wait_ge(s["m_split"], 5 * b + 2)
                    nc.vector.tensor_copy(max_part[:, 1, :], max_rest[:, 0, :]).then_inc(s["m_split"], 1)
                    dve.wait_ge(s["m_split"], 5 * b + 3)
                    nc.vector.tensor_tensor(max_rest[:, 1, :], max_rest[:, 0, :], max_part[:, 1, :],
                                            ALU.subtract).then_inc(s["m_split"], 1)
                    dve.wait_ge(s["m_split"], 5 * b + 4)
                    nc.vector.tensor_copy(max_part[:, 2, :], max_rest[:, 1, :]).then_inc(s["m_split"], 1)
                    dve.wait_ge(s["eii_out"], b + 1)
                    dve.wait_ge(s["v_sb"], b + 1)
                    nc.vector.tensor_tensor(vn[:, :, :, :], vn[:, :, :, :],
                                            eii[:, :, :].unsqueeze(3).to_broadcast([P, TPB, NH, HD]),
                                            ALU.mult).then_inc(s["v_out"], 1)
                    for hd in range(NH):
                        dve.wait_ge(s["e_out"], b * SCORE_GROUPS * GROUP + hd + 1 + 2)
                        nc.vector.tensor_reduce(z_col[:, :, hd], e_nat[:, hd, :, :], AX.X, ALU.add).then_inc(s["sums_out"], 1)
                    dve.wait_ge(s["sums_out"], (b + 1) * NH)
                    nc.vector.tensor_tensor(z_col[:, :, :], z_col[:, :, :], eii[:, :, :], ALU.add).then_inc(s["z_out"], 1)
                    dve.wait_ge(s["z_out"], b * (GROUPS + 1) + 1)
                    for g in range(GROUPS):
                        dve.wait_ge(s["zoT_ps"], b * GROUPS + g + 1)
                        heads = slice(g * GROUP, (g + 1) * GROUP)
                        nc.vector.tensor_tensor(
                            z_col[:, 1:TPB, heads], z_col[:, 1:TPB, heads],
                            ps[:, MISC, 0:3 * P].rearrange("p (t h c) -> p t h c", t=TPB - 1, c=HEAD_COLS)[:, :, :, 0],
                            ALU.add).then_inc(s["z_out"], 1)
                    done = b * (BLK_STEPS + 2)
                    dve.wait_ge(s["z_loaded"], 16 * (b + 1))
                    nc.vector.reciprocal(zi_blk[:, :, :], z_blk[:, :, :]).then_inc(s["zi_out"], 1)
                    dve.wait_ge(s["zi_out"], b + 1)
                    dve.wait_ge(s["e_loaded"], 16 * (b + 1))
                    nc.vector.tensor_tensor(m_blk[:, :, :, :], e_blk[:, :, :, :],
                                            zi_blk[:, :, :].unsqueeze(3).to_broadcast([P, TPB, BLK, BLK]),
                                            ALU.mult).then_inc(s["blk_step"], 1)
                    for i in range(1, BLK):
                        dve.wait_ge(s["blk_step"], done + 2 * i - 1)
                        nc.vector.tensor_tensor(prod[:, :, 0:i, 0:i], xT_blk[:, :, 0:i, 0:i],
                                                m_blk[:, :, i, 0:i].unsqueeze(2).to_broadcast([P, TPB, i, i]),
                                                ALU.mult).then_inc(s["blk_step"], 1)
                        dve.wait_ge(s["blk_step"], done + 2 * i)
                        nc.vector.tensor_reduce(xT_blk[:, :, 0:i, i], prod[:, :, 0:i, 0:i], AX.X,
                                                ALU.add).then_inc(s["blk_step"], 1)
                    dve.wait_ge(s["blk_step"], done + BLK_STEPS + 1)
                    nc.vector.tensor_tensor(xz_blk[:, :, :, :], xT_blk[:, :, :, :],
                                            zi_blk[:, :, :].unsqueeze(3).to_broadcast([P, TPB, BLK, BLK]),
                                            ALU.mult).then_inc(s["blk_step"], 1)
                    for t in range(TPB):
                        first = (b * TPB + t) * BLKS
                        if t == 0:
                            dve.wait_ge(s["v_out"], b + 1)
                            nc.vector.tensor_copy(g_nat[:, :, 0:HD], vn[:, t, :, :]).then_inc(s["gn_sb"], 1)
                        else:
                            dve.wait_ge(s["g_ps"], b * (TPB - 1) + t)
                            nc.vector.tensor_copy(gT[:, :, :].rearrange("p g i -> p (g i)"),
                                                  ps[:, STEP, :]).then_inc(s["gT_sb"], 1)
                            dve.wait_ge(s["gn_ps"], b * (TPB - 1) + t)
                            nc.vector.tensor_tensor(
                                g_nat[:, :, 0:HD], vn[:, t, :, :],
                                ps[:, MISC, :].rearrange("p (h c) -> p h c", c=HEAD_COLS)[:, :, 0:HD],
                                ALU.add).then_inc(s["gn_sb"], 1)
                        dve.wait_ge(s["at_ps"], first + 1)
                        nc.vector.tensor_copy(xg[:, :, :].rearrange("p g i -> p (g i)"), ps[:, STEP, :]).then_inc(s["at_sb"], 1)
                        dve.wait_ge(s["at_sb"], first + 1)
                        dve.sem_inc(s["passed"], 1)
                        with dve.Fori(1, BLKS) as k:
                            dve.wait_ge(s["at_ps"], first + k + 1)
                            nc.vector.tensor_tensor(aT[:, :, :].rearrange("p g i -> p (g i)"), ps[:, STEP, :],
                                                    xg[:, :, :].rearrange("p g i -> p (g i)"),
                                                    ALU.add).then_inc(s["at_sb"], 1)
                        dve.wait_ge(s["o_ps"], b * TPB + t + 1)
                        nc.vector.tensor_tensor(x_sb[:, b * TPB + t, :], x_sb[:, b * TPB + t, :], ps[:, WIDE[0], 0:H],
                                                ALU.add).then_inc(s["o_step"], 1)
                        dve.wait_ge(s["o_step"], b * TPB + t + 1)
                        nc.vector.tensor_tensor(x_sb[:, b * TPB + t, :], x_sb[:, b * TPB + t, :], row(core, "d_bd"),
                                                ALU.add).then_inc(s["x_out"], 1)

            @block.tensor
            def _(pe):
                pe.wait_ge(s["set"], 4)
                with pe.Fori(0, B) as b:
                    def turn(src, done, n=TPB):
                        for t in range(n):
                            last = nc.tensor.transpose(ps[:, MISC, t * P:(t + 1) * P], src(t), core.ident[:, :])
                        last.then_inc(done, 1)

                    pe.wait_ge(s["ln_done"], b + 1)
                    turn(lambda t: ln["out"][:, t, :], s["hT_ps"])
                    pe.wait_ge(s["hT_sb"], b + 1)
                    for i in range(2):
                        last = nc.tensor.matmul(ps[:, WIDE[i], :], w["d_wqkv"][:, i * H:(i + 1) * H], hT[:, :],
                                                start=True, stop=True)
                    last.then_inc(s["qk_ps"], 1)
                    for t in range(TPB):
                        last = nc.tensor.matmul(ps[:, MISC, t * H:(t + 1) * H], hT[:, t * P:(t + 1) * P],
                                                w["d_wqkv"][:, 2 * H:3 * H], start=True, stop=True)
                    last.then_inc(s["v_ps"], 1)
                    pe.wait_ge(s["prod_out"], b + 1)
                    pe.wait_ge(s["v_sb"], b + 1)
                    for t in range(TPB):
                        last = nc.tensor.matmul(ps[:, MISC, t * NH:(t + 1) * NH], swap[:, 0, t * P:(t + 1) * P],
                                                w["head_sum"], start=True, stop=True)
                    last.then_inc(s["sii_ps"], 1)
                    pe.wait_ge(s["q_loaded"], 16 * PARTS * PARTS * (b + 1))
                    pe.wait_ge(s["k_loaded"], 16 * (PARTS * PARTS + 1) * (b + 1))
                    for i in range(HEADS_Q):
                        hd, t = i // TPB, i % TPB
                        n = (t + 1) * P
                        pe.wait_ge(s["max_out"], b * HEADS_Q + i + 1)
                        nc.tensor.matmul(ps[:, MAXQ[i % 2], 0:n], q_op[0:QK_ROWS, hd, t * P:(t + 1) * P],
                                         k_op[0:QK_ROWS, hd, 0:n], start=True, stop=False)
                        nc.tensor.matmul(ps[:, MAXQ[i % 2], t * P:n], w["ident_b"], w["mask_up"],
                                         start=False, stop=True).then_inc(s["max_ps"], 1)
                    pe.wait_ge(s["max_out"], (b + 1) * HEADS_Q + 2)
                    pe.sem_inc(s["passed"], 1)
                    nc.tensor.transpose(ps[0:HEADS_Q, MISC, 0:P], row_max[:, :, :].rearrange("p h t -> p (h t)"),
                                        core.ident[:, :]).then_inc(s["mT_ps"], 1)
                    pe.wait_ge(s["m_loaded"], 16 * (b + 1))
                    for i in range(SCORES):
                        pe.wait_ge(s["e_out"], b * SCORE_GROUPS * GROUP + i + 1)
                        bank = SCORE[i % 2]
                        if i < NH:
                            nc.tensor.matmul(ps[:, bank, :], w["ident_b"], w["mask_diag4"], start=True, stop=False)
                            for t in range(TPB):
                                own = slice(t * P, (t + 1) * P)
                                last = nc.tensor.matmul(ps[:, bank, own], q_op[0:SHIFT_ROWS, i, own],
                                                        k_op[0:SHIFT_ROWS, i, own], start=False, stop=(t == TPB - 1))
                        else:
                            g, j, hh = (i - NH) // (3 * GROUP), (i - NH) // GROUP % 3, (i - NH) % GROUP
                            hd = g * GROUP + hh
                            last = nc.tensor.matmul(ps[:, bank, 0:(3 - j) * P], k_op[0:SHIFT_ROWS, hd, j * P:(j + 1) * P],
                                                    q_op[0:SHIFT_ROWS, hd, (j + 1) * P:S], start=True, stop=True)
                        last.then_inc(s["s_ps"], 1)
                    for g in range(GROUPS):
                        pe.wait_ge(s["e_out"], b * SCORE_GROUPS * GROUP + NH + (g + 1) * 3 * GROUP + 2)
                        for j in range(3):
                            for hh in range(GROUP):
                                last = nc.tensor.matmul(
                                    ps[hh * HEAD_COLS:(hh + 1) * HEAD_COLS, STEP, j * P:3 * P], w["ones_f"],
                                    e_off[:, g * GROUP + hh, OFF[j]:OFF[j] + (3 - j) * P], start=(j == 0), stop=(j == 2))
                        last.then_inc(s["zo_ps"], 1)
                        pe.wait_ge(s["zo_sb"], b * GROUPS + g + 1)
                        if g > 0:
                            pe.wait_ge(s["z_out"], b * (GROUPS + 1) + g + 1)
                        else:
                            pe.wait_ge(s["m_split"], 5 * b + 2)
                        turn(lambda t: z_off[:, t * P:(t + 1) * P], s["zoT_ps"], TPB - 1)
                    pe.wait_ge(s["z_out"], (b + 1) * (GROUPS + 1))
                    pe.sem_inc(s["passed"], 1)
                    nc.tensor.transpose(ps[0:TPB * NH, MISC, 0:P], z_col[:, :, :].rearrange("p t h -> p (t h)"),
                                        core.ident[:, :]).then_inc(s["zT_ps"], 1)
                    pe.wait_ge(s["x_loaded"], 16 * BLKS * (b + 1))
                    for hd in range(NH):
                        pe.wait_ge(s["masked"], b * NH + hd + 1)
                        if hd >= 2:
                            pe.wait_ge(s["mt_sb"], b * NH + hd - 1)
                        for t in range(TPB):
                            last = nc.tensor.matmul(ps[:, MAXQ[hd % 2], t * P:(t + 1) * P], e_nat[:, hd, t, :],
                                                    xT[:, hd, t, :], start=True, stop=True)
                        last.then_inc(s["mt_ps"], 1)
                    pe.wait_ge(s["mt_sb"], (b + 1) * NH)

                    def side_by_side(lhs, rhs, done):
                        for g in range(GROUPS):
                            for hh in range(GROUP):
                                hd = g * GROUP + hh
                                last = nc.tensor.matmul(ps[hh * HEAD_COLS:(hh + 1) * HEAD_COLS, STEP, g * P:(g + 1) * P],
                                                        lhs(hd), rhs(hd), start=True, stop=True)
                        last.then_inc(done, 1)

                    for t in range(TPB):
                        first = (b * TPB + t) * BLKS
                        if t > 0:
                            for g in range(GROUPS):
                                for j in range(t):
                                    c = (t - 1 - j) * P
                                    for hh in range(GROUP):
                                        hd = g * GROUP + hh
                                        last = nc.tensor.matmul(
                                            ps[hh * HEAD_COLS:(hh + 1) * HEAD_COLS, STEP, g * P:(g + 1) * P],
                                            a_all[:, j, hd, :], e_off[:, hd, OFF[j] + c:OFF[j] + c + P],
                                            start=(j == 0), stop=(j == t - 1))
                            last.then_inc(s["g_ps"], 1)
                            pe.wait_ge(s["gT_sb"], b * (TPB - 1) + t)
                            turn(lambda g: gT[:, g, :], s["gn_ps"])
                        pe.wait_ge(s["gn_sb"], b * TPB + t + 1)
                        side_by_side(lambda hd: g_nat[:, hd, :], lambda hd: xT[:, hd, t, :], s["at_ps"])
                        pe.wait_ge(s["at_sb"], first + 1)
                        turn(lambda g: xg[:, g, :], s["an_ps"])
                        with pe.Fori(1, BLKS) as k:
                            pe.wait_ge(s["an_sb"], first + k)
                            side_by_side(lambda hd: a_nat[:, hd, :], lambda hd: mT[:, hd, t, :], s["at_ps"])
                            pe.wait_ge(s["at_sb"], first + k + 1)
                            turn(lambda g: aT[:, g, :], s["an_ps"])
                        for g in range(GROUPS):
                            last = nc.tensor.matmul(ps[:, WIDE[0], 0:H], aT[:, g, :], w["d_wd"][:, g, :],
                                                    start=(g == 0), stop=(g == GROUPS - 1))
                        last.then_inc(s["o_ps"], 1)
                        pe.wait_ge(s["an_sb"], first + BLKS)
                        pe.wait_ge(s["x_out"], b * TPB + t + 1)


def store_phase(core, nc):
    stored = core.sem("stored")
    with nc.Block() as block:
        @block.sync
        def _(sp):
            sp.dma_start(core.out.rearrange("b (n p) h -> p (b n) h", p=P), core.x[:, :, :]).then_inc(stored, 16)
            sp.wait_ge(stored, 16)


@contextmanager
def semaphores_of_phase(core, nc):
    handles = []

    def allocate(name):
        handles.append(nc.alloc_semaphore(name))
        return handles[-1]

    core.sem = allocate
    yield
    core.sem = nc.alloc_semaphore
    nc.clear_and_free_semaphores(handles)
    nc.all_engine_barrier()


def build(nc, arrays, layers=(0, 1, 2, 3)):
    core = Core()
    with ExitStack() as ctx:
        core.sem = nc.alloc_semaphore
        core.dram = {}
        for name, a in arrays.items():
            core.dram[name] = nc.dram_tensor(name, a.shape, mybir.dt.from_np(a.dtype), kind="ExternalInput").ap()
        core.out = nc.dram_tensor("out_0", [B, S, H], F32, kind="ExternalOutput").ap()

        def keep(name, shape, dt=F32):
            return ctx.enter_context(nc.sbuf_tensor(name, shape, dt))

        core.x = keep("x", [P, TILES, H])[:, :, :]
        core.minus_half = keep("minus_half", [P, TPB])[:, :]
        core.w = {}
        mamba_weights = ExitStack()
        later = ("in_L0_attn_a_x", "ones", "f_w1", "f_w2")
        for name, a in sorted(arrays.items(), key=lambda item: item[0].startswith("m_")):
            if name not in later:
                core.w[name] = (mamba_weights if name.startswith("m_") else ctx).enter_context(nc.sbuf_tensor("sb_" + name, list(a.shape), mybir.dt.from_np(a.dtype)))[
                    tuple(slice(None) for _ in a.shape)]
        core.vec, core.rows, core.ident = core.w["vec"], core.w["rows"], core.w["ident"]
        core.pick = core.w["pick"]
        core.q_scr, core.k_scr = (nc.dram_tensor(n, [B, PARTS, P, S], BF16, kind="Internal").ap() for n in ("q_scr", "k_scr"))
        core.m_scr = nc.dram_tensor("m_scr", [B, PARTS, NH * TPB, P], BF16, kind="Internal").ap()
        core.e_scr = nc.dram_tensor("e_scr", [B, BLKS, NH, TPB, BLK, BLK], F32, kind="Internal").ap()
        core.x_scr = nc.dram_tensor("x_scr", [B, BLKS, NH, TPB, BLK, BLK], F32, kind="Internal").ap()
        core.z_scr = nc.dram_tensor("z_scr", [B, BLKS, NH, TPB, BLK], F32, kind="Internal").ap()
        load_phase(core, nc)
        if 0 in layers:
            with semaphores_of_phase(core, nc):
                mamba_phase(core, nc)
        mamba_weights.close()
        if 1 in layers:
            with semaphores_of_phase(core, nc):
                ffn_phase(core, nc, "f1_")
        if 2 in layers:
            with semaphores_of_phase(core, nc):
                delta_phase(core, nc)
        if 3 in layers:
            with semaphores_of_phase(core, nc):
                ffn_phase(core, nc, "f3_")
        store_phase(core, nc)


def kernel(**inputs):
    from concourse import bacc
    from concourse.bass_utils import run_bass_kernel_spmd

    nc = bacc.Bacc("TRN2", target_bir_lowering=False, num_devices=1)
    arrays = lay_out(inputs)
    build(nc, arrays)
    r = run_bass_kernel_spmd(nc, [arrays], core_ids=[0])
    return r.results[0]["out_0"]
```

```python
from contextlib import ExitStack, contextmanager

import numpy as np

import concourse.bass as bass
import concourse.mybir as mybir

F32 = mybir.dt.float32
BF16 = mybir.dt.bfloat16
ALU = mybir.AluOpType
ACT = mybir.ActivationFunctionType
AX = mybir.AxisListType

P = 128
B, S, H = 4, 512, 128
T = B * S
TPB = S // P
TILES = T // P
EPS = 1e-5

MLP, N_STATE, DT_RANK, CONV_K = 256, 16, 64, 4
HALVES = MLP // P
NH, HD = 16, 8
E, F = 8, 512
FT = F // P
SCALE = float(HD) ** -0.5

VEC = {}
for _name, _n in (("b1", HALVES), ("b2", HALVES), ("conv_w", HALVES * CONV_K), ("conv_b", HALVES),
                  ("A_log", HALVES * N_STATE), ("dt_b", HALVES), ("D", HALVES),
                  ("ln1_g", 1), ("ln1_b", 1), ("ln2_g", 1), ("ln2_b", 1), ("bq", 1), ("bk", 1),
                  ("moe_b1", E * FT), ("dbq", 1), ("dbk", 1)):
    VEC[_name] = (sum(n for _, n in VEC.values()), _n)
NVEC = sum(n for _, n in VEC.values())
ROW = {}
for _name, _n in (("m_bo", H), ("f_bv", H), ("f_bo", H), ("gate_b", E), ("d_bv", H), ("d_bd", H)):
    ROW[_name] = (sum(n for _, n in ROW.values()), _n)
NROW = sum(n for _, n in ROW.values())


def lay_out(inputs):
    g = {k: np.asarray(v) for k, v in inputs.items()}

    def a(n):
        return g["L0_attn_a_" + n]

    def f(n):
        return g["L0_ffn_" + n]

    def d(n):
        return g["L0_attn_b_" + n]

    def halves(v):
        return v.reshape(HALVES, P, -1).transpose(1, 0, 2).reshape(P, -1)

    def padded_heads(m):
        wide = np.zeros((GROUPS, GROUP, HEAD_COLS, H), np.float32)
        wide[:, :, :HD] = m.reshape(GROUPS, GROUP, HD, H)
        return wide.reshape(GROUPS, P, H).transpose(1, 0, 2)

    def rotary(fn, other):
        angle = np.tile(np.arange(S, dtype=np.float32), (P, 1))
        return np.where((np.arange(P) % HD < 2)[:, None], fn(angle), np.float32(other)).astype(np.float32)

    bf16 = mybir.dt.np(BF16)
    cols = {"b1": halves(a("b1")), "b2": halves(a("b2")), "conv_w": halves(a("conv_w")),
            "conv_b": halves(a("conv_b")), "A_log": halves(a("A_log")), "dt_b": halves(a("dt_proj_b")),
            "D": halves(a("D_skip")), "ln1_g": f("ln1_g")[:, None], "ln1_b": f("ln1_b")[:, None],
            "ln2_g": f("ln2_g")[:, None], "ln2_b": f("ln2_b")[:, None], "bq": f("bq")[:, None],
            "bk": f("bk")[:, None], "moe_b1": f("b1").reshape(E * FT, P).T,
            "dbq": d("bqkv")[0:H, None], "dbk": d("bqkv")[H:2 * H, None]}
    rows = {"m_bo": a("bo"), "f_bv": f("bv"), "f_bo": f("bo"), "gate_b": f("gate_b"),
            "d_bv": d("bqkv")[2 * H:], "d_bd": d("bd")}
    arrays = {
        "in_L0_attn_a_x": g["L0_attn_a_x"],
        "vec": np.concatenate([cols[n] for n in VEC], axis=1),
        "rows": np.broadcast_to(np.concatenate([rows[n] for n in ROW])[None, :], (P, NROW)),
        "m_W1": a("W1"), "m_W2": a("W2"),
        "m_xp": a("x_proj_w").reshape(HALVES, P, -1).transpose(1, 0, 2),
        "m_dt": a("dt_proj_w"),
        "m_Wo": a("Wo").reshape(HALVES, P, H).transpose(1, 0, 2),
        "f_wq": f("wq"), "f_wk": f("wk"), "f_wv": f("wv"), "f_wo": f("wo"), "gate_w": f("gate_w"),
        "f_w1": f("w1").transpose(1, 0, 2), "f_w2": f("w2").reshape(E, FT, P, H).transpose(2, 0, 1, 3),
        "f_b2": f("b2"), "countdown": np.tile(E - np.arange(E, dtype=np.float32), (P, 1)),
        "d_wqkv": d("Wqkv").T, "d_wd": padded_heads(d("Wd").T),
        "cos": rotary(np.cos, 1.0), "sin": rotary(np.sin, 0.0) * np.where(np.arange(P) % HD == 0, -1, 1)[:, None].astype(np.float32),
        "head_sum": np.kron(np.eye(NH), np.ones((HD, 1))).astype(np.float32),
        "off_blocks": 1 - np.kron(np.eye(P // 16), np.ones((16, 16))).astype(np.float32),
        "ident_b": np.eye(P).astype(bf16), "mask_up": (np.triu(np.ones((P, P)), 1) * -1e30).astype(bf16),
        "mask_diag4": np.tile(np.triu(np.ones((P, P)), 0) * -1e30, (1, TPB)).astype(bf16),
        "ones_f": np.ones((P, HEAD_COLS), np.float32), "ones": np.ones((PARTS, NH * S), bf16),
        "ident": np.eye(P, dtype=np.float32),
        "pick": np.tile(np.eye(2 * N_STATE), (3, 1)).astype(mybir.dt.np(BF16)),
    }
    return {k: np.ascontiguousarray(v) for k, v in arrays.items()}


class Core:
    pass


def vec(core, name, k=0, n=1):
    c = VEC[name][0] + k
    return core.vec[:, c:c + n]


def row(core, name):
    c, n = ROW[name]
    return core.rows[:, c:c + n]


def load_phase(core, nc):
    loaded = core.sem("x_and_weights_loaded")
    with nc.Block() as block:
        @block.sync
        def _(sp):
            n = 0
            x_tiles = core.dram["in_L0_attn_a_x"].rearrange("b (n p) h -> p (b n) h", p=P)
            for dst, src in [(core.x[:, :, :], x_tiles)] + [(core.w[k], core.dram[k]) for k in core.w]:
                sp.dma_start(dst, src).then_inc(loaded, 16)
                n += 16
            sp.wait_ge(loaded, n)

        @block.vector
        def _(dve):
            nc.vector.memset(core.minus_half[:, :], -0.5)


def mamba_phase(core, nc):
    sem, x_sb = core.sem, core.x
    with ExitStack() as ctx:
        def sb(name, shape, dt=F32):
            return ctx.enter_context(nc.sbuf_tensor("m_" + name, shape, dt))

        ps = ctx.enter_context(nc.psum_tensor("m_ps", [P, 8, 512], F32))
        XT, U_IN, G_IN, XP, DT = 0, 1, 3, 5, 6
        DECAY, B_BANK, C_BANK, Y = 0, 4, 5, 6
        AHEAD = 4
        ln = {"stats": sb("stats", [P, TPB, 6]), "mv": sb("mv", [P, TPB, 2]), "var_eps": sb("var", [P, TPB]),
              "rstd": sb("rstd", [P, TPB]), "out": sb("xn", [P, TPB, H])}
        xnT = sb("xnT", [P, S])
        u_pad = sb("u_pad", [P, HALVES, S + CONV_K - 1])
        conv = sb("conv", [P, HALVES, S])
        gate = sb("gate", [P, HALVES, T])
        u = sb("u", [P, HALVES, T])
        delta = sb("delta", [P, HALVES, T])
        du = sb("du", [P, HALVES, T])
        xp = sb("projected", [DT_RANK + 2 * N_STATE, S])
        bc = sb("bc", [3 * 32, T], BF16)
        part = sb("part", [32, S], BF16)
        bc_own = sb("bc_own", [32, S])
        rest = sb("rest", [32, 2, S])
        z_neg = sb("z_neg", [P, HALVES, S])
        e_abs = sb("e_abs", [P, HALVES, S])
        one_e = sb("one_e", [P, HALVES, S])
        lost = sb("lost", [P, HALVES, S])
        log_e = sb("log_e", [P, HALVES, S])
        A = sb("A", [P, HALVES, N_STATE])
        b_row = sb("b_row", [P, AHEAD, S])
        drive = sb("drive", [P, AHEAD, HALVES, S])
        h = sb("h", [P, 2, HALVES, S])
        hC = sb("hC", [P, 2, HALVES, S])
        yD = sb("yD", [P, HALVES, S])
        yg = sb("yg", [P, HALVES, S])

        names = ("passed pad_zeroed a_exp a_ready ln_stats ln_mv ln_var ln_rstd ln_done xT_ps xT_sb proj_ps u_in gate_out "
                 "conv_step conv_out u_out xp_ps xp_sb bc_sb split dt_ps z_out z_abs e_out one_e_out lost_out "
                 "log_out log1p_out delta_out du_out b_ps b_sb decay_out drive_out c_ps scan_out hC_out "
                 "y_ps yD_out yg_out o_ps o_added x_out")
        s = {n: sem("m_" + n) for n in names.split()}
        W1, W2, Wx, Wdt, Wo = (core.w[n] for n in ("m_W1", "m_W2", "m_xp", "m_dt", "m_Wo"))
        FREE = {"b_sb": 1, "scan_out": AHEAD, "drive_out": AHEAD, "hC_out": 1, "y_ps": 2, "x_out": 1, "u_out": 1,
                "gate_out": 1, "split": 1}

        with nc.Block() as block:
            @block.gpsimd
            def _(pool):
                with pool.Fori(0, B) as b:
                    layer_norm_rstd(nc, pool, core, ln, s, "ln", b + 1)
                pool.sem_inc(s["split"], FREE["split"])
                with pool.Fori(0, B) as b:
                    now = bass.ds(b * S, S)
                    pool.wait_ge(s["bc_sb"], b + 1)
                    pool.sem_inc(s["passed"], 1)
                    nc.gpsimd.tensor_copy(part[:, :], bc_own[:, :]).then_inc(s["split"], 1)
                    pool.wait_ge(s["split"], 7 * b + 1 + FREE["split"])
                    pool.sem_inc(s["passed"], 1)
                    nc.gpsimd.tensor_copy(bc[0:32, now], part[:, :]).then_inc(s["split"], 1)
                    nc.gpsimd.tensor_tensor(rest[:, 0, :], bc_own[:, :], part[:, :], ALU.subtract).then_inc(s["split"], 1)
                    pool.wait_ge(s["split"], 7 * b + 3 + FREE["split"])
                    pool.sem_inc(s["passed"], 1)
                    nc.gpsimd.tensor_copy(part[:, :], rest[:, 0, :]).then_inc(s["split"], 1)
                    pool.wait_ge(s["split"], 7 * b + 4 + FREE["split"])
                    pool.sem_inc(s["passed"], 1)
                    nc.gpsimd.tensor_copy(bc[32:64, now], part[:, :]).then_inc(s["split"], 1)
                    nc.gpsimd.tensor_tensor(rest[:, 1, :], rest[:, 0, :], part[:, :], ALU.subtract).then_inc(s["split"], 1)
                    pool.wait_ge(s["split"], 7 * b + 6 + FREE["split"])
                    pool.sem_inc(s["passed"], 1)
                    nc.gpsimd.tensor_copy(bc[64:96, now], rest[:, 1, :]).then_inc(s["split"], 1)
                    pool.wait_ge(s["split"], 7 * b + 7 + FREE["split"])
                pool.sem_inc(s["drive_out"], FREE["drive_out"])
                with pool.Fori(0, B) as b:
                    now = bass.ds(b * S, S)
                    pool.wait_ge(s["du_out"], b + 1)
                    for n in range(N_STATE):
                        step = b * N_STATE + n
                        pool.wait_ge(s["b_sb"], step + 1 + FREE["b_sb"])
                        pool.wait_ge(s["scan_out"], step + 1)
                        pool.sem_inc(s["passed"], 1)
                        nc.gpsimd.tensor_tensor(drive[:, n % AHEAD, :, :], du[:, :, now],
                                                b_row[:, n % AHEAD, :].unsqueeze(1).to_broadcast([P, HALVES, S]),
                                                ALU.mult).then_inc(s["drive_out"], 1)

            @block.scalar
            def _(act):
                nc.scalar.activation(A[:, :, :], vec(core, "A_log", 0, HALVES * N_STATE).rearrange(
                    "p (a n) -> p a n", a=HALVES), ACT.Exp).then_inc(s["a_exp"], 1)
                act.wait_ge(s["pad_zeroed"], 1)

                def turned(b):
                    act.wait_ge(s["xT_ps"], b + 1)
                    nc.scalar.copy(xnT[:, :], ps[:, XT, :]).then_inc(s["xT_sb"], 1)

                def projected(b, ahead):
                    now = bass.ds(b * S, S)
                    act.wait_ge(s["proj_ps"], b + 1)
                    for k in range(HALVES):
                        nc.scalar.activation(u_pad[:, k, CONV_K - 1:], ps[:, U_IN + k, :], ACT.Identity,
                                             bias=vec(core, "b1", k)).then_inc(s["u_in"], 1)
                    for k in range(HALVES):
                        nc.scalar.activation(gate[:, k, now], ps[:, G_IN + k, :], ACT.Sigmoid,
                                             bias=vec(core, "b2", k)).then_inc(s["gate_out"], 1)
                    if ahead:
                        turned(b + 1)
                    act.wait_ge(s["conv_out"], b + 1)
                    act.sem_inc(s["passed"], 1)
                    nc.scalar.activation(u[:, :, now], conv[:, :, :], ACT.Sigmoid).then_inc(s["u_out"], 1)

                act.sem_inc(s["u_out"], FREE["u_out"])
                act.sem_inc(s["gate_out"], FREE["gate_out"])
                turned(0)
                with act.Fori(0, B - 1) as b:
                    projected(b, True)
                projected(B - 1, False)
                with act.Fori(0, B) as b:
                    act.wait_ge(s["z_abs"], b + 1)
                    nc.scalar.activation(e_abs[:, :, :], z_neg[:, :, :], ACT.Exp).then_inc(s["e_out"], 1)
                    act.wait_ge(s["one_e_out"], b + 1)
                    nc.scalar.activation(log_e[:, :, :], one_e[:, :, :], ACT.Ln).then_inc(s["log_out"], 1)
                act.wait_ge(s["a_ready"], 1)
                act.sem_inc(s["b_sb"], FREE["b_sb"])
                with act.Fori(0, B) as b:
                    now = bass.ds(b * S, S)
                    act.wait_ge(s["delta_out"], b + 1)
                    for n in range(N_STATE):
                        step = b * N_STATE + n
                        act.wait_ge(s["b_ps"], step + 1)
                        act.wait_ge(s["drive_out"], step + 1)
                        nc.scalar.copy(b_row[:, n % AHEAD, :], ps[:, B_BANK, :]).then_inc(s["b_sb"], 1)
                        act.wait_ge(s["scan_out"], step + AHEAD - 1)
                        act.sem_inc(s["passed"], 1)
                        for k in range(HALVES):
                            last = nc.scalar.activation(ps[:, DECAY + HALVES * (n % 2) + k, :], delta[:, k, now],
                                                        ACT.Exp, scale=A[:, k, n:n + 1])
                        last.then_inc(s["decay_out"], 1)

            @block.vector
            def _(dve):
                nc.vector.memset(u_pad[:, :, 0:CONV_K - 1], 0.0).then_inc(s["pad_zeroed"], 1)
                dve.wait_ge(s["a_exp"], 1)
                nc.vector.tensor_scalar(A[:, :, :], A[:, :, :], -1.0, None, ALU.mult).then_inc(s["a_ready"], 1)

                def norm(b):
                    layer_norm_stats(nc, dve, None, lambda t: x_sb[:, b * TPB + t, :], TPB, ln, s, "ln", b + 1)

                def convolve(b):
                    dve.wait_ge(s["u_in"], HALVES * (b + 1))
                    dve.wait_ge(s["u_out"], b + FREE["u_out"])
                    for k in range(HALVES):
                        last = nc.vector.tensor_scalar(conv[:, k, :], u_pad[:, k, 0:S], vec(core, "conv_w", k * CONV_K),
                                                       vec(core, "conv_b", k), ALU.mult, ALU.add)
                    last.then_inc(s["conv_step"], 1)
                    for j in range(1, CONV_K):
                        dve.wait_ge(s["conv_step"], b * (CONV_K - 1) + j)
                        for k in range(HALVES):
                            last = nc.vector.scalar_tensor_tensor(
                                out=conv[:, k, :], in0=u_pad[:, k, j:j + S], scalar=vec(core, "conv_w", k * CONV_K + j),
                                in1=conv[:, k, :], op0=ALU.mult, op1=ALU.add)
                        last.then_inc(s["conv_step"] if j < CONV_K - 1 else s["conv_out"], 1)

                norm(0)
                with dve.Fori(0, B - 1) as b:
                    dve.wait_ge(s["xT_ps"], b + 1)
                    norm(b + 1)
                    convolve(b)
                convolve(B - 1)
                with dve.Fori(0, B) as b:
                    now = bass.ds(b * S, S)
                    dve.wait_ge(s["xp_ps"], b + 1)
                    nc.vector.tensor_copy(xp[0:DT_RANK, :], ps[0:DT_RANK, XP, :]).then_inc(s["xp_sb"], 1)
                    dve.wait_ge(s["split"], 7 * b + FREE["split"])
                    nc.vector.tensor_copy(bc_own[:, :], ps[DT_RANK:DT_RANK + 2 * N_STATE, XP, :]).then_inc(s["bc_sb"], 1)
                    dve.wait_ge(s["dt_ps"], b + 1)
                    for k in range(HALVES):
                        last = nc.vector.tensor_scalar(delta[:, k, now], ps[:, DT + k, :], vec(core, "dt_b", k), None,
                                                       ALU.add)
                    last.then_inc(s["z_out"], 1)
                    dve.wait_ge(s["z_out"], b + 1)
                    nc.vector.scalar_tensor_tensor(out=z_neg[:, :, :], in0=delta[:, :, now], scalar=-1.0,
                                                   in1=delta[:, :, now], op0=ALU.mult,
                                                   op1=ALU.min).then_inc(s["z_abs"], 1)
                    dve.wait_ge(s["e_out"], b + 1)
                    nc.vector.tensor_scalar(one_e[:, :, :], e_abs[:, :, :], 1.0, None,
                                            ALU.add).then_inc(s["one_e_out"], 1)
                    dve.wait_ge(s["one_e_out"], b + 1)
                    nc.vector.scalar_tensor_tensor(out=lost[:, :, :], in0=one_e[:, :, :], scalar=-1.0, in1=e_abs[:, :, :],
                                                   op0=ALU.add, op1=ALU.subtract).then_inc(s["lost_out"], 1)
                    dve.wait_ge(s["lost_out"], b + 1)
                    dve.wait_ge(s["log_out"], b + 1)
                    nc.vector.tensor_tensor(lost[:, :, :], log_e[:, :, :], lost[:, :, :],
                                            ALU.subtract).then_inc(s["log1p_out"], 1)
                    dve.wait_ge(s["log1p_out"], b + 1)
                    nc.vector.scalar_tensor_tensor(out=delta[:, :, now], in0=delta[:, :, now], scalar=0.0,
                                                   in1=lost[:, :, :], op0=ALU.max,
                                                   op1=ALU.add).then_inc(s["delta_out"], 1)
                    dve.wait_ge(s["delta_out"], b + 1)
                    nc.vector.tensor_tensor(du[:, :, now], delta[:, :, now], u[:, :, now],
                                            ALU.mult).then_inc(s["du_out"], 1)
                dve.sem_inc(s["scan_out"], FREE["scan_out"])
                dve.sem_inc(s["hC_out"], FREE["hC_out"])
                dve.sem_inc(s["x_out"], FREE["x_out"])
                with dve.Fori(0, B) as b:
                    now = bass.ds(b * S, S)
                    tiles = bass.ds(b * TPB, TPB)
                    for n in range(N_STATE):
                        step = b * N_STATE + n
                        dve.wait_ge(s["decay_out"], step + 1)
                        dve.wait_ge(s["drive_out"], step + 1 + FREE["drive_out"])
                        for k in range(HALVES):
                            last = nc.vector.tensor_tensor_scan(h[:, n % 2, k, :],
                                                                ps[:, DECAY + HALVES * (n % 2) + k, :],
                                                                drive[:, n % AHEAD, k, :], 0.0, ALU.mult, ALU.add)
                        last.then_inc(s["scan_out"], 1)
                        dve.wait_ge(s["scan_out"], step + 1 + FREE["scan_out"])
                        dve.wait_ge(s["c_ps"], step + 1)
                        dve.wait_ge(s["y_ps"], step + 1)
                        nc.vector.tensor_tensor(hC[:, n % 2, :, :], h[:, n % 2, :, :],
                                                ps[:, C_BANK, :].unsqueeze(1).to_broadcast([P, HALVES, S]),
                                                ALU.mult).then_inc(s["hC_out"], 1)
                    dve.wait_ge(s["y_ps"], b * N_STATE + N_STATE + FREE["y_ps"])
                    for k in range(HALVES):
                        last = nc.vector.scalar_tensor_tensor(out=yD[:, k, :], in0=u[:, k, now],
                                                              scalar=vec(core, "D", k), in1=ps[:, Y + k, :],
                                                              op0=ALU.mult, op1=ALU.add)
                    last.then_inc(s["yD_out"], 1)
                    dve.wait_ge(s["yD_out"], b + 1)
                    nc.vector.tensor_tensor(yg[:, :, :], yD[:, :, :], gate[:, :, now], ALU.mult).then_inc(s["yg_out"], 1)
                    dve.wait_ge(s["o_ps"], b + 1)
                    nc.vector.tensor_tensor(x_sb[:, tiles, :], x_sb[:, tiles, :],
                                            ps[:, C_BANK, :].rearrange("p (t h) -> p t h", t=TPB),
                                            ALU.add).then_inc(s["o_added"], 1)
                    dve.wait_ge(s["o_added"], b + 1)
                    nc.vector.tensor_tensor(x_sb[:, tiles, :], x_sb[:, tiles, :],
                                            row(core, "m_bo").unsqueeze(1).to_broadcast([P, TPB, H]),
                                            ALU.add).then_inc(s["x_out"], 1)

            @block.tensor
            def _(pe):
                def turn(b):
                    pe.wait_ge(s["ln_done"], b + 1)
                    for t in range(TPB):
                        last = nc.tensor.transpose(ps[:, XT, t * P:(t + 1) * P], ln["out"][:, t, :], core.ident[:, :])
                    last.then_inc(s["xT_ps"], 1)

                def project(b):
                    pe.wait_ge(s["xT_sb"], b + 1)
                    pe.wait_ge(s["gate_out"], HALVES * b + FREE["gate_out"])
                    for k in range(HALVES):
                        nc.tensor.matmul(ps[:, U_IN + k, :], W1[:, k * P:(k + 1) * P], xnT[:, :], start=True, stop=True)
                    for k in range(HALVES):
                        last = nc.tensor.matmul(ps[:, G_IN + k, :], W2[:, k * P:(k + 1) * P], xnT[:, :],
                                                start=True, stop=True)
                    last.then_inc(s["proj_ps"], 1)

                turn(0)
                with pe.Fori(0, B - 1) as b:
                    project(b)
                    turn(b + 1)
                project(B - 1)
                with pe.Fori(0, B) as b:
                    now = bass.ds(b * S, S)
                    pe.wait_ge(s["u_out"], b + 1 + FREE["u_out"])
                    for k in range(HALVES):
                        last = nc.tensor.matmul(ps[0:DT_RANK + 2 * N_STATE, XP, :], Wx[:, k, :], u[:, k, now],
                                                start=(k == 0), stop=(k == HALVES - 1))
                    last.then_inc(s["xp_ps"], 1)
                    pe.wait_ge(s["xp_sb"], b + 1)
                    for k in range(HALVES):
                        last = nc.tensor.matmul(ps[:, DT + k, :], Wdt[:, k * P:(k + 1) * P], xp[0:DT_RANK, :],
                                                start=True, stop=True)
                    last.then_inc(s["dt_ps"], 1)
                    pe.wait_ge(s["bc_sb"], b + 1)
                    pe.wait_ge(s["z_out"], b + 1)
                pe.sem_inc(s["y_ps"], FREE["y_ps"])
                with pe.Fori(0, B) as b:
                    now = bass.ds(b * S, S)

                    def spread(bank, r):
                        return nc.tensor.matmul(ps[:, bank, :], core.pick[:, r:r + 1].to_broadcast([96, P]),
                                                bc[:, now], start=True, stop=True)

                    for n in range(N_STATE):
                        step = b * N_STATE + n
                        if n == 0:
                            pe.wait_ge(s["split"], 7 * (b + 1) + FREE["split"])
                            for m in range(2):
                                pe.wait_ge(s["b_sb"], step + m + FREE["b_sb"])
                                spread(B_BANK, m).then_inc(s["b_ps"], 1)
                            pe.wait_ge(s["x_out"], b + FREE["x_out"])
                            spread(C_BANK, N_STATE).then_inc(s["c_ps"], 1)
                        if n + 2 < N_STATE:
                            pe.wait_ge(s["b_sb"], step + 2 + FREE["b_sb"])
                            spread(B_BANK, n + 2).then_inc(s["b_ps"], 1)
                        pe.wait_ge(s["hC_out"], step + 1 + FREE["hC_out"])
                        if n + 1 < N_STATE:
                            spread(C_BANK, N_STATE + n + 1).then_inc(s["c_ps"], 1)
                        for k in range(HALVES):
                            last = nc.tensor.matmul(ps[:, Y + k, :], core.ident[:, :], hC[:, n % 2, k, :],
                                                    start=(n == 0), stop=(n == N_STATE - 1))
                        last.then_inc(s["y_ps"], 1)
                    pe.wait_ge(s["yg_out"], b + 1)
                    for t in range(TPB):
                        for k in range(HALVES):
                            last = nc.tensor.matmul(ps[:, C_BANK, t * H:(t + 1) * H], yg[:, k, t * P:(t + 1) * P],
                                                    Wo[:, k, :], start=(k == 0), stop=(k == HALVES - 1))
                    last.then_inc(s["o_ps"], 1)


def layer_norm_stats(nc, dve, pool_rstd, src, tiles, buf, s, pre, i):
    for t in range(tiles):
        last = nc.vector.bn_stats(buf["stats"][:, t, :], src(t))
    last.then_inc(s[pre + "_stats"], 1)
    dve.wait_ge(s[pre + "_stats"], i)
    dve.sem_inc(s["passed"], 1)
    for t in range(tiles):
        last = nc.vector.bn_aggr(buf["mv"][:, t, :], buf["stats"][:, t, :])
    last.then_inc(s[pre + "_mv"], 1)
    dve.wait_ge(s[pre + "_mv"], i)
    nc.vector.tensor_scalar(buf["var_eps"][:, :], buf["mv"][:, :, 1], EPS, None, ALU.add).then_inc(s[pre + "_var"], 1)
    dve.wait_ge(s[pre + "_rstd"], i)
    for t in range(tiles):
        last = nc.vector.tensor_scalar(buf["out"][:, t, :], src(t), buf["mv"][:, t, 0:1], buf["rstd"][:, t:t + 1],
                                       ALU.subtract, ALU.mult)
    last.then_inc(s[pre + "_done"], 1)


def layer_norm_rstd(nc, pool, core, buf, s, pre, i):
    pool.wait_ge(s[pre + "_var"], i)
    nc.gpsimd.tensor_tensor(buf["rstd"][:, :], buf["var_eps"][:, :], core.minus_half[:, 0:TPB],
                            ALU.pow).then_inc(s[pre + "_rstd"], 1)


LN_NAMES = ("stats", "mv", "var", "rstd", "done")
PARTS = 3
QK_ROWS = PARTS * PARTS * HD
SHIFT_ROWS = QK_ROWS + PARTS
HEAD_COLS = 32
GROUP = P // HEAD_COLS
GROUPS = NH // GROUP


def split_parts(eng, ops, src, part, rest, s, b):
    done = b * (2 * PARTS - 1)
    for j in range(PARTS):
        eng.sem_inc(s["passed"], 1)
        ops.tensor_copy(part[:, :, j, :], src).then_inc(s["split"], 1)
        eng.wait_ge(s["split"], done + 2 * j + 1)
        if j < PARTS - 1:
            ops.tensor_tensor(rest[j], src, part[:, :, j, :], ALU.subtract).then_inc(s["split"], 1)
            eng.wait_ge(s["split"], done + 2 * j + 2)
            src = rest[j]


def load_operand(sp, operand, parts, which, loaded):
    for i in range(PARTS):
        rows = operand[i * PARTS * HD:(i + 1) * PARTS * HD, :, :]
        if which == 0:
            source = parts[i:i + 1].to_broadcast([PARTS, HD, NH, S]).rearrange("j d h s -> j d (h s)")
        else:
            source = parts.rearrange("j d h s -> (j d) h s")
        sp.dma_start(rows, source).then_inc(loaded, 16)


def ffn_phase(core, nc, tag):
    x_sb = core.x
    with ExitStack() as ctx:
        def sb(name, shape, dt=F32):
            return ctx.enter_context(nc.sbuf_tensor(tag + name, shape, dt))

        ps = ctx.enter_context(nc.psum_tensor(tag + "ps", [P, 8, 512], F32))
        UP, MAXQ, SCORE, O_BANK, MISC, MOE2, PROJ = (0, 1), (2, 3), (0, 2), (4, 6), 5, (6, 7), 7
        ln = {}
        for n in ("ln0", "ln1", "ln2"):
            ln[n] = {"stats": sb(n + "stats", [P, TPB, 6]), "mv": sb(n + "mv", [P, TPB, 2]),
                     "var_eps": sb(n + "var", [P, TPB]), "rstd": sb(n + "rstd", [P, TPB]),
                     "out": sb(n + "out", [P, TPB, H])}
        hnT = sb("hnT", [P, S])
        qk = sb("qk", [P, 2, S])
        part = sb("part", [P, 2, PARTS, S], BF16)
        rest = sb("rest", [P, 2, 2, S])
        q_op = sb("q_op", [P, NH, S], BF16)
        k_op = sb("k_op", [P, NH, S], BF16)
        v_op = sb("v_op", [P, TPB, NH, HEAD_COLS])
        row_max = sb("row_max", [P, NH, TPB])
        max_part = sb("max_part", [NH * TPB, PARTS, P], BF16)
        max_rest = sb("max_rest", [NH * TPB, 2, P])
        e_sb = sb("e", [P, 2, GROUP, S])
        o_raw = sb("o_raw", [P, S])
        z_inv = sb("z_inv", [P, TPB, GROUP])
        o_nat = sb("o_nat", [P, TPB, NH, HD])
        oT = sb("oT", [P, S])
        x2 = sb("x2", [P, TPB, H])
        h2T = sb("h2T", [P, S])
        lg = sb("lg", [P, TPB, E])
        top = sb("top", [P, TPB])
        first = sb("first", [P, TPB])
        onehot = sb("onehot", [P, TPB, E])
        onehotT = sb("onehotT", [E, S])
        mid = sb("mid", [P, 2, FT, S])
        acc = sb("acc", [P, TPB, H])
        w1 = sb("w1", [P, E, F])
        w2 = sb("w2", [P, E, FT, H])

        names = ("passed weights_in rows_zeroed ones_in v_zeroed hT_ps hT_sb qk_ps qk_sb split v_ps v_sb parts_stored q_loaded k_loaded "
                 "max_ps max_out mT_ps m_split m_stored m_loaded s_ps e_out pv_ps o_raw_out oT_ps z_out o_out "
                 "on_ps on_sb wo_ps x2_step x2_out h2_ps h2_sb lg_ps lg_out top_out tie_out rank_out pick_out hot_out "
                 "hotT_ps hotT_sb b2_ps acc_out up_ps mid_out down_ps x_out")
        s = {n: core.sem(tag + n) for n in names.split()}
        s.update({n + m: core.sem(tag + n + m) for n in ("ln_", "ln2_") for m in LN_NAMES})
        w = core.w
        q_scr, k_scr, m_scr = core.q_scr, core.k_scr, core.m_scr
        HEADS_Q = NH * TPB
        STEPS = GROUPS * TPB
        PAIRS = GROUP // 2
        AHEAD_AT = 8
        LAST_WITH = 5
        WITH_EXPERT = [range(e * HEADS_Q // (LAST_WITH + 1), (e + 1) * HEADS_Q // (LAST_WITH + 1))
                       if e <= LAST_WITH else () for e in range(E)]

        with nc.Block() as block:
            @block.gpsimd
            def _(pool):
                def early(b, split):
                    layer_norm_rstd(nc, pool, core, ln["ln0"], s, "ln", 2 * b + 1)
                    layer_norm_rstd(nc, pool, core, ln["ln1"], s, "ln", 2 * b + 2)
                    if split:
                        pool.wait_ge(s["qk_sb"], 2 * b + 2)
                        split_parts(pool, nc.gpsimd, qk[:, :, :], part, (rest[:, :, 0, :], rest[:, :, 1, :]), s, b)

                early(0, False)
                for operand in (q_op, k_op):
                    nc.gpsimd.memset(operand[:, :, :].rearrange("p h s -> p (h s)").bitcast(F32), 0.0).then_inc(s["rows_zeroed"], 1)
                pool.wait_ge(s["rows_zeroed"], 2)
                with pool.Fori(0, B - 1) as b:
                    early(b + 1, True)
                    layer_norm_rstd(nc, pool, core, ln["ln2"], s, "ln2", b + 1)
                layer_norm_rstd(nc, pool, core, ln["ln2"], s, "ln2", B)

            @block.sync
            def _(sp):
                def operands(b):
                    sp.wait_ge(s["split"], (b + 1) * (2 * PARTS - 1))
                    for i, scr in enumerate((q_scr, k_scr)):
                        for j in range(PARTS):
                            sp.dma_start(scr[b, j].rearrange("d h s -> h d s"), part[:, i, j, :]).then_inc(s["parts_stored"], 16)
                    sp.wait_ge(s["parts_stored"], 16 * 2 * PARTS * (b + 1))
                    sp.wait_ge(s["s_ps"], b * STEPS * PAIRS + 1)
                    load_operand(sp, q_op, q_scr[b], 0, s["q_loaded"])
                    load_operand(sp, k_op, k_scr[b], 1, s["k_loaded"])

                def shifts(b):
                    sp.wait_ge(s["m_split"], 5 * (b + 1))
                    sp.dma_start(m_scr[b].rearrange("j r s -> r j s"), max_part[:, :, :]).then_inc(s["m_stored"], 16)
                    sp.wait_ge(s["m_stored"], 16 * (b + 1))
                    sp.dma_start(q_op[QK_ROWS:SHIFT_ROWS, :, :],
                                 m_scr[b].rearrange("j (h t) s -> j h (t s)", t=TPB)).then_inc(s["m_loaded"], 16)

                sp.dma_start(w1[:, :, :], core.dram["f_w1"]).then_inc(s["weights_in"], 16)
                sp.dma_start(w2[:, :, :, :], core.dram["f_w2"]).then_inc(s["weights_in"], 16)
                sp.wait_ge(s["rows_zeroed"], 2)
                sp.dma_start(k_op[QK_ROWS:SHIFT_ROWS, :, :],
                             core.dram["ones"].rearrange("j (h s) -> j h s", h=NH)).then_inc(s["ones_in"], 16)
                sp.sem_inc(s["s_ps"], 1)
                operands(0)
                shifts(0)
                with sp.Fori(1, B) as b:
                    operands(b)
                    shifts(b)

            @block.scalar
            def _(act):
                act.sem_inc(s["e_out"], 2)
                act.sem_inc(s["o_raw_out"], 2)

                def biased(b, i):
                    act.wait_ge(s["qk_ps"], 2 * b + i + 1)
                    nc.scalar.activation(qk[:, i, :], ps[:, PROJ, :], ACT.Identity,
                                         bias=vec(core, ("bq", "bk")[i])).then_inc(s["qk_sb"], 1)

                def attention(b, ahead):
                    def leave(g):
                        act.wait_ge(s["pv_ps"], b * STEPS + g * TPB + TPB + 2)
                        act.wait_ge(s["oT_ps"], b * GROUPS + g + 1)
                        nc.scalar.copy(o_raw[:, :], ps[:, O_BANK[g % 2], :]).then_inc(s["o_raw_out"], 1)

                    for q in range(STEPS):
                        act.wait_ge(s["pv_ps"], b * STEPS + q + 1)
                        for pair in range(PAIRS):
                            i = q * PAIRS + pair
                            act.wait_ge(s["s_ps"], b * STEPS * PAIRS + i + 1 + 1)
                            nc.scalar.activation(e_sb[:, q % 2, 2 * pair:2 * pair + 2, :],
                                                 ps[:, SCORE[i % 2]:SCORE[i % 2] + 2, :], ACT.Exp,
                                                 scale=SCALE).then_inc(s["e_out"], 1)
                        if q % TPB == 1 and q > TPB:
                            leave(q // TPB - 1)
                        if ahead and q in (AHEAD_AT + 2, AHEAD_AT + 3):
                            biased(b + 1, q - AHEAD_AT - 2)
                    leave(GROUPS - 1)
                    act.wait_ge(s["on_ps"], b + 1)
                    nc.scalar.copy(oT[:, :], ps[:, MISC, :]).then_inc(s["on_sb"], 1)

                def experts(b):
                    for e in range(E):
                        for f in range(FT):
                            i = e * FT + f
                            act.wait_ge(s["up_ps"], b * E * FT + i + 1)
                            if f == 0:
                                act.wait_ge(s["down_ps"], b * E + e + 1)
                            nc.scalar.activation(mid[:, e % 2, f, :], ps[:, UP[i % 2], :], ACT.Relu,
                                                 bias=vec(core, "moe_b1", i)).then_inc(s["mid_out"], 1)
                        if e == 0:
                            act.wait_ge(s["hotT_ps"], b + 1)
                            nc.scalar.copy(onehotT[:, :], ps[0:E, MISC, :]).then_inc(s["hotT_sb"], 1)

                biased(0, 0)
                biased(0, 1)
                with act.Fori(0, B - 1) as b:
                    attention(b, True)
                    experts(b)
                attention(B - 1, False)
                experts(B - 1)

            @block.vector
            def _(dve):
                nc.vector.memset(v_op[:, :, :, :], 0.0).then_inc(s["v_zeroed"], 1)
                dve.wait_ge(s["v_zeroed"], 1)
                nc.vector.memset(v_op[:, :, :, HD:HD + 1], 1.0).then_inc(s["v_zeroed"], 1)
                dve.sem_inc(s["max_out"], 2)
                dve.sem_inc(s["acc_out"], 2)

                def norms(b):
                    layer_norm_stats(nc, dve, None, lambda t: x_sb[:, b * TPB + t, :], TPB, ln["ln0"], s, "ln", 2 * b + 1)
                    dve.wait_ge(s["ln_done"], 2 * b + 1)
                    layer_norm_stats(nc, dve, None, lambda t: ln["ln0"]["out"][:, t, :], TPB, ln["ln1"], s, "ln", 2 * b + 2)

                def normed(b):
                    dve.wait_ge(s["hT_ps"], b + 1)
                    nc.vector.tensor_scalar(hnT[:, :], ps[:, MISC, :], vec(core, "ln1_g"), vec(core, "ln1_b"),
                                            ALU.mult, ALU.add).then_inc(s["hT_sb"], 1)

                def values(b):
                    dve.wait_ge(s["v_ps"], b + 1)
                    nc.vector.tensor_tensor(v_op[:, :, :, 0:HD],
                                            ps[:, MISC, :].rearrange("p (t h d) -> p t h d", t=TPB, d=HD),
                                            row(core, "f_bv").rearrange("p (h d) -> p h d", d=HD).unsqueeze(1)
                                            .to_broadcast([P, TPB, NH, HD]), ALU.add).then_inc(s["v_sb"], 1)

                def maxima(b, some):
                    for i in some:
                        dve.wait_ge(s["max_ps"], b * HEADS_Q + i + 1)
                        nc.vector.tensor_reduce(row_max[:, i // TPB, i % TPB:i % TPB + 1], ps[:, MAXQ[i % 2], :], AX.X,
                                                ALU.max).then_inc(s["max_out"], 1)

                def minus_maxima(b):
                    dve.wait_ge(s["mT_ps"], b + 1)
                    minus = ps[0:HEADS_Q, MISC, 0:P]
                    nc.vector.tensor_scalar(max_part[:, 0, :], minus, -1.0, None, ALU.mult).then_inc(s["m_split"], 1)
                    dve.wait_ge(s["m_split"], 5 * b + 1)
                    nc.vector.scalar_tensor_tensor(out=max_rest[:, 0, :], in0=minus, scalar=-1.0, in1=max_part[:, 0, :],
                                                   op0=ALU.mult, op1=ALU.subtract).then_inc(s["m_split"], 1)
                    dve.wait_ge(s["m_split"], 5 * b + 2)
                    nc.vector.tensor_copy(max_part[:, 1, :], max_rest[:, 0, :]).then_inc(s["m_split"], 1)
                    dve.wait_ge(s["m_split"], 5 * b + 3)
                    nc.vector.tensor_tensor(max_rest[:, 1, :], max_rest[:, 0, :], max_part[:, 1, :],
                                            ALU.subtract).then_inc(s["m_split"], 1)
                    dve.wait_ge(s["m_split"], 5 * b + 4)
                    nc.vector.tensor_copy(max_part[:, 2, :], max_rest[:, 1, :]).then_inc(s["m_split"], 1)

                def attention(b, ahead):
                    dve.wait_ge(s["ln_done"], 2 * b + 2)
                    nc.vector.tensor_tensor(x2[:, :, :], ln["ln0"]["out"][:, :, :],
                                            row(core, "f_bo").unsqueeze(1).to_broadcast([P, TPB, H]),
                                            ALU.add).then_inc(s["x2_step"], 1)
                    if ahead:
                        dve.wait_ge(s["x2_step"], b + 1)
                        norms(b + 1)
                    for g in range(GROUPS):
                        dve.wait_ge(s["oT_ps"], b * GROUPS + g + 2)
                        o_ps = ps[:, MISC, :].rearrange("p (t h c) -> p t h c", t=TPB, c=HEAD_COLS)
                        nc.vector.reciprocal(z_inv[:, :, :], o_ps[:, :, :, HD]).then_inc(s["z_out"], 1)
                        dve.wait_ge(s["z_out"], b * GROUPS + g + 1)
                        nc.vector.tensor_tensor(o_nat[:, :, g * GROUP:(g + 1) * GROUP, :], o_ps[:, :, :, 0:HD],
                                                z_inv[:, :, :].unsqueeze(3).to_broadcast([P, TPB, GROUP, HD]),
                                                ALU.mult).then_inc(s["o_out"], 1)
                        if ahead and g == 0:
                            normed(b + 1)

                def router(b):
                    dve.wait_ge(s["wo_ps"], b + 1)
                    dve.wait_ge(s["x2_step"], b + 1)
                    nc.vector.tensor_tensor(x2[:, :, :], ps[:, MISC, :].rearrange("p (t h) -> p t h", t=TPB),
                                            x2[:, :, :], ALU.add).then_inc(s["x2_out"], 1)
                    dve.wait_ge(s["x2_out"], b + 1)
                    layer_norm_stats(nc, dve, None, lambda t: x2[:, t, :], TPB, ln["ln2"], s, "ln2", b + 1)
                    dve.wait_ge(s["h2_ps"], b + 1)
                    nc.vector.tensor_scalar(h2T[:, :], ps[:, MISC, :], vec(core, "ln2_g"), vec(core, "ln2_b"),
                                            ALU.mult, ALU.add).then_inc(s["h2_sb"], 1)
                    dve.wait_ge(s["lg_ps"], b + 1)
                    nc.vector.tensor_tensor(lg[:, :, :], ps[:, MISC, 0:TPB * E].rearrange("p (t e) -> p t e", t=TPB),
                                            row(core, "gate_b").unsqueeze(1).to_broadcast([P, TPB, E]),
                                            ALU.add).then_inc(s["lg_out"], 1)
                    dve.wait_ge(s["lg_out"], b + 1)
                    nc.vector.tensor_reduce(top[:, :], lg[:, :, :], AX.X, ALU.max).then_inc(s["top_out"], 1)
                    dve.wait_ge(s["top_out"], b + 1)
                    nc.vector.tensor_tensor(lg[:, :, :], lg[:, :, :], top[:, :].unsqueeze(2).to_broadcast([P, TPB, E]),
                                            ALU.is_equal).then_inc(s["tie_out"], 1)
                    dve.wait_ge(s["tie_out"], b + 1)
                    down_count = w["countdown"].unsqueeze(1).to_broadcast([P, TPB, E])
                    nc.vector.tensor_tensor(lg[:, :, :], lg[:, :, :], down_count, ALU.mult).then_inc(s["rank_out"], 1)
                    dve.wait_ge(s["rank_out"], b + 1)
                    nc.vector.tensor_reduce(first[:, :], lg[:, :, :], AX.X, ALU.max).then_inc(s["pick_out"], 1)
                    dve.wait_ge(s["pick_out"], b + 1)
                    nc.vector.tensor_tensor(onehot[:, :, :], down_count,
                                            first[:, :].unsqueeze(2).to_broadcast([P, TPB, E]),
                                            ALU.is_equal).then_inc(s["hot_out"], 1)

                def experts(b, ahead):
                    dve.wait_ge(s["b2_ps"], b + 1)
                    nc.vector.tensor_tensor(acc[:, :, :], ps[:, MISC, :].rearrange("p (t h) -> p t h", t=TPB),
                                            x2[:, :, :], ALU.add).then_inc(s["acc_out"], 1)
                    if ahead:
                        values(b + 1)
                    for e in range(E):
                        if ahead:
                            maxima(b + 1, WITH_EXPERT[e])
                            if e == LAST_WITH:
                                minus_maxima(b + 1)
                        dve.wait_ge(s["down_ps"], b * E + e + 1 + 2)
                        dve.wait_ge(s["acc_out"], b * (E + 1) + e + 1 + 2)
                        for t in range(TPB):
                            last = nc.vector.scalar_tensor_tensor(
                                out=acc[:, t, :], in0=ps[:, MOE2[e % 2], t * H:(t + 1) * H], scalar=onehot[:, t, e:e + 1],
                                in1=acc[:, t, :], op0=ALU.mult, op1=ALU.add)
                        last.then_inc(s["acc_out"], 1)
                    dve.wait_ge(s["acc_out"], (b + 1) * (E + 1) + 2)
                    tiles = bass.ds(b * TPB, TPB)
                    nc.vector.tensor_tensor(x_sb[:, tiles, :], x_sb[:, tiles, :], acc[:, :, :],
                                            ALU.add).then_inc(s["x_out"], 1)

                norms(0)
                normed(0)
                dve.wait_ge(s["qk_sb"], 2)
                split_parts(dve, nc.vector, qk[:, :, :], part, (rest[:, :, 0, :], rest[:, :, 1, :]), s, 0)
                values(0)
                maxima(0, range(HEADS_Q))
                minus_maxima(0)
                with dve.Fori(0, B - 1) as b:
                    attention(b, True)
                    router(b)
                    experts(b, True)
                attention(B - 1, False)
                router(B - 1)
                experts(B - 1, False)

            @block.tensor
            def _(pe):
                pe.wait_ge(s["v_zeroed"], 2)
                pe.sem_inc(s["pv_ps"], 2)
                pe.sem_inc(s["oT_ps"], 1)
                pe.sem_inc(s["down_ps"], 2)

                def turn(src, done):
                    for t in range(TPB):
                        last = nc.tensor.transpose(ps[:, MISC, t * P:(t + 1) * P], src(t), core.ident[:, :])
                    last.then_inc(done, 1)

                def turn_normed(b):
                    pe.wait_ge(s["ln_done"], 2 * b + 2)
                    turn(lambda t: ln["ln1"]["out"][:, t, :], s["hT_ps"])

                def project(b, i):
                    if i == 0:
                        pe.wait_ge(s["hT_sb"], b + 1)
                    else:
                        pe.wait_ge(s["qk_sb"], 2 * b + 1)
                    nc.tensor.matmul(ps[:, PROJ, :], w[("f_wq", "f_wk")[i]], hnT[:, :],
                                     start=True, stop=True).then_inc(s["qk_ps"], 1)

                def project_values(b):
                    for t in range(TPB):
                        last = nc.tensor.matmul(ps[:, MISC, t * H:(t + 1) * H], hnT[:, t * P:(t + 1) * P], w["f_wv"],
                                                start=True, stop=True)
                    last.then_inc(s["v_ps"], 1)

                def for_maximum(b, i):
                    hd, t = i // TPB, i % TPB
                    if i == 0:
                        pe.wait_ge(s["q_loaded"], 16 * PARTS * (b + 1))
                        pe.wait_ge(s["k_loaded"], 16 * PARTS * (b + 1))
                    pe.wait_ge(s["max_out"], b * HEADS_Q + i + 1)
                    nc.tensor.matmul(ps[:, MAXQ[i % 2], :], q_op[0:QK_ROWS, hd, t * P:(t + 1) * P],
                                     k_op[0:QK_ROWS, hd, :], start=True, stop=True).then_inc(s["max_ps"], 1)

                def turn_maxima(b):
                    pe.wait_ge(s["v_sb"], b + 1)
                    pe.wait_ge(s["max_out"], (b + 1) * HEADS_Q + 2)
                    pe.sem_inc(s["passed"], 1)
                    nc.tensor.transpose(ps[0:HEADS_Q, MISC, 0:P], row_max[:, :, :].rearrange("p h t -> p (h t)"),
                                        core.ident[:, :]).then_inc(s["mT_ps"], 1)

                def attention(b, ahead):
                    pe.wait_ge(s["m_loaded"], 16 * (b + 1))

                    def scores(q):
                        g, t = q // TPB, q % TPB
                        for pair in range(PAIRS):
                            i = q * PAIRS + pair
                            pe.wait_ge(s["e_out"], b * STEPS * PAIRS + i + 1)
                            for k in range(2):
                                hd = g * GROUP + 2 * pair + k
                                last = nc.tensor.matmul(ps[:, SCORE[i % 2] + k, :], k_op[:, hd, t * P:(t + 1) * P],
                                                        q_op[:, hd, :], start=True, stop=True)
                            last.then_inc(s["s_ps"], 1)

                    def weighted(q):
                        g, t = q // TPB, q % TPB
                        pe.wait_ge(s["e_out"], b * STEPS * PAIRS + (q + 1) * PAIRS + 2)
                        if t == 0:
                            pe.wait_ge(s["o_raw_out"], b * GROUPS + g + 1)
                        if q == TPB:
                            pe.wait_ge(s["acc_out"], b * (E + 1) + 2)
                        for hh in range(GROUP):
                            last = nc.tensor.matmul(ps[hh * HEAD_COLS:(hh + 1) * HEAD_COLS, O_BANK[g % 2], :],
                                                    v_op[:, t, g * GROUP + hh, :], e_sb[:, q % 2, hh, :],
                                                    start=(t == 0), stop=(t == TPB - 1))
                        last.then_inc(s["pv_ps"], 1)

                    def turn_group(g):
                        pe.wait_ge(s["o_raw_out"], b * GROUPS + g + 3)
                        if g > 0:
                            pe.wait_ge(s["o_out"], b * GROUPS + g)
                        else:
                            pe.wait_ge(s["m_split"], 5 * b + 2)
                        turn(lambda t: o_raw[:, t * P:(t + 1) * P], s["oT_ps"])

                    for q in range(STEPS + 1):
                        if q < STEPS:
                            scores(q)
                        if q >= 1:
                            weighted(q - 1)
                        if q % TPB == 2 and q > TPB:
                            turn_group(q // TPB - 1)
                        if ahead and q == AHEAD_AT:
                            pe.wait_ge(s["o_out"], b * GROUPS + 1)
                            turn_normed(b + 1)
                        if ahead and q in (AHEAD_AT + 1, AHEAD_AT + 2):
                            project(b + 1, q - AHEAD_AT - 1)
                    turn_group(GROUPS - 1)
                    pe.wait_ge(s["o_out"], (b + 1) * GROUPS)
                    turn(lambda t: o_nat[:, t, :, :].rearrange("p h d -> p (h d)"), s["on_ps"])
                    pe.wait_ge(s["on_sb"], b + 1)
                    for t in range(TPB):
                        last = nc.tensor.matmul(ps[:, MISC, t * H:(t + 1) * H], oT[:, t * P:(t + 1) * P], w["f_wo"],
                                                start=True, stop=True)
                    last.then_inc(s["wo_ps"], 1)
                    pe.wait_ge(s["ln2_done"], b + 1)
                    turn(lambda t: ln["ln2"]["out"][:, t, :], s["h2_ps"])
                    pe.wait_ge(s["h2_sb"], b + 1)
                    for t in range(TPB):
                        last = nc.tensor.matmul(ps[:, MISC, t * E:(t + 1) * E], h2T[:, t * P:(t + 1) * P], w["gate_w"],
                                                start=True, stop=True)
                    last.then_inc(s["lg_ps"], 1)

                def experts(b, ahead):
                    def up(e, f):
                        i = e * FT + f
                        if i >= 2:
                            pe.wait_ge(s["mid_out"], b * E * FT + i - 1)
                        nc.tensor.matmul(ps[:, UP[i % 2], :], w1[:, e, f * P:(f + 1) * P], h2T[:, :],
                                         start=True, stop=True).then_inc(s["up_ps"], 1)

                    def down(e, t):
                        if t == 0:
                            pe.wait_ge(s["mid_out"], b * E * FT + (e + 1) * FT)
                            if e >= 2:
                                pe.wait_ge(s["acc_out"], b * (E + 1) + e + 2)
                        for f in range(FT):
                            last = nc.tensor.matmul(ps[:, MOE2[e % 2], t * H:(t + 1) * H],
                                                    mid[:, e % 2, f, t * P:(t + 1) * P], w2[:, e, f, :],
                                                    start=(f == 0), stop=(f == FT - 1))
                        if t == TPB - 1:
                            last.then_inc(s["down_ps"], 1)

                    pe.wait_ge(s["weights_in"], 32)
                    for f in range(FT):
                        up(0, f)
                    pe.wait_ge(s["hot_out"], b + 1)
                    for t in range(TPB):
                        last = nc.tensor.transpose(ps[0:E, MISC, t * P:(t + 1) * P], onehot[:, t, :], core.ident[:, :])
                    last.then_inc(s["hotT_ps"], 1)
                    pe.wait_ge(s["hotT_sb"], b + 1)
                    for t in range(TPB):
                        last = nc.tensor.matmul(ps[:, MISC, t * H:(t + 1) * H], onehotT[:, t * P:(t + 1) * P], w["f_b2"],
                                                start=True, stop=True)
                    last.then_inc(s["b2_ps"], 1)
                    if ahead:
                        pe.wait_ge(s["acc_out"], b * (E + 1) + 1 + 2)
                        project_values(b + 1)
                    for e in range(E):
                        steps = [(up, e + 1, f) for f in range(FT) if e + 1 < E] + [(down, e, t) for t in range(TPB)]
                        some = list(WITH_EXPERT[e]) if ahead else []
                        for k, (product, of, part_of) in enumerate(steps):
                            product(of, part_of)
                            for i in some[k * len(some) // len(steps):(k + 1) * len(some) // len(steps)]:
                                for_maximum(b + 1, i)
                        if ahead and e == LAST_WITH:
                            turn_maxima(b + 1)

                turn_normed(0)
                project(0, 0)
                project(0, 1)
                project_values(0)
                for i in range(HEADS_Q):
                    for_maximum(0, i)
                turn_maxima(0)
                pe.wait_ge(s["ones_in"], 16)
                with pe.Fori(0, B - 1) as b:
                    attention(b, True)
                    experts(b, True)
                attention(B - 1, False)
                experts(B - 1, False)


BLK = 16
BLKS = P // BLK
TURNS = BLKS - 1
OFF = [0, 3 * P, 5 * P]
OFF_COLS = 6 * P


def delta_phase(core, nc):
    x_sb = core.x
    with ExitStack() as ctx:
        def sb(name, shape, dt=F32):
            return ctx.enter_context(nc.sbuf_tensor("d_" + name, shape, dt))

        ps = ctx.enter_context(nc.psum_tensor("d_ps", [P, 8, 512], F32))
        SCORE, MISC, WIDE, Z_BANK, ZT_BANK = (0, 1, 2, 3), 5, (6, 7), (4, 6), (5, 7)
        MT_BANK, STEP, TURN = (0, 1), (4, 2), (5, 3)
        ln = {"stats": sb("stats", [P, TPB, 6]), "mv": sb("mv", [P, TPB, 2]), "var_eps": sb("var", [P, TPB]),
              "rstd": sb("rstd", [P, TPB]), "out": sb("xh", [P, TPB, H])}
        hT = sb("hT", [P, S])
        early = sb("early", [P, 9 * S])
        qk, swap, rest = (early[:, i * S:(i + 2) * S].rearrange("p (i s) -> p i s", i=2) for i in (0, 2, 7))
        part = early[:, 4 * S:7 * S].bitcast(BF16).rearrange("p (i j s) -> p i j s", i=2, j=PARTS)
        e_blk, m_blk, prod, xz_blk = (early[:, i * S:(i + 2) * S].rearrange("p (t i j) -> p t i j", t=TPB, i=BLK)
                                      for i in (0, 2, 4, 6))
        shared = sb("shared", [P, NH * TPB * P])
        mT = shared[:, :].rearrange("p (t h i) -> p t h i", h=NH, t=TPB)
        k_op = shared[0:96, 0:NH * S // 2].bitcast(BF16).rearrange("p (h s) -> p h s", h=NH)
        vn = sb("vn", [P, TPB, NH, HD])
        row_max = sb("row_max", [P, NH, TPB])
        max_part = sb("max_part", [NH * TPB, PARTS, P], BF16)
        max_rest = sb("max_rest", [NH * TPB, 2, P])
        sii = sb("sii", [P, TPB, NH])
        eii = sb("eii", [P, TPB, NH])
        z_col = sb("z_col", [P, TPB, NH])
        zT = sb("zT", [TPB * NH, P])
        z_off = sb("z_off", [P, 2, 3 * P])
        e_off = sb("e_off", [P, NH, OFF_COLS])
        e_nat = sb("e_nat", [P, NH, TPB, P])
        z_blk = sb("z_blk", [P, TPB, BLK])
        zi_blk = sb("zi_blk", [P, TPB, BLK])
        xT_blk = sb("xT_blk", [P, TPB, BLK, BLK])
        xT = sb("xT", [P, NH, TPB, P])
        g_nat = sb("g_nat", [P, NH, HEAD_COLS])
        late = e_nat[:, :, :, :].rearrange("p h t j -> p (h t j)")
        gT, xg, aT = (late[:, i * S:(i + 1) * S].rearrange("p (g i) -> p g i", g=GROUPS) for i in range(3))
        a_nat = late[:, 3 * S:4 * S].rearrange("p (h c) -> p h c", h=NH)
        a_all = late[:, 4 * S:(4 + TPB) * S].rearrange("p (t h c) -> p t h c", t=TPB, h=NH)
        q_op = late[0:96, NH * S // 2:].bitcast(BF16).rearrange("p (h s) -> p h s", h=NH)

        names = ("passed set hT_ps hT_sb qk_ps qk_sb swapped rot1 rot2 rot3 split parts_stored q_loaded k_loaded v_ps v_sb "
                 "prod_out sii_ps sii_sb max_ps max_out mT_ps m_split m_stored m_loaded diff_out eii_out v_out "
                 "s_ps e_out sums_out zo_ps zo_sb zoT_ps z_out zT_ps zT_sb e_stored z_stored e_loaded z_loaded "
                 "zi_out blk_step x_stored x_loaded masked mt_ps mt_sb g_ps gT_sb gn_ps gn_sb at_ps at_sb an_ps an_sb "
                 "o_ps bias_out x_out").split()
        s = {n: core.sem("d_" + n) for n in names}
        for m in LN_NAMES:
            s["ln_" + m] = core.sem("d_ln_" + m)
        w = core.w
        q_scr, k_scr, m_scr = core.q_scr, core.k_scr, core.m_scr
        e_scr, z_scr, x_scr = core.e_scr, core.z_scr, core.x_scr
        HEADS_Q = NH * TPB
        SCORES = 3 * NH
        FREE_SCORES = len(SCORE)
        BLK_STEPS = 2 * (BLK - 1)

        def rows_first(t):
            return t.rearrange("p h t c -> p (h t) c")

        def of_half(t, half):
            n = t.shape[1] // 2
            return t[:, half * n:(half + 1) * n, :].rearrange("p g c -> p (g c)")

        def step_bank(half):
            return ps[:, STEP[half], 0:GROUPS // 2 * P]

        def turn_bank(half):
            return ps[:, TURN[half], 0:GROUPS // 2 * P]

        with nc.Block() as block:
            @block.gpsimd
            def _(pool):
                nc.gpsimd.memset(xT[:, :, :, :], 0.0).then_inc(s["set"], 1)

                def early(b, split):
                    layer_norm_rstd(nc, pool, core, ln, s, "ln", b + 1)
                    if split:
                        pool.wait_ge(s["rot3"], b + 1)
                        split_parts(pool, nc.gpsimd, qk, part, (rest, rest), s, b)

                def mask(b):
                    pool.wait_ge(s["e_stored"], 16 * BLKS * (b + 1))
                    pool.wait_ge(s["sums_out"], NH * (b + 1))
                    for hd in range(NH):
                        nc.gpsimd.tensor_tensor(e_nat[:, hd, :, :], e_nat[:, hd, :, :],
                                                w["off_blocks"].unsqueeze(1).to_broadcast([P, TPB, P]),
                                                ALU.mult).then_inc(s["masked"], 1)

                early(0, False)
                with pool.Fori(0, B - 1) as b:
                    mask(b)
                    pool.wait_ge(s["x_stored"], 16 * (b + 1))
                    early(b + 1, True)
                mask(B - 1)

            @block.sync
            def _(sp):
                def parts_to_dram(b):
                    sp.wait_ge(s["split"], (b + 1) * (2 * PARTS - 1))
                    for i, scr in enumerate((q_scr, k_scr)):
                        for j in range(PARTS):
                            sp.dma_start(scr[b, j].rearrange("d h s -> h d s"), part[:, i, j, :]).then_inc(s["parts_stored"], 16)
                    sp.wait_ge(s["parts_stored"], 16 * 2 * PARTS * (b + 1))

                def q_operand(b):
                    load_operand(sp, q_op, q_scr[b], 0, s["q_loaded"])

                def k_operand(b):
                    load_operand(sp, k_op, k_scr[b], 1, s["k_loaded"])
                    sp.dma_start(k_op[QK_ROWS:SHIFT_ROWS, :, :],
                                 core.dram["ones"].rearrange("j (h s) -> j h s", h=NH)).then_inc(s["k_loaded"], 16)

                def blocks(b):
                    sp.wait_ge(s["m_split"], 5 * (b + 1))
                    sp.dma_start(m_scr[b].rearrange("j r s -> r j s"), max_part[:, :, :]).then_inc(s["m_stored"], 16)
                    sp.wait_ge(s["m_stored"], 16 * (b + 1))
                    sp.dma_start(q_op[QK_ROWS:SHIFT_ROWS, :, :],
                                 m_scr[b].rearrange("j (h t) s -> j h (t s)", t=TPB)).then_inc(s["m_loaded"], 16)
                    sp.wait_ge(s["e_out"], (b + 1) * SCORES + FREE_SCORES)
                    for k in range(BLKS):
                        own = slice(k * BLK, (k + 1) * BLK)
                        sp.dma_start(e_scr[b, k].rearrange("h t i j -> i (h t) j"),
                                     rows_first(e_nat[own, :, :, own])).then_inc(s["e_stored"], 16)
                    sp.wait_ge(s["e_stored"], 16 * BLKS * (b + 1))
                    sp.dma_start(e_blk[:, :, :, :], e_scr[b].rearrange("k h t i j -> (k h) t i j")).then_inc(s["e_loaded"], 16)
                    sp.wait_ge(s["zT_sb"], b + 1)
                    for t in range(TPB):
                        sp.dma_start(z_scr[b, :, :, t, :].rearrange("k h i -> h k i"),
                                     zT[t * NH:(t + 1) * NH, :].rearrange("h (k i) -> h k i", i=BLK)).then_inc(s["z_stored"], 16)
                    sp.wait_ge(s["z_stored"], 16 * TPB * (b + 1))
                    sp.dma_start(z_blk[:, :, :], z_scr[b].rearrange("k h t i -> (k h) t i")).then_inc(s["z_loaded"], 16)
                    sp.wait_ge(s["blk_step"], (b + 1) * (BLK_STEPS + 2))
                    sp.dma_start(x_scr[b].rearrange("k h t c i -> (k h) t c i"), xz_blk[:, :, :, :]).then_inc(s["x_stored"], 16)
                    sp.wait_ge(s["x_stored"], 16 * (b + 1))
                    for k in range(BLKS):
                        own = slice(k * BLK, (k + 1) * BLK)
                        sp.dma_start(rows_first(xT[own, :, :, own]),
                                     x_scr[b, k].rearrange("h t c i -> c (h t) i")).then_inc(s["x_loaded"], 16)

                parts_to_dram(0)
                q_operand(0)
                k_operand(0)
                with sp.Fori(0, B - 1) as b:
                    blocks(b)
                    parts_to_dram(b + 1)
                    sp.wait_ge(s["mt_ps"], NH * (b + 1))
                    q_operand(b + 1)
                    sp.wait_ge(s["x_out"], TPB * b + TPB // 2)
                    k_operand(b + 1)
                blocks(B - 1)

            @block.scalar
            def _(act):
                act.sem_inc(s["e_out"], FREE_SCORES)

                def early(b):
                    act.wait_ge(s["hT_ps"], b + 1)
                    nc.scalar.copy(hT[:, :], ps[:, MISC, :]).then_inc(s["hT_sb"], 1)
                    act.wait_ge(s["qk_ps"], b + 1)
                    for i, n in enumerate(("dbq", "dbk")):
                        nc.scalar.activation(qk[:, i, :], ps[:, WIDE[i], :], ACT.Identity,
                                             bias=vec(core, n)).then_inc(s["qk_sb"], 1)

                def exponentials(b):
                    act.wait_ge(s["diff_out"], b + 1)
                    nc.scalar.activation(eii[:, :, :], sii[:, :, :], ACT.Exp, scale=SCALE).then_inc(s["eii_out"], 1)

                    def sums(g):
                        act.wait_ge(s["zo_ps"], b * GROUPS + g + 1)
                        if g >= 2:
                            act.wait_ge(s["zoT_ps"], b * GROUPS + g - 1)
                        nc.scalar.copy(z_off[:, g % 2, :], ps[:, Z_BANK[g % 2], 0:3 * P]).then_inc(s["zo_sb"], 1)

                    for hd in range(NH):
                        e_of = (e_off[:, hd, 0:OFF[1]], e_off[:, hd, OFF[1]:OFF_COLS],
                                e_nat[:, hd, :, :].rearrange("p t j -> p (t j)"))
                        for k, out in enumerate(e_of):
                            i = hd * len(e_of) + k
                            act.wait_ge(s["s_ps"], b * SCORES + i + 1)
                            nc.scalar.activation(out, ps[:, SCORE[i % FREE_SCORES], 0:out.shape[1]], ACT.Exp,
                                                 scale=SCALE).then_inc(s["e_out"], 1)
                        if hd % GROUP == GROUP - 1 and hd > GROUP:
                            sums(hd // GROUP - 1)
                    sums(GROUPS - 1)
                    act.wait_ge(s["zT_ps"], b + 1)
                    nc.scalar.copy(zT[:, :], ps[0:TPB * NH, MISC, 0:P]).then_inc(s["zT_sb"], 1)

                def solve(b):
                    for hd in range(NH):
                        act.wait_ge(s["mt_ps"], b * NH + hd + 1)
                        nc.scalar.copy(mT[:, :, hd, :], ps[:, MT_BANK[hd % 2], :].rearrange(
                            "p (t i) -> p t i", t=TPB)).then_inc(s["mt_sb"], 1)
                    for t in range(TPB):
                        first = (b * TPB + t) * BLKS

                        def turned(k, half, out):
                            act.wait_ge(s["an_ps"], 2 * (first + k) + half + 1)
                            nc.scalar.copy(of_half(out, half), turn_bank(half)).then_inc(s["an_sb"], 1)

                        turned(0, 0, a_nat)
                        with act.Fori(1, TURNS) as k:
                            turned(k - 1, 1, a_nat)
                            turned(k, 0, a_nat)
                        turned(TURNS - 1, 1, a_nat)
                        turned(TURNS, 0, a_all[:, t, :, :])
                        turned(TURNS, 1, a_all[:, t, :, :])

                early(0)
                with act.Fori(0, B - 1) as b:
                    exponentials(b)
                    early(b + 1)
                    solve(b)
                exponentials(B - 1)
                solve(B - 1)

            @block.vector
            def _(dve):
                nc.vector.memset(xT_blk[:, :, :, :], 0.0).then_inc(s["set"], 1)
                nc.vector.memset(g_nat[:, :, :], 0.0).then_inc(s["set"], 1)
                dve.wait_ge(s["set"], 3)
                for c in range(BLK):
                    last = nc.vector.memset(xT_blk[:, :, c, c:c + 1], 1.0)
                last.then_inc(s["set"], 1)
                dve.wait_ge(s["set"], 4)
                dve.sem_inc(s["max_out"], FREE_SCORES)
                swap_pairs = [i ^ 1 if i % HD < 2 else i for i in range(32)]

                def early(b):
                    layer_norm_stats(nc, dve, None, lambda t: x_sb[:, b * TPB + t, :], TPB, ln, s, "ln", b + 1)
                    dve.wait_ge(s["qk_sb"], 2 * b + 2)
                    dve.sem_inc(s["passed"], 1)
                    nc.vector.stream_shuffle(swap[:, :, :], qk[:, :, :], swap_pairs).then_inc(s["swapped"], 1)
                    dve.wait_ge(s["swapped"], b + 1)
                    nc.vector.tensor_tensor(qk[:, :, :], qk[:, :, :], w["cos"].unsqueeze(1).to_broadcast([P, 2, S]),
                                            ALU.mult).then_inc(s["rot1"], 1)
                    nc.vector.tensor_tensor(swap[:, :, :], swap[:, :, :], w["sin"].unsqueeze(1).to_broadcast([P, 2, S]),
                                            ALU.mult).then_inc(s["rot2"], 1)
                    dve.wait_ge(s["rot1"], b + 1)
                    dve.wait_ge(s["rot2"], b + 1)
                    nc.vector.tensor_tensor(qk[:, :, :], qk[:, :, :], swap[:, :, :], ALU.add).then_inc(s["rot3"], 1)
                    dve.wait_ge(s["rot3"], b + 1)
                    nc.vector.tensor_tensor(swap[:, 0, :], qk[:, 0, :], qk[:, 1, :], ALU.mult).then_inc(s["prod_out"], 1)

                def maxima(b):
                    dve.wait_ge(s["v_ps"], b + 1)
                    nc.vector.tensor_tensor(vn[:, :, :, :],
                                            ps[:, MISC, :].rearrange("p (t h d) -> p t h d", t=TPB, d=HD),
                                            row(core, "d_bv").rearrange("p (h d) -> p h d", d=HD).unsqueeze(1)
                                            .to_broadcast([P, TPB, NH, HD]), ALU.add).then_inc(s["v_sb"], 1)
                    dve.wait_ge(s["sii_ps"], b + 1)
                    nc.vector.tensor_copy(sii[:, :, :], ps[:, MISC, 0:TPB * NH].rearrange("p (t h) -> p t h", t=TPB)).then_inc(
                        s["sii_sb"], 1)
                    for i in range(HEADS_Q):
                        n = (i % TPB + 1) * P
                        dve.wait_ge(s["max_ps"], b * HEADS_Q + i + 1)
                        nc.vector.tensor_reduce(row_max[:, i // TPB, i % TPB:i % TPB + 1],
                                                ps[:, SCORE[i % FREE_SCORES], 0:n], AX.X, ALU.max).then_inc(s["max_out"], 1)
                    dve.wait_ge(s["max_out"], (b + 1) * HEADS_Q + FREE_SCORES)
                    dve.wait_ge(s["sii_sb"], b + 1)
                    nc.vector.tensor_tensor(sii[:, :, :], sii[:, :, :], row_max[:, :, :].rearrange("p h t -> p t h"),
                                            ALU.subtract).then_inc(s["diff_out"], 1)
                    dve.wait_ge(s["mT_ps"], b + 1)
                    minus = ps[0:HEADS_Q, MISC, 0:P]
                    nc.vector.tensor_scalar(max_part[:, 0, :], minus, -1.0, None, ALU.mult).then_inc(s["m_split"], 1)
                    dve.wait_ge(s["m_split"], 5 * b + 1)
                    nc.vector.scalar_tensor_tensor(out=max_rest[:, 0, :], in0=minus, scalar=-1.0, in1=max_part[:, 0, :],
                                                   op0=ALU.mult, op1=ALU.subtract).then_inc(s["m_split"], 1)
                    dve.wait_ge(s["m_split"], 5 * b + 2)
                    nc.vector.tensor_copy(max_part[:, 1, :], max_rest[:, 0, :]).then_inc(s["m_split"], 1)
                    dve.wait_ge(s["m_split"], 5 * b + 3)
                    nc.vector.tensor_tensor(max_rest[:, 1, :], max_rest[:, 0, :], max_part[:, 1, :],
                                            ALU.subtract).then_inc(s["m_split"], 1)
                    dve.wait_ge(s["m_split"], 5 * b + 4)
                    nc.vector.tensor_copy(max_part[:, 2, :], max_rest[:, 1, :]).then_inc(s["m_split"], 1)

                def blocks(b):
                    dve.wait_ge(s["eii_out"], b + 1)
                    dve.wait_ge(s["v_sb"], b + 1)
                    nc.vector.tensor_tensor(vn[:, :, :, :], vn[:, :, :, :],
                                            eii[:, :, :].unsqueeze(3).to_broadcast([P, TPB, NH, HD]),
                                            ALU.mult).then_inc(s["v_out"], 1)
                    for hd in range(NH):
                        dve.wait_ge(s["e_out"], b * SCORES + 3 * (hd + 1) + FREE_SCORES)
                        nc.vector.tensor_reduce(z_col[:, :, hd], e_nat[:, hd, :, :], AX.X, ALU.add).then_inc(s["sums_out"], 1)
                    dve.wait_ge(s["sums_out"], (b + 1) * NH)
                    nc.vector.tensor_tensor(z_col[:, :, :], z_col[:, :, :], eii[:, :, :], ALU.add).then_inc(s["z_out"], 1)
                    dve.wait_ge(s["z_out"], b * (GROUPS + 1) + 1)
                    for g in range(GROUPS):
                        dve.wait_ge(s["zoT_ps"], b * GROUPS + g + 1)
                        heads = slice(g * GROUP, (g + 1) * GROUP)
                        nc.vector.tensor_tensor(
                            z_col[:, 1:TPB, heads], z_col[:, 1:TPB, heads],
                            ps[:, ZT_BANK[g % 2], 0:3 * P].rearrange("p (t h c) -> p t h c", t=TPB - 1, c=HEAD_COLS)[:, :, :, 0],
                            ALU.add).then_inc(s["z_out"], 1)
                    done = b * (BLK_STEPS + 2)
                    dve.wait_ge(s["z_loaded"], 16 * (b + 1))
                    nc.vector.reciprocal(zi_blk[:, :, :], z_blk[:, :, :]).then_inc(s["zi_out"], 1)
                    dve.wait_ge(s["zi_out"], b + 1)
                    dve.wait_ge(s["e_loaded"], 16 * (b + 1))
                    nc.vector.tensor_tensor(m_blk[:, :, :, :], e_blk[:, :, :, :],
                                            zi_blk[:, :, :].unsqueeze(3).to_broadcast([P, TPB, BLK, BLK]),
                                            ALU.mult).then_inc(s["blk_step"], 1)
                    for i in range(1, BLK):
                        dve.wait_ge(s["blk_step"], done + 2 * i - 1)
                        nc.vector.tensor_tensor(prod[:, :, 0:i, 0:i], xT_blk[:, :, 0:i, 0:i],
                                                m_blk[:, :, i, 0:i].unsqueeze(2).to_broadcast([P, TPB, i, i]),
                                                ALU.mult).then_inc(s["blk_step"], 1)
                        dve.wait_ge(s["blk_step"], done + 2 * i)
                        nc.vector.tensor_reduce(xT_blk[:, :, 0:i, i], prod[:, :, 0:i, 0:i], AX.X,
                                                ALU.add).then_inc(s["blk_step"], 1)
                    dve.wait_ge(s["blk_step"], done + BLK_STEPS + 1)
                    nc.vector.tensor_tensor(xz_blk[:, :, :, :], xT_blk[:, :, :, :],
                                            zi_blk[:, :, :].unsqueeze(3).to_broadcast([P, TPB, BLK, BLK]),
                                            ALU.mult).then_inc(s["blk_step"], 1)

                def solve(b):
                    tiles = bass.ds(b * TPB, TPB)
                    dve.wait_ge(s["ln_done"], b + 1)
                    nc.vector.tensor_tensor(x_sb[:, tiles, :], x_sb[:, tiles, :],
                                            row(core, "d_bd").unsqueeze(1).to_broadcast([P, TPB, H]),
                                            ALU.add).then_inc(s["bias_out"], 1)

                    def add_output(t):
                        dve.wait_ge(s["o_ps"], b * TPB + t + 1)
                        dve.wait_ge(s["bias_out"], b + 1)
                        nc.vector.tensor_tensor(x_sb[:, b * TPB + t, :], x_sb[:, b * TPB + t, :], ps[:, WIDE[0], 0:H],
                                                ALU.add).then_inc(s["x_out"], 1)

                    for t in range(TPB):
                        first = (b * TPB + t) * BLKS
                        earlier = 2 * (b * (TPB - 1) + t - 1)
                        heads = [slice(half * NH // 2, (half + 1) * NH // 2) for half in range(2)]
                        if t == 0:
                            dve.wait_ge(s["v_out"], b + 1)
                            nc.vector.tensor_copy(g_nat[:, :, 0:HD], vn[:, t, :, :]).then_inc(s["gn_sb"], 2)
                        else:
                            for half in range(2):
                                dve.wait_ge(s["g_ps"], earlier + half + 1)
                                nc.vector.tensor_copy(of_half(gT, half), step_bank(half)).then_inc(s["gT_sb"], 1)
                            for half in range(2):
                                dve.wait_ge(s["gn_ps"], earlier + half + 1)
                                nc.vector.tensor_tensor(
                                    g_nat[:, heads[half], 0:HD], vn[:, t, heads[half], :],
                                    turn_bank(half).rearrange("p (h c) -> p h c", c=HEAD_COLS)[:, :, 0:HD],
                                    ALU.add).then_inc(s["gn_sb"], 1)
                            add_output(t - 1)
                        for half in range(2):
                            dve.wait_ge(s["at_ps"], 2 * first + half + 1)
                            nc.vector.tensor_copy(of_half(xg, half), step_bank(half)).then_inc(s["at_sb"], 1)
                        dve.wait_ge(s["at_sb"], 2 * first + 2)
                        dve.sem_inc(s["passed"], 1)
                        with dve.Fori(1, BLKS) as k:
                            for half in range(2):
                                dve.wait_ge(s["at_ps"], 2 * (first + k) + half + 1)
                                nc.vector.tensor_tensor(of_half(aT, half), step_bank(half), of_half(xg, half),
                                                        ALU.add).then_inc(s["at_sb"], 1)
                    add_output(TPB - 1)

                early(0)
                split_parts(dve, nc.vector, qk, part, (rest, rest), s, 0)
                with dve.Fori(0, B - 1) as b:
                    maxima(b)
                    blocks(b)
                    early(b + 1)
                    solve(b)
                maxima(B - 1)
                blocks(B - 1)
                solve(B - 1)

            @block.tensor
            def _(pe):
                pe.wait_ge(s["set"], 4)

                def turn(src, done, n=TPB, bank=MISC):
                    for t in range(n):
                        last = nc.tensor.transpose(ps[:, bank, t * P:(t + 1) * P], src(t), core.ident[:, :])
                    last.then_inc(done, 1)

                def early(b):
                    pe.wait_ge(s["ln_done"], b + 1)
                    turn(lambda t: ln["out"][:, t, :], s["hT_ps"])
                    pe.wait_ge(s["hT_sb"], b + 1)
                    for i in range(2):
                        last = nc.tensor.matmul(ps[:, WIDE[i], :], w["d_wqkv"][:, i * H:(i + 1) * H], hT[:, :],
                                                start=True, stop=True)
                    last.then_inc(s["qk_ps"], 1)

                def maxima(b):
                    for t in range(TPB):
                        last = nc.tensor.matmul(ps[:, MISC, t * H:(t + 1) * H], hT[:, t * P:(t + 1) * P],
                                                w["d_wqkv"][:, 2 * H:3 * H], start=True, stop=True)
                    last.then_inc(s["v_ps"], 1)
                    pe.wait_ge(s["prod_out"], b + 1)
                    pe.wait_ge(s["v_sb"], b + 1)
                    for t in range(TPB):
                        last = nc.tensor.matmul(ps[:, MISC, t * NH:(t + 1) * NH], swap[:, 0, t * P:(t + 1) * P],
                                                w["head_sum"], start=True, stop=True)
                    last.then_inc(s["sii_ps"], 1)
                    pe.wait_ge(s["q_loaded"], 16 * PARTS * (b + 1))
                    pe.wait_ge(s["k_loaded"], 16 * (PARTS + 1) * (b + 1))
                    for i in range(HEADS_Q):
                        hd, t = i // TPB, i % TPB
                        n = (t + 1) * P
                        bank = SCORE[i % FREE_SCORES]
                        pe.wait_ge(s["max_out"], b * HEADS_Q + i + 1)
                        nc.tensor.matmul(ps[:, bank, 0:n], q_op[0:QK_ROWS, hd, t * P:(t + 1) * P],
                                         k_op[0:QK_ROWS, hd, 0:n], start=True, stop=False)
                        nc.tensor.matmul(ps[:, bank, t * P:n], w["ident_b"], w["mask_up"],
                                         start=False, stop=True).then_inc(s["max_ps"], 1)
                    pe.wait_ge(s["max_out"], (b + 1) * HEADS_Q + FREE_SCORES)
                    pe.sem_inc(s["passed"], 1)
                    nc.tensor.transpose(ps[0:HEADS_Q, MISC, 0:P], row_max[:, :, :].rearrange("p h t -> p (h t)"),
                                        core.ident[:, :]).then_inc(s["mT_ps"], 1)

                def scores(b):
                    pe.wait_ge(s["m_loaded"], 16 * (b + 1))

                    def of_head(hd):
                        q, k = q_op[0:SHIFT_ROWS, hd, :], k_op[0:SHIFT_ROWS, hd, :]
                        i = b * SCORES + 3 * hd
                        pe.wait_ge(s["e_out"], i + 1)
                        nc.tensor.matmul(ps[:, SCORE[3 * hd % FREE_SCORES], 0:3 * P], k[:, 0:P], q[:, P:S],
                                         start=True, stop=True).then_inc(s["s_ps"], 1)
                        pe.wait_ge(s["e_out"], i + 2)
                        bank = SCORE[(3 * hd + 1) % FREE_SCORES]
                        nc.tensor.matmul(ps[:, bank, 0:2 * P], k[:, P:2 * P], q[:, 2 * P:S], start=True, stop=True)
                        nc.tensor.matmul(ps[:, bank, 2 * P:3 * P], k[:, 2 * P:3 * P], q[:, 3 * P:S],
                                         start=True, stop=True).then_inc(s["s_ps"], 1)
                        pe.wait_ge(s["e_out"], i + 3)
                        bank = SCORE[(3 * hd + 2) % FREE_SCORES]
                        nc.tensor.matmul(ps[:, bank, :], w["ident_b"], w["mask_diag4"], start=True, stop=False)
                        for t in range(TPB):
                            own = slice(t * P, (t + 1) * P)
                            last = nc.tensor.matmul(ps[:, bank, own], q[:, own], k[:, own],
                                                    start=False, stop=(t == TPB - 1))
                        last.then_inc(s["s_ps"], 1)

                    def sums(g):
                        pe.wait_ge(s["e_out"], b * SCORES + 3 * GROUP * (g + 1) + FREE_SCORES)
                        if g >= 2:
                            pe.wait_ge(s["zo_sb"], b * GROUPS + g - 1)
                        for j in range(3):
                            for hh in range(GROUP):
                                last = nc.tensor.matmul(
                                    ps[hh * HEAD_COLS:(hh + 1) * HEAD_COLS, Z_BANK[g % 2], j * P:3 * P], w["ones_f"],
                                    e_off[:, g * GROUP + hh, OFF[j]:OFF[j] + (3 - j) * P], start=(j == 0), stop=(j == 2))
                        last.then_inc(s["zo_ps"], 1)

                    def turn_sums(g):
                        pe.wait_ge(s["zo_sb"], b * GROUPS + g + 1)
                        if g == 0:
                            pe.wait_ge(s["m_split"], 5 * b + 2)
                        elif g >= 2:
                            pe.wait_ge(s["z_out"], b * (GROUPS + 1) + g)
                        turn(lambda t: z_off[:, g % 2, t * P:(t + 1) * P], s["zoT_ps"], TPB - 1, ZT_BANK[g % 2])

                    for g in range(GROUPS):
                        for hh in range(GROUP):
                            of_head(g * GROUP + hh)
                        if g >= 1:
                            sums(g - 1)
                        if g >= 2:
                            turn_sums(g - 2)
                    sums(GROUPS - 1)
                    turn_sums(GROUPS - 2)
                    turn_sums(GROUPS - 1)
                    pe.wait_ge(s["z_out"], (b + 1) * (GROUPS + 1))
                    pe.sem_inc(s["passed"], 1)
                    nc.tensor.transpose(ps[0:TPB * NH, MISC, 0:P], z_col[:, :, :].rearrange("p t h -> p (t h)"),
                                        core.ident[:, :]).then_inc(s["zT_ps"], 1)
                    pe.wait_ge(s["zT_sb"], b + 1)

                def solve(b):
                    pe.wait_ge(s["x_loaded"], 16 * BLKS * (b + 1))
                    for hd in range(NH):
                        pe.wait_ge(s["masked"], b * NH + hd + 1)
                        if hd >= 2:
                            pe.wait_ge(s["mt_sb"], b * NH + hd - 1)
                        for t in range(TPB):
                            last = nc.tensor.matmul(ps[:, MT_BANK[hd % 2], t * P:(t + 1) * P], e_nat[:, hd, t, :],
                                                    xT[:, hd, t, :], start=True, stop=True)
                        last.then_inc(s["mt_ps"], 1)
                    pe.wait_ge(s["mt_sb"], (b + 1) * NH)

                    def groups_of(half):
                        return range(half * GROUPS // 2, (half + 1) * GROUPS // 2)

                    def side_by_side(half, lhs, rhs, done):
                        for j, g in enumerate(groups_of(half)):
                            for hh in range(GROUP):
                                hd = g * GROUP + hh
                                last = nc.tensor.matmul(
                                    ps[hh * HEAD_COLS:(hh + 1) * HEAD_COLS, STEP[half], j * P:(j + 1) * P],
                                    lhs(hd), rhs(hd), start=True, stop=True)
                        last.then_inc(done, 1)

                    def turn_half(half, src, done):
                        for j, g in enumerate(groups_of(half)):
                            last = nc.tensor.transpose(ps[:, TURN[half], j * P:(j + 1) * P], src[:, g, :], core.ident[:, :])
                        last.then_inc(done, 1)

                    def output(t):
                        for g in range(GROUPS):
                            last = nc.tensor.matmul(ps[:, WIDE[0], 0:H], aT[:, g, :], w["d_wd"][:, g, :],
                                                    start=(g == 0), stop=(g == GROUPS - 1))
                        last.then_inc(s["o_ps"], 1)

                    for t in range(TPB):
                        first = (b * TPB + t) * BLKS
                        if t > 0:
                            earlier = 2 * (b * (TPB - 1) + t - 1)
                            for half in range(2):
                                pe.wait_ge(s["an_sb"], 2 * first - 1 + half)
                                for n, g in enumerate(groups_of(half)):
                                    for j in range(t):
                                        c = OFF[j] + (t - 1 - j) * P
                                        for hh in range(GROUP):
                                            hd = g * GROUP + hh
                                            last = nc.tensor.matmul(
                                                ps[hh * HEAD_COLS:(hh + 1) * HEAD_COLS, STEP[half], n * P:(n + 1) * P],
                                                a_all[:, j, hd, :], e_off[:, hd, c:c + P], start=(j == 0), stop=(j == t - 1))
                                last.then_inc(s["g_ps"], 1)
                            if t > 1:
                                pe.wait_ge(s["x_out"], b * TPB + t - 1)
                            output(t - 1)
                            for half in range(2):
                                pe.wait_ge(s["gT_sb"], earlier + half + 1)
                                turn_half(half, gT, s["gn_ps"])

                        def inverse(half):
                            pe.wait_ge(s["gn_sb"], 2 * (b * TPB + t) + half + 1)
                            side_by_side(half, lambda hd: g_nat[:, hd, :], lambda hd: xT[:, hd, t, :], s["at_ps"])

                        def product(half, k):
                            pe.wait_ge(s["an_sb"], 2 * (first + k - 1) + half + 1)
                            side_by_side(half, lambda hd: a_nat[:, hd, :], lambda hd: mT[:, t, hd, :], s["at_ps"])

                        def turned(half, k, src):
                            pe.wait_ge(s["at_sb"], 2 * (first + k) + half + 1)
                            turn_half(half, src, s["an_ps"])

                        inverse(0)
                        inverse(1)
                        turned(0, 0, xg)
                        turned(1, 0, xg)
                        product(0, 1)
                        turned(0, 1, aT)
                        product(1, 1)
                        with pe.Fori(2, BLKS) as k:
                            product(0, k)
                            turned(1, k - 1, aT)
                            turned(0, k, aT)
                            product(1, k)
                        turned(1, BLKS - 1, aT)
                    pe.wait_ge(s["x_out"], b * TPB + TPB - 1)
                    output(TPB - 1)
                    pe.wait_ge(s["an_sb"], 2 * BLKS * TPB * (b + 1))
                    pe.wait_ge(s["x_out"], b * TPB + TPB)

                early(0)
                with pe.Fori(0, B - 1) as b:
                    maxima(b)
                    scores(b)
                    early(b + 1)
                    solve(b)
                maxima(B - 1)
                scores(B - 1)
                solve(B - 1)


def store_phase(core, nc):
    stored = core.sem("stored")
    with nc.Block() as block:
        @block.sync
        def _(sp):
            sp.dma_start(core.out.rearrange("b (n p) h -> p (b n) h", p=P), core.x[:, :, :]).then_inc(stored, 16)
            sp.wait_ge(stored, 16)


@contextmanager
def semaphores_of_phase(core, nc):
    handles = []

    def allocate(name):
        handles.append(nc.alloc_semaphore(name))
        return handles[-1]

    core.sem = allocate
    yield
    core.sem = nc.alloc_semaphore
    nc.clear_and_free_semaphores(handles)
    nc.all_engine_barrier()


def build(nc, arrays, layers=(0, 1, 2, 3)):
    core = Core()
    with ExitStack() as ctx:
        core.sem = nc.alloc_semaphore
        core.dram = {}
        for name, a in arrays.items():
            core.dram[name] = nc.dram_tensor(name, a.shape, mybir.dt.from_np(a.dtype), kind="ExternalInput").ap()
        core.out = nc.dram_tensor("out_0", [B, S, H], F32, kind="ExternalOutput").ap()

        def keep(name, shape, dt=F32):
            return ctx.enter_context(nc.sbuf_tensor(name, shape, dt))

        core.x = keep("x", [P, TILES, H])[:, :, :]
        core.minus_half = keep("minus_half", [P, TPB])[:, :]
        core.w = {}
        mamba_weights = ExitStack()
        later = ("in_L0_attn_a_x", "ones", "f_w1", "f_w2")
        for name, a in sorted(arrays.items(), key=lambda item: item[0].startswith("m_")):
            if name not in later:
                core.w[name] = (mamba_weights if name.startswith("m_") else ctx).enter_context(nc.sbuf_tensor("sb_" + name, list(a.shape), mybir.dt.from_np(a.dtype)))[
                    tuple(slice(None) for _ in a.shape)]
        core.vec, core.rows, core.ident = core.w["vec"], core.w["rows"], core.w["ident"]
        core.pick = core.w["pick"]
        core.q_scr, core.k_scr = (nc.dram_tensor(n, [B, PARTS, HD, NH, S], BF16, kind="Internal").ap() for n in ("q_scr", "k_scr"))
        core.m_scr = nc.dram_tensor("m_scr", [B, PARTS, NH * TPB, P], BF16, kind="Internal").ap()
        core.e_scr = nc.dram_tensor("e_scr", [B, BLKS, NH, TPB, BLK, BLK], F32, kind="Internal").ap()
        core.x_scr = nc.dram_tensor("x_scr", [B, BLKS, NH, TPB, BLK, BLK], F32, kind="Internal").ap()
        core.z_scr = nc.dram_tensor("z_scr", [B, BLKS, NH, TPB, BLK], F32, kind="Internal").ap()
        load_phase(core, nc)
        if 0 in layers:
            with semaphores_of_phase(core, nc):
                mamba_phase(core, nc)
        mamba_weights.close()
        if 1 in layers:
            with semaphores_of_phase(core, nc):
                ffn_phase(core, nc, "f1_")
        if 2 in layers:
            with semaphores_of_phase(core, nc):
                delta_phase(core, nc)
        if 3 in layers:
            with semaphores_of_phase(core, nc):
                ffn_phase(core, nc, "f3_")
        store_phase(core, nc)


def kernel(**inputs):
    from concourse import bacc
    from concourse.bass_utils import run_bass_kernel_spmd

    nc = bacc.Bacc("TRN2", target_bir_lowering=False, num_devices=1)
    arrays = lay_out(inputs)
    build(nc, arrays)
    r = run_bass_kernel_spmd(nc, [arrays], core_ids=[0])
    return r.results[0]["out_0"]
```

```python
from contextlib import ExitStack, contextmanager

import numpy as np

import concourse.bass as bass
import concourse.mybir as mybir

F32 = mybir.dt.float32
U32 = mybir.dt.uint32
BF16 = mybir.dt.bfloat16
ALU = mybir.AluOpType
ACT = mybir.ActivationFunctionType
AX = mybir.AxisListType

P = 128
B, S, H = 4, 512, 128
T = B * S
TPB = S // P
TILES = T // P
EPS = 1e-5

MLP, N_STATE, DT_RANK, CONV_K = 256, 16, 64, 4
HALVES = MLP // P
NH, HD = 16, 8
E, F = 8, 512
FT = F // P
SCALE = float(HD) ** -0.5
SLOTS = TPB + E - 1

VEC = {}
for _name, _n in (("b1", HALVES), ("b2", HALVES), ("conv_w", HALVES * CONV_K), ("conv_b", HALVES),
                  ("A_log", HALVES * N_STATE), ("dt_b", HALVES), ("D", HALVES),
                  ("ln1_g", 1), ("ln1_b", 1), ("ln2_g", 1), ("ln2_b", 1), ("bq", 1), ("bk", 1),
                  ("moe_b1", E * FT),                   ("dbq", 1), ("dbk", 1)):
    VEC[_name] = (sum(n for _, n in VEC.values()), _n)
NVEC = sum(n for _, n in VEC.values())
ROW = {}
for _name, _n in (("m_bo", H), ("f_bv", H), ("f_bo", H), ("gate_b", E), ("d_bv", H), ("d_bd", H)):
    ROW[_name] = (sum(n for _, n in ROW.values()), _n)
NROW = sum(n for _, n in ROW.values())


def lay_out(inputs):
    g = {k: np.asarray(v) for k, v in inputs.items()}

    def a(n):
        return g["L0_attn_a_" + n]

    def f(n):
        return g["L0_ffn_" + n]

    def d(n):
        return g["L0_attn_b_" + n]

    def halves(v):
        return v.reshape(HALVES, P, -1).transpose(1, 0, 2).reshape(P, -1)

    def padded_heads(m):
        wide = np.zeros((GROUPS, GROUP, HEAD_COLS, H), np.float32)
        wide[:, :, :HD] = m.reshape(GROUPS, GROUP, HD, H)
        return wide.reshape(GROUPS, P, H).transpose(1, 0, 2)

    def rotary(fn, other):
        angle = np.tile(np.arange(S, dtype=np.float32), (P, 1))
        return np.where((np.arange(P) % HD < 2)[:, None], fn(angle), np.float32(other)).astype(np.float32)

    bf16 = mybir.dt.np(BF16)
    cols = {"b1": halves(a("b1")), "b2": halves(a("b2")), "conv_w": halves(a("conv_w")),
            "conv_b": halves(a("conv_b")), "A_log": halves(a("A_log")), "dt_b": halves(a("dt_proj_b")),
            "D": halves(a("D_skip")), "ln1_g": f("ln1_g")[:, None], "ln1_b": f("ln1_b")[:, None],
            "ln2_g": f("ln2_g")[:, None], "ln2_b": f("ln2_b")[:, None], "bq": f("bq")[:, None],
            "bk": f("bk")[:, None], "moe_b1": f("b1").reshape(E * FT, P).T,
            "dbq": d("bqkv")[0:H, None], "dbk": d("bqkv")[H:2 * H, None]}
    rows = {"m_bo": a("bo"), "f_bv": f("bv"), "f_bo": f("bo"), "gate_b": f("gate_b"),
            "d_bv": d("bqkv")[2 * H:], "d_bd": d("bd")}
    arrays = {
        "in_L0_attn_a_x": g["L0_attn_a_x"],
        "vec": np.concatenate([cols[n] for n in VEC], axis=1),
        "rows": np.broadcast_to(np.concatenate([rows[n] for n in ROW])[None, :], (P, NROW)),
        "m_W1": a("W1"), "m_W2": a("W2"),
        "m_xp": a("x_proj_w").reshape(HALVES, P, -1).transpose(1, 0, 2),
        "m_dt": a("dt_proj_w"),
        "m_Wo": a("Wo").reshape(HALVES, P, H).transpose(1, 0, 2),
        "f_wq": f("wq"), "f_wk": f("wk"), "f_wv": f("wv"), "f_wo": f("wo"), "gate_w": f("gate_w"),
        "f_w1": f("w1").transpose(1, 0, 2), "f_w2": f("w2").reshape(E, FT, P, H).transpose(2, 0, 1, 3),
        "f_b2": f("b2"), "before": np.triu(np.ones((P, P)), 1).astype(bf16),
        "all_before": np.ones((P, P), bf16), "tile_edges": np.tile(np.arange(TPB, dtype=np.float32) * P, (P, 1)),
        "slot_edges": np.tile(np.arange(SLOTS, dtype=np.float32) * P, (P, 1)),
        "expert_before": np.tile(np.tril(np.full((E, E), P, np.float32), -1).reshape(1, -1), (P, 1)),
        "countdown": np.tile(E - np.arange(E, dtype=np.float32), (P, 1)),
        "d_wqkv": d("Wqkv").T, "d_wd": padded_heads(d("Wd").T),
        "cos": rotary(np.cos, 1.0), "sin": rotary(np.sin, 0.0) * np.where(np.arange(P) % HD == 0, -1, 1)[:, None].astype(np.float32),
        "head_sum": np.kron(np.eye(NH), np.ones((HD, 1))).astype(np.float32),
        "off_blocks": 1 - np.kron(np.eye(P // 16), np.ones((16, 16))).astype(np.float32),
        "ident_b": np.eye(P).astype(bf16), "mask_up": (np.triu(np.ones((P, P)), 1) * -1e30).astype(bf16),
        "mask_diag4": np.tile(np.triu(np.ones((P, P)), 0) * -1e30, (1, TPB)).astype(bf16),
        "ones_f": np.ones((P, HEAD_COLS), np.float32), "ones": np.ones((PARTS, NH * S), bf16),
        "ident": np.eye(P, dtype=np.float32),
        "pick": np.tile(np.eye(2 * N_STATE), (3, 1)).astype(mybir.dt.np(BF16)),
    }
    return {k: np.ascontiguousarray(v) for k, v in arrays.items()}


class Core:
    pass


def vec(core, name, k=0, n=1):
    c = VEC[name][0] + k
    return core.vec[:, c:c + n]


def row(core, name):
    c, n = ROW[name]
    return core.rows[:, c:c + n]


def load_phase(core, nc):
    loaded = core.sem("x_and_weights_loaded")
    with nc.Block() as block:
        @block.sync
        def _(sp):
            n = 0
            x_tiles = core.dram["in_L0_attn_a_x"].rearrange("b (n p) h -> p (b n) h", p=P)
            for dst, src in [(core.x[:, :, :], x_tiles)] + [(core.w[k], core.dram[k]) for k in core.w]:
                sp.dma_start(dst, src).then_inc(loaded, 16)
                n += 16
            sp.wait_ge(loaded, n)

        @block.vector
        def _(dve):
            nc.vector.memset(core.minus_half[:, :], -0.5)


def mamba_phase(core, nc):
    sem, x_sb = core.sem, core.x
    with ExitStack() as ctx:
        def sb(name, shape, dt=F32):
            return ctx.enter_context(nc.sbuf_tensor("m_" + name, shape, dt))

        ps = ctx.enter_context(nc.psum_tensor("m_ps", [P, 8, 512], F32))
        XT, U_IN, G_IN, XP, DT = 0, 1, 3, 5, 6
        DECAY, B_BANK, C_BANK, Y = 0, 4, 5, 6
        AHEAD = 4
        ln = {"stats": sb("stats", [P, TPB, 6]), "mv": sb("mv", [P, TPB, 2]), "var_eps": sb("var", [P, TPB]),
              "rstd": sb("rstd", [P, TPB]), "out": sb("xn", [P, TPB, H])}
        xnT = sb("xnT", [P, S])
        u_pad = sb("u_pad", [P, HALVES, S + CONV_K - 1])
        conv = sb("conv", [P, HALVES, S])
        gate = sb("gate", [P, HALVES, T])
        u = sb("u", [P, HALVES, T])
        delta = sb("delta", [P, HALVES, T])
        du = sb("du", [P, HALVES, T])
        xp = sb("projected", [DT_RANK + 2 * N_STATE, S])
        bc = sb("bc", [3 * 32, T], BF16)
        part = sb("part", [32, S], BF16)
        bc_own = sb("bc_own", [32, S])
        rest = sb("rest", [32, 2, S])
        z_neg = sb("z_neg", [P, HALVES, S])
        e_abs = sb("e_abs", [P, HALVES, S])
        one_e = sb("one_e", [P, HALVES, S])
        lost = sb("lost", [P, HALVES, S])
        log_e = sb("log_e", [P, HALVES, S])
        A = sb("A", [P, HALVES, N_STATE])
        b_row = sb("b_row", [P, AHEAD, S])
        drive = sb("drive", [P, AHEAD, HALVES, S])
        h = sb("h", [P, 2, HALVES, S])
        hC = sb("hC", [P, 2, HALVES, S])
        yD = sb("yD", [P, HALVES, S])
        yg = sb("yg", [P, HALVES, S])

        names = ("passed pad_zeroed a_exp a_ready ln_stats ln_mv ln_var ln_rstd ln_done xT_ps xT_sb proj_ps u_in gate_out "
                 "conv_step conv_out u_out xp_ps xp_sb bc_sb split dt_ps z_out z_abs e_out one_e_out lost_out "
                 "log_out log1p_out delta_out du_out b_ps b_sb decay_out drive_out c_ps scan_out hC_out "
                 "y_ps yD_out yg_out o_ps bias_out x_out")
        s = {n: sem("m_" + n) for n in names.split()}
        W1, W2, Wx, Wdt, Wo = (core.w[n] for n in ("m_W1", "m_W2", "m_xp", "m_dt", "m_Wo"))
        FREE = {"b_sb": 1, "scan_out": AHEAD, "drive_out": AHEAD, "hC_out": 1, "y_ps": 2, "x_out": 1, "u_out": 1,
                "gate_out": 1, "split": 1}

        with nc.Block() as block:
            @block.gpsimd
            def _(pool):
                with pool.Fori(0, B) as b:
                    layer_norm_rstd(nc, pool, core, ln, s, "ln", b + 1)
                    tiles = bass.ds(b * TPB, TPB)
                    pool.wait_ge(s["ln_done"], b + 1)
                    pool.sem_inc(s["passed"], 1)
                    nc.gpsimd.tensor_tensor(x_sb[:, tiles, :], x_sb[:, tiles, :],
                                            row(core, "m_bo").unsqueeze(1).to_broadcast([P, TPB, H]),
                                            ALU.add).then_inc(s["bias_out"], 1)
                    pool.wait_ge(s["bias_out"], b + 1)
                pool.sem_inc(s["split"], FREE["split"])
                with pool.Fori(0, B) as b:
                    now = bass.ds(b * S, S)
                    pool.wait_ge(s["bc_sb"], b + 1)
                    pool.sem_inc(s["passed"], 1)
                    nc.gpsimd.tensor_copy(bc[0:32, now], bc_own[:, :]).then_inc(s["split"], 1)
                    pool.wait_ge(s["split"], 6 * b + 1 + FREE["split"])
                    pool.sem_inc(s["passed"], 1)
                    nc.gpsimd.tensor_tensor(rest[:, 0, :], bc_own[:, :], bc[0:32, now], ALU.subtract).then_inc(s["split"], 1)
                    pool.wait_ge(s["split"], 6 * b + 2 + FREE["split"])
                    pool.sem_inc(s["passed"], 1)
                    nc.gpsimd.tensor_copy(part[:, :], rest[:, 0, :]).then_inc(s["split"], 1)
                    pool.wait_ge(s["split"], 6 * b + 3 + FREE["split"])
                    pool.sem_inc(s["passed"], 1)
                    nc.gpsimd.tensor_copy(bc[32:64, now], part[:, :]).then_inc(s["split"], 1)
                    nc.gpsimd.tensor_tensor(rest[:, 1, :], rest[:, 0, :], part[:, :], ALU.subtract).then_inc(s["split"], 1)
                    pool.wait_ge(s["split"], 6 * b + 5 + FREE["split"])
                    pool.sem_inc(s["passed"], 1)
                    nc.gpsimd.tensor_copy(bc[64:96, now], rest[:, 1, :]).then_inc(s["split"], 1)
                    pool.wait_ge(s["split"], 6 * b + 6 + FREE["split"])
                pool.sem_inc(s["drive_out"], FREE["drive_out"])
                with pool.Fori(0, B) as b:
                    now = bass.ds(b * S, S)
                    pool.wait_ge(s["du_out"], b + 1)
                    for n in range(N_STATE):
                        step = b * N_STATE + n
                        pool.wait_ge(s["b_sb"], step + 1 + FREE["b_sb"])
                        pool.wait_ge(s["scan_out"], step + 1)
                        pool.sem_inc(s["passed"], 1)
                        nc.gpsimd.tensor_tensor(drive[:, n % AHEAD, :, :], du[:, :, now],
                                                b_row[:, n % AHEAD, :].unsqueeze(1).to_broadcast([P, HALVES, S]),
                                                ALU.mult).then_inc(s["drive_out"], 1)

            @block.scalar
            def _(act):
                nc.scalar.activation(A[:, :, :], vec(core, "A_log", 0, HALVES * N_STATE).rearrange(
                    "p (a n) -> p a n", a=HALVES), ACT.Exp).then_inc(s["a_exp"], 1)
                act.wait_ge(s["pad_zeroed"], 1)

                def turned(b):
                    act.wait_ge(s["xT_ps"], b + 1)
                    nc.scalar.copy(xnT[:, :], ps[:, XT, :]).then_inc(s["xT_sb"], 1)

                def projected(b, ahead):
                    now = bass.ds(b * S, S)
                    act.wait_ge(s["proj_ps"], b + 1)
                    for k in range(HALVES):
                        nc.scalar.activation(u_pad[:, k, CONV_K - 1:], ps[:, U_IN + k, :], ACT.Identity,
                                             bias=vec(core, "b1", k)).then_inc(s["u_in"], 1)
                    for k in range(HALVES):
                        nc.scalar.activation(gate[:, k, now], ps[:, G_IN + k, :], ACT.Sigmoid,
                                             bias=vec(core, "b2", k)).then_inc(s["gate_out"], 1)
                    if ahead:
                        turned(b + 1)
                    act.wait_ge(s["conv_out"], b + 1)
                    act.sem_inc(s["passed"], 1)
                    nc.scalar.activation(u[:, :, now], conv[:, :, :], ACT.Sigmoid).then_inc(s["u_out"], 1)

                act.sem_inc(s["u_out"], FREE["u_out"])
                act.sem_inc(s["gate_out"], FREE["gate_out"])
                turned(0)
                with act.Fori(0, B - 1) as b:
                    projected(b, True)
                projected(B - 1, False)
                with act.Fori(0, B) as b:
                    act.wait_ge(s["z_abs"], b + 1)
                    nc.scalar.activation(e_abs[:, :, :], z_neg[:, :, :], ACT.Exp).then_inc(s["e_out"], 1)
                    act.wait_ge(s["one_e_out"], b + 1)
                    nc.scalar.activation(log_e[:, :, :], one_e[:, :, :], ACT.Ln).then_inc(s["log_out"], 1)
                act.wait_ge(s["a_ready"], 1)
                act.sem_inc(s["b_sb"], FREE["b_sb"])
                with act.Fori(0, B) as b:
                    now = bass.ds(b * S, S)
                    act.wait_ge(s["delta_out"], b + 1)
                    for n in range(N_STATE):
                        step = b * N_STATE + n
                        act.wait_ge(s["b_ps"], step + 1)
                        act.wait_ge(s["drive_out"], step + 1)
                        nc.scalar.copy(b_row[:, n % AHEAD, :], ps[:, B_BANK, :]).then_inc(s["b_sb"], 1)
                        act.wait_ge(s["scan_out"], step + AHEAD - 1)
                        act.sem_inc(s["passed"], 1)
                        for k in range(HALVES):
                            last = nc.scalar.activation(ps[:, DECAY + HALVES * (n % 2) + k, :], delta[:, k, now],
                                                        ACT.Exp, scale=A[:, k, n:n + 1])
                        last.then_inc(s["decay_out"], 1)

            @block.vector
            def _(dve):
                nc.vector.memset(u_pad[:, :, 0:CONV_K - 1], 0.0).then_inc(s["pad_zeroed"], 1)
                dve.wait_ge(s["a_exp"], 1)
                nc.vector.tensor_scalar(A[:, :, :], A[:, :, :], -1.0, None, ALU.mult).then_inc(s["a_ready"], 1)

                def norm(b):
                    layer_norm_stats(nc, dve, None, lambda t: x_sb[:, b * TPB + t, :], TPB, ln, s, "ln", b + 1)

                def convolve(b):
                    dve.wait_ge(s["u_in"], HALVES * (b + 1))
                    dve.wait_ge(s["u_out"], b + FREE["u_out"])
                    for k in range(HALVES):
                        last = nc.vector.tensor_scalar(conv[:, k, :], u_pad[:, k, 0:S], vec(core, "conv_w", k * CONV_K),
                                                       vec(core, "conv_b", k), ALU.mult, ALU.add)
                    last.then_inc(s["conv_step"], 1)
                    for j in range(1, CONV_K):
                        dve.wait_ge(s["conv_step"], b * (CONV_K - 1) + j)
                        for k in range(HALVES):
                            last = nc.vector.scalar_tensor_tensor(
                                out=conv[:, k, :], in0=u_pad[:, k, j:j + S], scalar=vec(core, "conv_w", k * CONV_K + j),
                                in1=conv[:, k, :], op0=ALU.mult, op1=ALU.add)
                        last.then_inc(s["conv_step"] if j < CONV_K - 1 else s["conv_out"], 1)

                norm(0)
                with dve.Fori(0, B - 1) as b:
                    dve.wait_ge(s["xT_ps"], b + 1)
                    norm(b + 1)
                    convolve(b)
                convolve(B - 1)

                def time_steps(b):
                    dve.wait_ge(s["xp_ps"], b + 1)
                    nc.vector.tensor_copy(xp[0:DT_RANK, :], ps[0:DT_RANK, XP, :]).then_inc(s["xp_sb"], 1)

                def b_and_c(b):
                    dve.wait_ge(s["split"], 6 * b + FREE["split"])
                    nc.vector.tensor_copy(bc_own[:, :], ps[DT_RANK:DT_RANK + 2 * N_STATE, XP, :]).then_inc(s["bc_sb"], 1)

                def softplus(b, ahead):
                    now = bass.ds(b * S, S)
                    dve.wait_ge(s["dt_ps"], b + 1)
                    for k in range(HALVES):
                        last = nc.vector.tensor_scalar(delta[:, k, now], ps[:, DT + k, :], vec(core, "dt_b", k), None,
                                                       ALU.add)
                    last.then_inc(s["z_out"], 1)
                    dve.wait_ge(s["z_out"], b + 1)
                    nc.vector.scalar_tensor_tensor(out=z_neg[:, :, :], in0=delta[:, :, now], scalar=-1.0,
                                                   in1=delta[:, :, now], op0=ALU.mult,
                                                   op1=ALU.min).then_inc(s["z_abs"], 1)
                    if ahead:
                        time_steps(b + 1)
                    dve.wait_ge(s["e_out"], b + 1)
                    nc.vector.tensor_scalar(one_e[:, :, :], e_abs[:, :, :], 1.0, None,
                                            ALU.add).then_inc(s["one_e_out"], 1)
                    dve.wait_ge(s["one_e_out"], b + 1)
                    nc.vector.scalar_tensor_tensor(out=lost[:, :, :], in0=one_e[:, :, :], scalar=-1.0, in1=e_abs[:, :, :],
                                                   op0=ALU.add, op1=ALU.subtract).then_inc(s["lost_out"], 1)
                    dve.wait_ge(s["lost_out"], b + 1)
                    dve.wait_ge(s["log_out"], b + 1)
                    nc.vector.tensor_tensor(lost[:, :, :], log_e[:, :, :], lost[:, :, :],
                                            ALU.subtract).then_inc(s["log1p_out"], 1)
                    dve.wait_ge(s["log1p_out"], b + 1)
                    nc.vector.scalar_tensor_tensor(out=delta[:, :, now], in0=delta[:, :, now], scalar=0.0,
                                                   in1=lost[:, :, :], op0=ALU.max,
                                                   op1=ALU.add).then_inc(s["delta_out"], 1)
                    dve.wait_ge(s["delta_out"], b + 1)
                    nc.vector.tensor_tensor(du[:, :, now], delta[:, :, now], u[:, :, now],
                                            ALU.mult).then_inc(s["du_out"], 1)
                    if ahead:
                        b_and_c(b + 1)

                time_steps(0)
                b_and_c(0)
                with dve.Fori(0, B - 1) as b:
                    softplus(b, True)
                softplus(B - 1, False)
                dve.sem_inc(s["scan_out"], FREE["scan_out"])
                dve.sem_inc(s["hC_out"], FREE["hC_out"])
                dve.sem_inc(s["x_out"], FREE["x_out"])

                def add_output(b):
                    tiles = bass.ds(b * TPB, TPB)
                    dve.wait_ge(s["o_ps"], b + 1)
                    dve.wait_ge(s["bias_out"], B)
                    dve.sem_inc(s["passed"], 1)
                    nc.vector.tensor_tensor(x_sb[:, tiles, :], x_sb[:, tiles, :],
                                            ps[:, Y, :].rearrange("p (t h) -> p t h", t=TPB),
                                            ALU.add).then_inc(s["x_out"], 1)

                def scan(b, before):
                    now = bass.ds(b * S, S)
                    for n in range(N_STATE):
                        step = b * N_STATE + n
                        dve.wait_ge(s["decay_out"], step + 1)
                        dve.wait_ge(s["drive_out"], step + 1 + FREE["drive_out"])
                        for k in range(HALVES):
                            last = nc.vector.tensor_tensor_scan(h[:, n % 2, k, :],
                                                                ps[:, DECAY + HALVES * (n % 2) + k, :],
                                                                drive[:, n % AHEAD, k, :], 0.0, ALU.mult, ALU.add)
                        last.then_inc(s["scan_out"], 1)
                        if before and n == 0:
                            add_output(b - 1)
                        dve.wait_ge(s["scan_out"], step + 1 + FREE["scan_out"])
                        dve.wait_ge(s["c_ps"], step + 1)
                        dve.wait_ge(s["y_ps"], step + 1)
                        nc.vector.tensor_tensor(hC[:, n % 2, :, :], h[:, n % 2, :, :],
                                                ps[:, C_BANK, :].unsqueeze(1).to_broadcast([P, HALVES, S]),
                                                ALU.mult).then_inc(s["hC_out"], 1)
                    dve.wait_ge(s["y_ps"], b * N_STATE + N_STATE + FREE["y_ps"])
                    for k in range(HALVES):
                        last = nc.vector.scalar_tensor_tensor(out=yD[:, k, :], in0=u[:, k, now],
                                                              scalar=vec(core, "D", k), in1=ps[:, Y + k, :],
                                                              op0=ALU.mult, op1=ALU.add)
                    last.then_inc(s["yD_out"], 1)
                    dve.wait_ge(s["yD_out"], b + 1)
                    nc.vector.tensor_tensor(yg[:, :, :], yD[:, :, :], gate[:, :, now], ALU.mult).then_inc(s["yg_out"], 1)

                scan(0, False)
                with dve.Fori(1, B) as b:
                    scan(b, True)
                add_output(B - 1)

            @block.tensor
            def _(pe):
                def turn(b):
                    pe.wait_ge(s["ln_done"], b + 1)
                    for t in range(TPB):
                        last = nc.tensor.transpose(ps[:, XT, t * P:(t + 1) * P], ln["out"][:, t, :], core.ident[:, :])
                    last.then_inc(s["xT_ps"], 1)

                def project(b):
                    pe.wait_ge(s["xT_sb"], b + 1)
                    pe.wait_ge(s["gate_out"], HALVES * b + FREE["gate_out"])
                    for k in range(HALVES):
                        nc.tensor.matmul(ps[:, U_IN + k, :], W1[:, k * P:(k + 1) * P], xnT[:, :], start=True, stop=True)
                    for k in range(HALVES):
                        last = nc.tensor.matmul(ps[:, G_IN + k, :], W2[:, k * P:(k + 1) * P], xnT[:, :],
                                                start=True, stop=True)
                    last.then_inc(s["proj_ps"], 1)

                turn(0)
                with pe.Fori(0, B - 1) as b:
                    project(b)
                    turn(b + 1)
                project(B - 1)

                def project_u(b):
                    now = bass.ds(b * S, S)
                    pe.wait_ge(s["u_out"], b + 1 + FREE["u_out"])
                    for k in range(HALVES):
                        last = nc.tensor.matmul(ps[0:DT_RANK + 2 * N_STATE, XP, :], Wx[:, k, :], u[:, k, now],
                                                start=(k == 0), stop=(k == HALVES - 1))
                    last.then_inc(s["xp_ps"], 1)

                def project_dt(b):
                    pe.wait_ge(s["xp_sb"], b + 1)
                    for k in range(HALVES):
                        last = nc.tensor.matmul(ps[:, DT + k, :], Wdt[:, k * P:(k + 1) * P], xp[0:DT_RANK, :],
                                                start=True, stop=True)
                    last.then_inc(s["dt_ps"], 1)

                project_u(0)
                project_dt(0)
                with pe.Fori(0, B - 1) as b:
                    pe.wait_ge(s["bc_sb"], b + 1)
                    project_u(b + 1)
                    pe.wait_ge(s["z_out"], b + 1)
                    project_dt(b + 1)
                pe.sem_inc(s["y_ps"], FREE["y_ps"])

                def spread(b, bank, r):
                    return nc.tensor.matmul(ps[:, bank, :], core.pick[:, r:r + 1].to_broadcast([96, P]),
                                            bc[:, bass.ds(b * S, S)], start=True, stop=True)

                def first_rows(b):
                    for m in range(2):
                        pe.wait_ge(s["b_sb"], b * N_STATE + m + FREE["b_sb"])
                        spread(b, B_BANK, m).then_inc(s["b_ps"], 1)
                    pe.wait_ge(s["hC_out"], b * N_STATE + FREE["hC_out"])
                    spread(b, C_BANK, N_STATE).then_inc(s["c_ps"], 1)

                def scan(b, ahead):
                    for n in range(N_STATE):
                        step = b * N_STATE + n
                        if n + 2 < N_STATE:
                            pe.wait_ge(s["b_sb"], step + 2 + FREE["b_sb"])
                            spread(b, B_BANK, n + 2).then_inc(s["b_ps"], 1)
                        pe.wait_ge(s["hC_out"], step + 1 + FREE["hC_out"])
                        if n + 1 < N_STATE:
                            spread(b, C_BANK, N_STATE + n + 1).then_inc(s["c_ps"], 1)
                        if n == 0:
                            pe.wait_ge(s["x_out"], b + FREE["x_out"])
                        for k in range(HALVES):
                            last = nc.tensor.matmul(ps[:, Y + k, :], core.ident[:, :], hC[:, n % 2, k, :],
                                                    start=(n == 0), stop=(n == N_STATE - 1))
                        last.then_inc(s["y_ps"], 1)
                    if ahead:
                        first_rows(b + 1)
                    pe.wait_ge(s["yg_out"], b + 1)
                    for t in range(TPB):
                        for k in range(HALVES):
                            last = nc.tensor.matmul(ps[:, Y, t * H:(t + 1) * H], yg[:, k, t * P:(t + 1) * P],
                                                    Wo[:, k, :], start=(k == 0), stop=(k == HALVES - 1))
                    last.then_inc(s["o_ps"], 1)

                pe.wait_ge(s["split"], 6 * B + FREE["split"])
                first_rows(0)
                with pe.Fori(0, B - 1) as b:
                    scan(b, True)
                scan(B - 1, False)


def layer_norm_stats(nc, dve, pool_rstd, src, tiles, buf, s, pre, i):
    for t in range(tiles):
        last = nc.vector.bn_stats(buf["stats"][:, t, :], src(t))
    last.then_inc(s[pre + "_stats"], 1)
    dve.wait_ge(s[pre + "_stats"], i)
    dve.sem_inc(s["passed"], 1)
    for t in range(tiles):
        last = nc.vector.bn_aggr(buf["mv"][:, t, :], buf["stats"][:, t, :])
    last.then_inc(s[pre + "_mv"], 1)
    dve.wait_ge(s[pre + "_mv"], i)
    nc.vector.tensor_scalar(buf["var_eps"][:, :], buf["mv"][:, :, 1], EPS, None, ALU.add).then_inc(s[pre + "_var"], 1)
    dve.wait_ge(s[pre + "_rstd"], i)
    for t in range(tiles):
        last = nc.vector.tensor_scalar(buf["out"][:, t, :], src(t), buf["mv"][:, t, 0:1], buf["rstd"][:, t:t + 1],
                                       ALU.subtract, ALU.mult)
    last.then_inc(s[pre + "_done"], 1)


def layer_norm_rstd(nc, pool, core, buf, s, pre, i):
    pool.wait_ge(s[pre + "_var"], i)
    nc.gpsimd.tensor_tensor(buf["rstd"][:, :], buf["var_eps"][:, :], core.minus_half[:, 0:TPB],
                            ALU.pow).then_inc(s[pre + "_rstd"], 1)


LN_NAMES = ("stats", "mv", "var", "rstd", "done")
PARTS = 3
QK_ROWS = PARTS * PARTS * HD
SHIFT_ROWS = QK_ROWS + PARTS
HEAD_COLS = 32
GROUP = P // HEAD_COLS
GROUPS = NH // GROUP


def split_parts(eng, ops, src, part, rest, s, b):
    done = b * (2 * PARTS - 1)
    for j in range(PARTS):
        eng.sem_inc(s["passed"], 1)
        ops.tensor_copy(part[:, :, j, :], src).then_inc(s["split"], 1)
        eng.wait_ge(s["split"], done + 2 * j + 1)
        if j < PARTS - 1:
            ops.tensor_tensor(rest[j], src, part[:, :, j, :], ALU.subtract).then_inc(s["split"], 1)
            eng.wait_ge(s["split"], done + 2 * j + 2)
            src = rest[j]


def load_operand(sp, operand, parts, which, loaded):
    for i in range(PARTS):
        rows = operand[i * PARTS * HD:(i + 1) * PARTS * HD, :, :]
        if which == 0:
            source = parts[i:i + 1].to_broadcast([PARTS, HD, NH, S]).rearrange("j d h s -> j d (h s)")
        else:
            source = parts.rearrange("j d h s -> (j d) h s")
        sp.dma_start(rows, source).then_inc(loaded, 16)


def ffn_phase(core, nc, tag):
    x_sb = core.x
    with ExitStack() as ctx:
        def sb(name, shape, dt=F32):
            return ctx.enter_context(nc.sbuf_tensor(tag + name, shape, dt))

        ps = ctx.enter_context(nc.psum_tensor(tag + "ps", [P, 8, 512], F32))
        UP, MAXQ, SCORE, O_BANK, MISC, PROJ = 0, (1, 2, 3), (0, 2), (4, 6), 5, 7
        XT_BANK, MIDT_BANK, DOWN = 4, 6, 7
        ln = {}
        for n in ("ln0", "ln1", "ln2"):
            ln[n] = {"stats": sb(n + "stats", [P, TPB, 6]), "mv": sb(n + "mv", [P, TPB, 2]),
                     "var_eps": sb(n + "var", [P, TPB]), "rstd": sb(n + "rstd", [P, TPB]),
                     "out": sb(n + "out", [P, TPB, H])}
        hnT = sb("hnT", [P, S])
        qk = sb("qk", [P, 2, S])
        part = sb("part", [P, 2, PARTS, S], BF16)
        rest = sb("rest", [P, 2, 2, S])
        q_op = sb("q_op", [P, NH, S], BF16)
        k_op = sb("k_op", [P, NH, S], BF16)
        v_op = sb("v_op", [P, TPB, NH, HEAD_COLS])
        row_max = sb("row_max", [P, NH, TPB])
        max_part = sb("max_part", [NH * TPB, PARTS, P], BF16)
        max_rest = sb("max_rest", [NH * TPB, 2, P])
        e_sb = sb("e", [P, 2, GROUP, S])
        o_raw = sb("o_raw", [P, S])
        z_inv = sb("z_inv", [P, TPB, GROUP])
        o_nat = sb("o_nat", [P, TPB, NH, HD])
        oT = sb("oT", [P, S])
        x2 = sb("x2", [P, TPB, H])
        h2T = sb("h2T", [P, S])
        lg = sb("lg", [P, TPB, E])
        top = sb("top", [P, TPB])
        first = sb("first", [P, TPB])
        onehot = sb("onehot", [P, TPB, E])
        onehotT = sb("onehotT", [E, S])
        onehot_b = sb("onehot_b", [P, TPB, E], BF16)
        tiles_of = sb("tiles_of", [P, E, TPB])
        tile_count = sb("tile_count", [P, E])
        starts = sb("starts", [P, E, E])
        start = sb("start", [P, E])
        end = sb("end", [P, E])
        place = sb("place", [P, TPB, E])
        place_f = sb("place_f", [P, TPB])
        place_u = sb("place_u", [P, TPB], U32)
        ended = sb("ended", [P, SLOTS, E])
        owner_f = sb("owner_f", [P, SLOTS])
        owner = sb("owner", [P, SLOTS], U32)
        xs = sb("xs", [P, SLOTS, H])
        xsT = sb("xsT", [P, 2, P])
        mid = sb("mid", [P, 2, F])
        midT = sb("midT", [P, FT, P])
        ys = sb("ys", [P, SLOTS, H])
        y_tok = sb("y_tok", [P, TPB, H])
        acc = sb("acc", [P, TPB, H])
        w1 = sb("w1", [P, E, F])
        w2 = sb("w2", [P, E, FT, H])

        names = ("passed weights_in rows_zeroed ones_in v_zeroed hT_ps hT_sb qk_ps qk_sb split v_ps v_sb parts_stored q_loaded k_loaded "
                 "max_ps max_out mT_ps m_split m_stored m_loaded s_ps e_out pv_ps o_raw_out oT_ps z_out o_out "
                 "on_ps on_sb wo_ps x2_step x2_out h2_ps h2_sb lg_ps lg_out top_out tie_out rank_out pick_out hot_out "
                 "hotT_ps hotT_sb b2_ps acc_out x_step hotb_out count_ps route place_out owner_out xs_zeroed scattered "
                 "xs_loaded xsT_ps xsT_sb up_ps mid_out midT_ps midT_sb down_ps y_out ys_stored gathered x_out")
        s = {n: core.sem(tag + n) for n in names.split()}
        s.update({n + m: core.sem(tag + n + m) for n in ("ln_", "ln2_") for m in LN_NAMES})
        w = core.w
        q_scr, k_scr, m_scr = core.q_scr, core.k_scr, core.m_scr
        HEADS_Q = NH * TPB
        STEPS = GROUPS * TPB
        PAIRS = GROUP // 2
        ROUTE_STEPS = 10
        AHEAD_AT = 8
        FIRST_MAXIMA, BESIDE = 1, 7
        LAST_BESIDE = (HEADS_Q - FIRST_MAXIMA) // BESIDE - 1

        with nc.Block() as block:
            @block.gpsimd
            def _(pool):
                def early(b, split):
                    layer_norm_rstd(nc, pool, core, ln["ln0"], s, "ln", 2 * b + 1)
                    layer_norm_rstd(nc, pool, core, ln["ln1"], s, "ln", 2 * b + 2)
                    if split:
                        pool.wait_ge(s["qk_sb"], 2 * b + 2)
                        split_parts(pool, nc.gpsimd, qk[:, :, :], part, (rest[:, :, 0, :], rest[:, :, 1, :]), s, b)

                early(0, False)
                for operand in (q_op, k_op):
                    nc.gpsimd.memset(operand[:, :, :].rearrange("p h s -> p (h s)").bitcast(F32), 0.0).then_inc(s["rows_zeroed"], 1)
                nc.gpsimd.memset(xs[:, :, :], 0.0).then_inc(s["rows_zeroed"], 1)
                pool.wait_ge(s["rows_zeroed"], 3)

                def through_experts(b):
                    layer_norm_rstd(nc, pool, core, ln["ln2"], s, "ln2", b + 1)
                    pool.wait_ge(s["place_out"], b + 1)
                    pool.wait_ge(s["xs_zeroed"], 16)
                    pool.sem_inc(s["passed"], 1)
                    for t in range(TPB):
                        nc.gpsimd.indirect_dma_start(
                            core.xs_scr, bass.IndirectOffsetOnAxis(ap=place_u[:, t:t + 1], axis=0),
                            ln["ln2"]["out"][:, t, :], None).then_inc(s["scattered"], 16)
                    pool.wait_ge(s["ys_stored"], 16 * (b + 1))
                    pool.sem_inc(s["passed"], 1)
                    for t in range(TPB):
                        nc.gpsimd.indirect_dma_start(
                            y_tok[:, t, :], None, core.ys_scr,
                            bass.IndirectOffsetOnAxis(ap=place_u[:, t:t + 1], axis=0)).then_inc(s["gathered"], 16)

                with pool.Fori(0, B - 1) as b:
                    early(b + 1, True)
                    through_experts(b)
                through_experts(B - 1)

            @block.sync
            def _(sp):
                def operands(b):
                    sp.wait_ge(s["split"], (b + 1) * (2 * PARTS - 1))
                    for i, scr in enumerate((q_scr, k_scr)):
                        for j in range(PARTS):
                            sp.dma_start(scr[b, j].rearrange("d h s -> h d s"), part[:, i, j, :]).then_inc(s["parts_stored"], 16)
                    sp.wait_ge(s["parts_stored"], 16 * 2 * PARTS * (b + 1))
                    sp.wait_ge(s["s_ps"], b * STEPS * PAIRS + 1)
                    load_operand(sp, q_op, q_scr[b], 0, s["q_loaded"])
                    load_operand(sp, k_op, k_scr[b], 1, s["k_loaded"])

                def shifts(b):
                    sp.wait_ge(s["m_split"], 5 * (b + 1))
                    sp.dma_start(m_scr[b].rearrange("j r s -> r j s"), max_part[:, :, :]).then_inc(s["m_stored"], 16)
                    sp.wait_ge(s["m_stored"], 16 * (b + 1))
                    sp.dma_start(q_op[QK_ROWS:SHIFT_ROWS, :, :],
                                 m_scr[b].rearrange("j (h t) s -> j h (t s)", t=TPB)).then_inc(s["m_loaded"], 16)

                sp.dma_start(w1[:, :, :], core.dram["f_w1"]).then_inc(s["weights_in"], 16)
                sp.dma_start(w2[:, :, :, :], core.dram["f_w2"]).then_inc(s["weights_in"], 16)
                sp.wait_ge(s["rows_zeroed"], 3)
                sp.dma_start(core.xs_scr.rearrange("(j p) h -> p j h", p=P), xs[:, :, :]).then_inc(s["xs_zeroed"], 16)
                sp.dma_start(k_op[QK_ROWS:SHIFT_ROWS, :, :],
                             core.dram["ones"].rearrange("j (h s) -> j h s", h=NH)).then_inc(s["ones_in"], 16)
                sp.sem_inc(s["s_ps"], 1)
                operands(0)
                shifts(0)
                def sorted_rows(b):
                    sp.wait_ge(s["scattered"], 16 * TPB * (b + 1))
                    sp.dma_start(xs[:, :, :], core.xs_scr.rearrange("(j p) h -> p j h", p=P)).then_inc(s["xs_loaded"], 16)

                with sp.Fori(1, B) as b:
                    operands(b)
                    sorted_rows(b - 1)
                    shifts(b)
                sorted_rows(B - 1)

            @block.scalar
            def _(act):
                act.sem_inc(s["e_out"], 2)
                act.sem_inc(s["o_raw_out"], 2)
                act.sem_inc(s["y_out"], 1)

                def biased(b, i):
                    act.wait_ge(s["qk_ps"], 2 * b + i + 1)
                    nc.scalar.activation(qk[:, i, :], ps[:, PROJ, :], ACT.Identity,
                                         bias=vec(core, ("bq", "bk")[i])).then_inc(s["qk_sb"], 1)

                def attention(b, ahead):
                    def leave(g):
                        act.wait_ge(s["pv_ps"], b * STEPS + g * TPB + TPB + 2)
                        act.wait_ge(s["oT_ps"], b * GROUPS + g + 1)
                        nc.scalar.copy(o_raw[:, :], ps[:, O_BANK[g % 2], :]).then_inc(s["o_raw_out"], 1)

                    for q in range(STEPS):
                        act.wait_ge(s["pv_ps"], b * STEPS + q + 1)
                        for pair in range(PAIRS):
                            i = q * PAIRS + pair
                            act.wait_ge(s["s_ps"], b * STEPS * PAIRS + i + 1 + 1)
                            nc.scalar.activation(e_sb[:, q % 2, 2 * pair:2 * pair + 2, :],
                                                 ps[:, SCORE[i % 2]:SCORE[i % 2] + 2, :], ACT.Exp,
                                                 scale=SCALE).then_inc(s["e_out"], 1)
                        if q % TPB == 1 and q > TPB:
                            leave(q // TPB - 1)
                        if ahead and q in (AHEAD_AT + 2, AHEAD_AT + 3):
                            biased(b + 1, q - AHEAD_AT - 2)
                    leave(GROUPS - 1)
                    act.wait_ge(s["on_ps"], b + 1)
                    nc.scalar.copy(oT[:, :], ps[:, MISC, :]).then_inc(s["on_sb"], 1)

                def experts(b):
                    act.wait_ge(s["hotT_ps"], b + 1)
                    nc.scalar.copy(onehotT[:, :], ps[0:E, MISC, :]).then_inc(s["hotT_sb"], 1)

                    def turned(j):
                        act.wait_ge(s["xsT_ps"], b * SLOTS + j + 1)
                        nc.scalar.activation(xsT[:, j % 2, :], ps[:, XT_BANK, 0:P], ACT.Identity, bias=vec(core, "ln2_b"),
                                             scale=vec(core, "ln2_g")).then_inc(s["xsT_sb"], 1)

                    def raised(j):
                        act.wait_ge(s["up_ps"], b * SLOTS + j + 1)
                        nc.scalar.copy(mid[:, j % 2, :], ps[:, UP, :]).then_inc(s["mid_out"], 1)

                    act.wait_ge(s["owner_out"], b + 1)
                    act.sem_inc(s["passed"], 1)
                    owners = [act.value_load(owner[0:1, j:j + 1], min_val=0, max_val=E - 1) for j in range(SLOTS)]
                    first_bias = VEC["moe_b1"][0]
                    turned(0)
                    raised(0)
                    for j in range(SLOTS):
                        if j + 1 < SLOTS:
                            turned(j + 1)
                        act.wait_ge(s["midT_ps"], b * SLOTS + j + 1)
                        act.sem_inc(s["passed"], 1)
                        for f in range(FT):
                            last = nc.scalar.activation(midT[:, f, :], ps[:, MIDT_BANK, f * P:(f + 1) * P], ACT.Relu,
                                                        bias=core.vec[:, bass.ds(owners[j] * FT + (first_bias + f), 1)])
                        last.then_inc(s["midT_sb"], 1)
                        if j + 1 < SLOTS:
                            raised(j + 1)
                        act.wait_ge(s["down_ps"], b * SLOTS + j + 1)
                        nc.scalar.copy(ys[:, j, :], ps[:, DOWN, 0:H]).then_inc(s["y_out"], 1)
                    act.wait_ge(s["y_out"], (b + 1) * SLOTS + 1)
                    act.sem_inc(s["passed"], 1)
                    act.dma_start(core.ys_scr.rearrange("(j p) h -> p j h", p=P), ys[:, :, :]).then_inc(s["ys_stored"], 16)

                biased(0, 0)
                biased(0, 1)
                with act.Fori(0, B - 1) as b:
                    attention(b, True)
                    experts(b)
                attention(B - 1, False)
                experts(B - 1)

            @block.vector
            def _(dve):
                nc.vector.memset(v_op[:, :, :, :], 0.0).then_inc(s["v_zeroed"], 1)
                dve.wait_ge(s["v_zeroed"], 1)
                nc.vector.memset(v_op[:, :, :, HD:HD + 1], 1.0).then_inc(s["v_zeroed"], 1)
                dve.sem_inc(s["max_out"], len(MAXQ))

                def norms(b):
                    layer_norm_stats(nc, dve, None, lambda t: x_sb[:, b * TPB + t, :], TPB, ln["ln0"], s, "ln", 2 * b + 1)
                    dve.wait_ge(s["ln_done"], 2 * b + 1)
                    layer_norm_stats(nc, dve, None, lambda t: ln["ln0"]["out"][:, t, :], TPB, ln["ln1"], s, "ln", 2 * b + 2)

                def normed(b):
                    dve.wait_ge(s["hT_ps"], b + 1)
                    nc.vector.tensor_scalar(hnT[:, :], ps[:, MISC, :], vec(core, "ln1_g"), vec(core, "ln1_b"),
                                            ALU.mult, ALU.add).then_inc(s["hT_sb"], 1)

                def values(b):
                    dve.wait_ge(s["v_ps"], b + 1)
                    nc.vector.tensor_tensor(v_op[:, :, :, 0:HD],
                                            ps[:, MISC, :].rearrange("p (t h d) -> p t h d", t=TPB, d=HD),
                                            row(core, "f_bv").rearrange("p (h d) -> p h d", d=HD).unsqueeze(1)
                                            .to_broadcast([P, TPB, NH, HD]), ALU.add).then_inc(s["v_sb"], 1)

                def maxima(b, some):
                    for i in some:
                        dve.wait_ge(s["max_ps"], b * HEADS_Q + i + 1)
                        nc.vector.tensor_reduce(row_max[:, i // TPB, i % TPB:i % TPB + 1], ps[:, MAXQ[i % len(MAXQ)], :], AX.X,
                                                ALU.max).then_inc(s["max_out"], 1)

                def minus_maxima(b):
                    dve.wait_ge(s["mT_ps"], b + 1)
                    minus = ps[0:HEADS_Q, MISC, 0:P]
                    nc.vector.tensor_scalar(max_part[:, 0, :], minus, -1.0, None, ALU.mult).then_inc(s["m_split"], 1)
                    dve.wait_ge(s["m_split"], 5 * b + 1)
                    nc.vector.scalar_tensor_tensor(out=max_rest[:, 0, :], in0=minus, scalar=-1.0, in1=max_part[:, 0, :],
                                                   op0=ALU.mult, op1=ALU.subtract).then_inc(s["m_split"], 1)
                    dve.wait_ge(s["m_split"], 5 * b + 2)
                    nc.vector.tensor_copy(max_part[:, 1, :], max_rest[:, 0, :]).then_inc(s["m_split"], 1)
                    dve.wait_ge(s["m_split"], 5 * b + 3)
                    nc.vector.tensor_tensor(max_rest[:, 1, :], max_rest[:, 0, :], max_part[:, 1, :],
                                            ALU.subtract).then_inc(s["m_split"], 1)
                    dve.wait_ge(s["m_split"], 5 * b + 4)
                    nc.vector.tensor_copy(max_part[:, 2, :], max_rest[:, 1, :]).then_inc(s["m_split"], 1)

                def add_experts(b):
                    tiles = bass.ds(b * TPB, TPB)
                    dve.wait_ge(s["gathered"], 16 * TPB * (b + 1))
                    dve.wait_ge(s["x_step"], b + 1)
                    dve.sem_inc(s["passed"], 1)
                    nc.vector.tensor_tensor(x_sb[:, tiles, :], x_sb[:, tiles, :], y_tok[:, :, :],
                                            ALU.add).then_inc(s["x_out"], 1)

                def attention(b, ahead, before):
                    dve.wait_ge(s["ln_done"], 2 * b + 2)
                    nc.vector.tensor_tensor(x2[:, :, :], ln["ln0"]["out"][:, :, :],
                                            row(core, "f_bo").unsqueeze(1).to_broadcast([P, TPB, H]),
                                            ALU.add).then_inc(s["x2_step"], 1)
                    if ahead:
                        dve.wait_ge(s["x2_step"], b + 1)
                        norms(b + 1)
                    if before:
                        add_experts(b - 1)
                    for g in range(GROUPS):
                        dve.wait_ge(s["oT_ps"], b * GROUPS + g + 2)
                        o_ps = ps[:, MISC, :].rearrange("p (t h c) -> p t h c", t=TPB, c=HEAD_COLS)
                        nc.vector.reciprocal(z_inv[:, :, :], o_ps[:, :, :, HD]).then_inc(s["z_out"], 1)
                        dve.wait_ge(s["z_out"], b * GROUPS + g + 1)
                        nc.vector.tensor_tensor(o_nat[:, :, g * GROUP:(g + 1) * GROUP, :], o_ps[:, :, :, 0:HD],
                                                z_inv[:, :, :].unsqueeze(3).to_broadcast([P, TPB, GROUP, HD]),
                                                ALU.mult).then_inc(s["o_out"], 1)
                        if ahead and g == 0:
                            normed(b + 1)

                def router(b):
                    dve.wait_ge(s["wo_ps"], b + 1)
                    dve.wait_ge(s["x2_step"], b + 1)
                    nc.vector.tensor_tensor(x2[:, :, :], ps[:, MISC, :].rearrange("p (t h) -> p t h", t=TPB),
                                            x2[:, :, :], ALU.add).then_inc(s["x2_out"], 1)
                    dve.wait_ge(s["x2_out"], b + 1)
                    layer_norm_stats(nc, dve, None, lambda t: x2[:, t, :], TPB, ln["ln2"], s, "ln2", b + 1)
                    dve.wait_ge(s["h2_ps"], b + 1)
                    nc.vector.tensor_scalar(h2T[:, :], ps[:, MISC, :], vec(core, "ln2_g"), vec(core, "ln2_b"),
                                            ALU.mult, ALU.add).then_inc(s["h2_sb"], 1)
                    dve.wait_ge(s["lg_ps"], b + 1)
                    nc.vector.tensor_tensor(lg[:, :, :], ps[:, MISC, 0:TPB * E].rearrange("p (t e) -> p t e", t=TPB),
                                            row(core, "gate_b").unsqueeze(1).to_broadcast([P, TPB, E]),
                                            ALU.add).then_inc(s["lg_out"], 1)
                    dve.wait_ge(s["lg_out"], b + 1)
                    nc.vector.tensor_reduce(top[:, :], lg[:, :, :], AX.X, ALU.max).then_inc(s["top_out"], 1)
                    dve.wait_ge(s["top_out"], b + 1)
                    nc.vector.tensor_tensor(lg[:, :, :], lg[:, :, :], top[:, :].unsqueeze(2).to_broadcast([P, TPB, E]),
                                            ALU.is_equal).then_inc(s["tie_out"], 1)
                    dve.wait_ge(s["tie_out"], b + 1)
                    down_count = w["countdown"].unsqueeze(1).to_broadcast([P, TPB, E])
                    nc.vector.tensor_tensor(lg[:, :, :], lg[:, :, :], down_count, ALU.mult).then_inc(s["rank_out"], 1)
                    dve.wait_ge(s["rank_out"], b + 1)
                    nc.vector.tensor_reduce(first[:, :], lg[:, :, :], AX.X, ALU.max).then_inc(s["pick_out"], 1)
                    dve.wait_ge(s["pick_out"], b + 1)
                    nc.vector.tensor_tensor(onehot[:, :, :], down_count,
                                            first[:, :].unsqueeze(2).to_broadcast([P, TPB, E]),
                                            ALU.is_equal).then_inc(s["hot_out"], 1)

                def route(b):
                    done = b * ROUTE_STEPS

                    def step(n, op, *args):
                        if n:
                            dve.wait_ge(s["route"], done + n)
                        op(*args).then_inc(s["route"], 1)

                    dve.wait_ge(s["hot_out"], b + 1)
                    nc.vector.tensor_copy(onehot_b[:, :, :], onehot[:, :, :]).then_inc(s["hotb_out"], 1)
                    dve.wait_ge(s["count_ps"], b + 1)
                    rank = ps[:, UP, 0:TPB * E].rearrange("p (t e) -> p t e", e=E)
                    total = ps[:, UP, TPB * E:(TPB + 1) * E]
                    step(0, nc.vector.tensor_tensor, tiles_of[:, :, :], total.unsqueeze(2).to_broadcast([P, E, TPB]),
                         w["tile_edges"].unsqueeze(1).to_broadcast([P, E, TPB]), ALU.is_gt)
                    step(1, nc.vector.tensor_reduce, tile_count[:, :], tiles_of[:, :, :], AX.X, ALU.add)
                    step(2, nc.vector.tensor_tensor, starts[:, :, :], w["expert_before"].rearrange("p (e f) -> p e f", e=E),
                         tile_count[:, :].unsqueeze(1).to_broadcast([P, E, E]), ALU.mult)
                    step(3, nc.vector.tensor_reduce, start[:, :], starts[:, :, :], AX.X, ALU.add)
                    step(4, nc.vector.tensor_tensor, place[:, :, :], rank,
                         start[:, :].unsqueeze(1).to_broadcast([P, TPB, E]), ALU.add)
                    step(5, nc.vector.tensor_tensor, place[:, :, :], place[:, :, :], onehot[:, :, :], ALU.mult)
                    step(6, nc.vector.tensor_reduce, place_f[:, :], place[:, :, :], AX.X, ALU.add)
                    dve.wait_ge(s["route"], done + 7)
                    nc.vector.tensor_copy(place_u[:, :], place_f[:, :]).then_inc(s["place_out"], 1)
                    nc.vector.scalar_tensor_tensor(out=end[:, :], in0=tile_count[:, :], scalar=float(P), in1=start[:, :],
                                                   op0=ALU.mult, op1=ALU.add).then_inc(s["route"], 1)
                    step(8, nc.vector.tensor_tensor, ended[:, :, :], end[:, :].unsqueeze(1).to_broadcast([P, SLOTS, E]),
                         w["slot_edges"].unsqueeze(2).to_broadcast([P, SLOTS, E]), ALU.is_le)
                    step(9, nc.vector.tensor_reduce, owner_f[:, :], ended[:, :, :], AX.X, ALU.add)
                    dve.wait_ge(s["route"], done + ROUTE_STEPS)
                    nc.vector.tensor_scalar(owner[:, :], owner_f[:, :], float(E - 1), None, ALU.min).then_inc(s["owner_out"], 1)

                def experts(b, ahead):
                    route(b)
                    dve.wait_ge(s["b2_ps"], b + 1)
                    nc.vector.tensor_tensor(acc[:, :, :], ps[:, MISC, :].rearrange("p (t h) -> p t h", t=TPB),
                                            x2[:, :, :], ALU.add).then_inc(s["acc_out"], 1)
                    dve.wait_ge(s["acc_out"], b + 1)
                    tiles = bass.ds(b * TPB, TPB)
                    dve.sem_inc(s["passed"], 1)
                    nc.vector.tensor_tensor(x_sb[:, tiles, :], x_sb[:, tiles, :], acc[:, :, :],
                                            ALU.add).then_inc(s["x_step"], 1)
                    if ahead:
                        values(b + 1)
                        maxima(b + 1, range(FIRST_MAXIMA))
                    for j in range(SLOTS):
                        if ahead and j <= LAST_BESIDE:
                            maxima(b + 1, range(FIRST_MAXIMA + j * BESIDE, FIRST_MAXIMA + (j + 1) * BESIDE))
                        if ahead and j == LAST_BESIDE:
                            minus_maxima(b + 1)

                norms(0)
                normed(0)
                dve.wait_ge(s["qk_sb"], 2)
                split_parts(dve, nc.vector, qk[:, :, :], part, (rest[:, :, 0, :], rest[:, :, 1, :]), s, 0)
                values(0)
                maxima(0, range(HEADS_Q))
                minus_maxima(0)
                attention(0, True, False)
                router(0)
                experts(0, True)
                with dve.Fori(1, B - 1) as b:
                    attention(b, True, True)
                    router(b)
                    experts(b, True)
                attention(B - 1, False, True)
                router(B - 1)
                experts(B - 1, False)
                add_experts(B - 1)

            @block.tensor
            def _(pe):
                pe.wait_ge(s["v_zeroed"], 2)
                pe.sem_inc(s["pv_ps"], 2)
                pe.sem_inc(s["oT_ps"], 1)

                def turn(src, done):
                    for t in range(TPB):
                        last = nc.tensor.transpose(ps[:, MISC, t * P:(t + 1) * P], src(t), core.ident[:, :])
                    last.then_inc(done, 1)

                def turn_normed(b):
                    pe.wait_ge(s["ln_done"], 2 * b + 2)
                    turn(lambda t: ln["ln1"]["out"][:, t, :], s["hT_ps"])

                def project(b, i, used):
                    if i == 0:
                        pe.wait_ge(s["hT_sb"], b + 1)
                        pe.wait_ge(s["y_out"], used * SLOTS + 1)
                    else:
                        pe.wait_ge(s["qk_sb"], 2 * b + 1)
                    nc.tensor.matmul(ps[:, PROJ, :], w[("f_wq", "f_wk")[i]], hnT[:, :],
                                     start=True, stop=True).then_inc(s["qk_ps"], 1)

                def project_values(b):
                    for t in range(TPB):
                        last = nc.tensor.matmul(ps[:, MISC, t * H:(t + 1) * H], hnT[:, t * P:(t + 1) * P], w["f_wv"],
                                                start=True, stop=True)
                    last.then_inc(s["v_ps"], 1)

                def for_maximum(b, i):
                    hd, t = i // TPB, i % TPB
                    if i == 0:
                        pe.wait_ge(s["q_loaded"], 16 * PARTS * (b + 1))
                        pe.wait_ge(s["k_loaded"], 16 * PARTS * (b + 1))
                    pe.wait_ge(s["max_out"], b * HEADS_Q + i + 1)
                    nc.tensor.matmul(ps[:, MAXQ[i % len(MAXQ)], :], q_op[0:QK_ROWS, hd, t * P:(t + 1) * P],
                                     k_op[0:QK_ROWS, hd, :], start=True, stop=True).then_inc(s["max_ps"], 1)

                def turn_maxima(b):
                    pe.wait_ge(s["v_sb"], b + 1)
                    pe.wait_ge(s["max_out"], (b + 1) * HEADS_Q + len(MAXQ))
                    pe.sem_inc(s["passed"], 1)
                    nc.tensor.transpose(ps[0:HEADS_Q, MISC, 0:P], row_max[:, :, :].rearrange("p h t -> p (h t)"),
                                        core.ident[:, :]).then_inc(s["mT_ps"], 1)

                def attention(b, ahead):
                    pe.wait_ge(s["m_loaded"], 16 * (b + 1))

                    def scores(q):
                        g, t = q // TPB, q % TPB
                        for pair in range(PAIRS):
                            i = q * PAIRS + pair
                            pe.wait_ge(s["e_out"], b * STEPS * PAIRS + i + 1)
                            for k in range(2):
                                hd = g * GROUP + 2 * pair + k
                                last = nc.tensor.matmul(ps[:, SCORE[i % 2] + k, :], k_op[:, hd, t * P:(t + 1) * P],
                                                        q_op[:, hd, :], start=True, stop=True)
                            last.then_inc(s["s_ps"], 1)

                    def weighted(q):
                        g, t = q // TPB, q % TPB
                        pe.wait_ge(s["e_out"], b * STEPS * PAIRS + (q + 1) * PAIRS + 2)
                        if t == 0:
                            pe.wait_ge(s["o_raw_out"], b * GROUPS + g + 1)
                        for hh in range(GROUP):
                            last = nc.tensor.matmul(ps[hh * HEAD_COLS:(hh + 1) * HEAD_COLS, O_BANK[g % 2], :],
                                                    v_op[:, t, g * GROUP + hh, :], e_sb[:, q % 2, hh, :],
                                                    start=(t == 0), stop=(t == TPB - 1))
                        last.then_inc(s["pv_ps"], 1)

                    def turn_group(g):
                        pe.wait_ge(s["o_raw_out"], b * GROUPS + g + 3)
                        if g > 0:
                            pe.wait_ge(s["o_out"], b * GROUPS + g)
                        else:
                            pe.wait_ge(s["m_split"], 5 * b + 2)
                        turn(lambda t: o_raw[:, t * P:(t + 1) * P], s["oT_ps"])

                    for q in range(STEPS + 1):
                        if q < STEPS:
                            scores(q)
                        if q >= 1:
                            weighted(q - 1)
                        if q % TPB == 2 and q > TPB:
                            turn_group(q // TPB - 1)
                        if ahead and q == AHEAD_AT:
                            pe.wait_ge(s["o_out"], b * GROUPS + 1)
                            turn_normed(b + 1)
                        if ahead and q in (AHEAD_AT + 1, AHEAD_AT + 2):
                            project(b + 1, q - AHEAD_AT - 1, b)
                    turn_group(GROUPS - 1)
                    pe.wait_ge(s["o_out"], (b + 1) * GROUPS)
                    turn(lambda t: o_nat[:, t, :, :].rearrange("p h d -> p (h d)"), s["on_ps"])
                    pe.wait_ge(s["on_sb"], b + 1)
                    for t in range(TPB):
                        last = nc.tensor.matmul(ps[:, MISC, t * H:(t + 1) * H], oT[:, t * P:(t + 1) * P], w["f_wo"],
                                                start=True, stop=True)
                    last.then_inc(s["wo_ps"], 1)
                    pe.wait_ge(s["ln2_done"], b + 1)
                    turn(lambda t: ln["ln2"]["out"][:, t, :], s["h2_ps"])
                    pe.wait_ge(s["h2_sb"], b + 1)
                    for t in range(TPB):
                        last = nc.tensor.matmul(ps[:, MISC, t * E:(t + 1) * E], h2T[:, t * P:(t + 1) * P], w["gate_w"],
                                                start=True, stop=True)
                    last.then_inc(s["lg_ps"], 1)

                def experts(b, ahead):
                    pe.wait_ge(s["hotb_out"], b + 1)
                    for t in range(TPB + 1):
                        counted = min(t + 1, TPB)
                        for r in range(counted):
                            last = nc.tensor.matmul(ps[:, UP, t * E:(t + 1) * E],
                                                    w["before"] if r == t else w["all_before"], onehot_b[:, r, :],
                                                    start=(r == 0), stop=(r == counted - 1))
                    last.then_inc(s["count_ps"], 1)
                    for t in range(TPB):
                        last = nc.tensor.transpose(ps[0:E, MISC, t * P:(t + 1) * P], onehot[:, t, :], core.ident[:, :])
                    last.then_inc(s["hotT_ps"], 1)
                    pe.wait_ge(s["hotT_sb"], b + 1)
                    for t in range(TPB):
                        last = nc.tensor.matmul(ps[:, MISC, t * H:(t + 1) * H], onehotT[:, t * P:(t + 1) * P], w["f_b2"],
                                                start=True, stop=True)
                    last.then_inc(s["b2_ps"], 1)
                    if ahead:
                        pe.wait_ge(s["acc_out"], b + 1)
                        project_values(b + 1)
                    pe.wait_ge(s["owner_out"], b + 1)
                    pe.sem_inc(s["passed"], 1)
                    owners = [pe.value_load(owner[0:1, j:j + 1], min_val=0, max_val=E - 1) for j in range(SLOTS)]
                    def beside(j, part, parts=4):
                        if ahead and j <= LAST_BESIDE:
                            for k in range(part * BESIDE // parts, (part + 1) * BESIDE // parts):
                                for_maximum(b + 1, FIRST_MAXIMA + j * BESIDE + k)

                    def turn_rows(j):
                        nc.tensor.transpose(ps[:, XT_BANK, 0:P], xs[:, j, :], core.ident[:, :]).then_inc(s["xsT_ps"], 1)

                    def up(j):
                        pe.wait_ge(s["xsT_sb"], b * SLOTS + j + 1)
                        nc.tensor.matmul(ps[:, UP, :], xsT[:, j % 2, :], w1[:, owners[j], :],
                                         start=True, stop=True).then_inc(s["up_ps"], 1)

                    def turn_mid(j):
                        pe.wait_ge(s["mid_out"], b * SLOTS + j + 1)
                        for f in range(FT):
                            last = nc.tensor.transpose(ps[:, MIDT_BANK, f * P:(f + 1) * P],
                                                       mid[:, j % 2, f * P:(f + 1) * P], core.ident[:, :])
                        last.then_inc(s["midT_ps"], 1)

                    def down(j):
                        pe.wait_ge(s["midT_sb"], b * SLOTS + j + 1)
                        pe.wait_ge(s["y_out"], b * SLOTS + j + 1)
                        for f in range(FT):
                            last = nc.tensor.matmul(ps[:, DOWN, 0:H], midT[:, f, :], w2[:, owners[j], f, :],
                                                    start=(f == 0), stop=(f == FT - 1))
                        last.then_inc(s["down_ps"], 1)

                    if ahead:
                        for i in range(FIRST_MAXIMA):
                            for_maximum(b + 1, i)
                    pe.wait_ge(s["weights_in"], 32)
                    pe.wait_ge(s["xs_loaded"], 16 * (b + 1))
                    pe.sem_inc(s["passed"], 1)
                    turn_rows(0)
                    up(0)
                    for j in range(SLOTS):
                        if j + 1 < SLOTS:
                            turn_rows(j + 1)
                        beside(j, 0)
                        turn_mid(j)
                        beside(j, 1)
                        if j + 1 < SLOTS:
                            up(j + 1)
                        beside(j, 2)
                        down(j)
                        beside(j, 3)
                        if ahead and j == LAST_BESIDE:
                            turn_maxima(b + 1)

                turn_normed(0)
                project(0, 0, 0)
                project(0, 1, 0)
                project_values(0)
                for i in range(HEADS_Q):
                    for_maximum(0, i)
                turn_maxima(0)
                pe.wait_ge(s["ones_in"], 16)
                with pe.Fori(0, B - 1) as b:
                    attention(b, True)
                    experts(b, True)
                attention(B - 1, False)
                experts(B - 1, False)


BLK = 16
BLKS = P // BLK
TURNS = BLKS - 1
OFF = [0, 3 * P, 5 * P]
OFF_COLS = 6 * P


def delta_phase(core, nc):
    x_sb = core.x
    with ExitStack() as ctx:
        def sb(name, shape, dt=F32):
            return ctx.enter_context(nc.sbuf_tensor("d_" + name, shape, dt))

        ps = ctx.enter_context(nc.psum_tensor("d_ps", [P, 8, 512], F32))
        SCORE, MISC, WIDE, Z_BANK, ZT_BANK = (0, 1, 2, 3), 5, (6, 7), (4, 6), (5, 7)
        MAXQ, FIRST_MAXQ, MAX_T, MT_BANK, STEP, TURN = (0, 1), (0, 1, 2, 3), 0, (0, 1), (4, 2), (5, 3)
        ln = {"stats": sb("stats", [P, TPB, 6]), "mv": sb("mv", [P, TPB, 2]), "var_eps": sb("var", [P, TPB]),
              "rstd": sb("rstd", [P, TPB]), "out": sb("xh", [P, TPB, H])}
        hT = sb("hT", [P, S])
        early = sb("early", [P, 9 * S])
        swap, qk, rest = (early[:, i * S:(i + 2) * S].rearrange("p (i s) -> p i s", i=2) for i in (0, 2, 7))
        part = early[:, 4 * S:7 * S].bitcast(BF16).rearrange("p (i j s) -> p i j s", i=2, j=PARTS)
        k_op = early[0:96, S:9 * S].bitcast(BF16).rearrange("p (h s) -> p h s", h=NH)
        e_blk, m_blk, prod, xz_blk = (early[:, i * S:(i + 2) * S].rearrange("p (t i j) -> p t i j", t=TPB, i=BLK)
                                      for i in (1, 3, 5, 7))
        mT = sb("mT", [P, TPB, NH, P])
        v_raw = sb("v_raw", [P, TPB, NH, HD])
        vn = sb("vn", [P, TPB, NH, HD])
        row_max = sb("row_max", [P, NH, TPB])
        max_part = sb("max_part", [NH * TPB, PARTS, P], BF16)
        max_rest = sb("max_rest", [NH * TPB, 2, P])
        sii = sb("sii", [P, TPB, NH])
        eii = sb("eii", [P, TPB, NH])
        z_col = sb("z_col", [P, TPB, NH])
        zT = sb("zT", [TPB * NH, P])
        z_off = sb("z_off", [P, 2, 3 * P])
        e_off = sb("e_off", [P, NH, OFF_COLS])
        e_nat = sb("e_nat", [P, NH, TPB, P])
        z_blk = sb("z_blk", [P, TPB, BLK])
        zi_blk = sb("zi_blk", [P, TPB, BLK])
        xT_blk = sb("xT_blk", [P, TPB, BLK, BLK])
        xT = sb("xT", [P, NH, TPB, P])
        g_nat = sb("g_nat", [P, NH, HEAD_COLS])
        late = e_nat[:, :, :, :].rearrange("p h t j -> p (h t j)")
        gT, xg, aT = (late[:, i * S:(i + 1) * S].rearrange("p (g i) -> p g i", g=GROUPS) for i in range(3))
        a_nat = late[:, 3 * S:4 * S].rearrange("p (h c) -> p h c", h=NH)
        a_all = late[:, 4 * S:(4 + TPB) * S].rearrange("p (t h c) -> p t h c", t=TPB, h=NH)
        q_op = late[0:96, NH * S // 2:].bitcast(BF16).rearrange("p (h s) -> p h s", h=NH)

        names = ("passed set hT_ps hT_sb qk_ps qk_sb swapped rot1 rot2 rot3 split parts_stored q_loaded k_loaded v_ps v_sb "
                 "prod_out sii_ps sii_sb max_ps max_out mT_ps m_split m_stored m_loaded diff_out eii_out v_out "
                 "s_ps e_out sums_out zo_ps zo_sb zoT_ps z_out zT_ps zT_sb e_stored z_stored e_loaded z_loaded "
                 "zi_out blk_step x_stored x_loaded masked mt_ps mt_sb g_ps gT_sb gn_ps gn_sb at_ps at_sb an_ps an_sb "
                 "o_ps bias_out x_out").split()
        s = {n: core.sem("d_" + n) for n in names}
        for m in LN_NAMES:
            s["ln_" + m] = core.sem("d_ln_" + m)
        w = core.w
        q_scr, k_scr, m_scr = core.q_scr, core.k_scr, core.m_scr
        e_scr, z_scr, x_scr = core.e_scr, core.z_scr, core.x_scr
        HEADS_Q = NH * TPB
        BESIDE = [(0, 0), (0, TURNS - 1), (TURNS - 1, TURNS - 1), (2 * (TURNS - 1), NH - 2 * (TURNS - 1))]
        SCORES = 3 * NH
        FREE_SCORES = len(SCORE)
        BLK_STEPS = 2 * (BLK - 1)

        def rows_first(t):
            return t.rearrange("p h t c -> p (h t) c")

        def of_half(t, half):
            n = t.shape[1] // 2
            return t[:, half * n:(half + 1) * n, :].rearrange("p g c -> p (g c)")

        def step_bank(half):
            return ps[:, STEP[half], 0:GROUPS // 2 * P]

        def turn_bank(half):
            return ps[:, TURN[half], 0:GROUPS // 2 * P]

        with nc.Block() as block:
            @block.gpsimd
            def _(pool):
                nc.gpsimd.memset(xT[:, :, :, :], 0.0).then_inc(s["set"], 1)

                def split(b):
                    pool.wait_ge(s["rot3"], b + 1)
                    split_parts(pool, nc.gpsimd, qk, part, (rest, rest), s, b)

                def mask(b):
                    pool.wait_ge(s["e_stored"], 16 * BLKS * (b + 1))
                    pool.wait_ge(s["sums_out"], NH * (b + 1))
                    for hd in range(NH):
                        nc.gpsimd.tensor_tensor(e_nat[:, hd, :, :], e_nat[:, hd, :, :],
                                                w["off_blocks"].unsqueeze(1).to_broadcast([P, TPB, P]),
                                                ALU.mult).then_inc(s["masked"], 1)

                layer_norm_rstd(nc, pool, core, ln, s, "ln", 1)
                with pool.Fori(0, B - 1) as b:
                    layer_norm_rstd(nc, pool, core, ln, s, "ln", b + 2)
                    mask(b)
                    split(b + 1)
                mask(B - 1)

            @block.sync
            def _(sp):
                def parts_to_dram(b):
                    sp.wait_ge(s["split"], (b + 1) * (2 * PARTS - 1))
                    for i, scr in enumerate((q_scr, k_scr)):
                        for j in range(PARTS):
                            sp.dma_start(scr[b, j].rearrange("d h s -> h d s"), part[:, i, j, :]).then_inc(s["parts_stored"], 16)
                    sp.wait_ge(s["parts_stored"], 16 * 2 * PARTS * (b + 1))

                def q_operand(b):
                    load_operand(sp, q_op, q_scr[b], 0, s["q_loaded"])

                def k_operand(b):
                    load_operand(sp, k_op, k_scr[b], 1, s["k_loaded"])
                    sp.dma_start(k_op[QK_ROWS:SHIFT_ROWS, :, :],
                                 core.dram["ones"].rearrange("j (h s) -> j h s", h=NH)).then_inc(s["k_loaded"], 16)

                def blocks(b):
                    sp.wait_ge(s["m_split"], 5 * (b + 1))
                    sp.dma_start(m_scr[b].rearrange("j r s -> r j s"), max_part[:, :, :]).then_inc(s["m_stored"], 16)
                    sp.wait_ge(s["m_stored"], 16 * (b + 1))
                    sp.dma_start(q_op[QK_ROWS:SHIFT_ROWS, :, :],
                                 m_scr[b].rearrange("j (h t) s -> j h (t s)", t=TPB)).then_inc(s["m_loaded"], 16)
                    sp.wait_ge(s["e_out"], (b + 1) * SCORES + FREE_SCORES)
                    for k in range(BLKS):
                        own = slice(k * BLK, (k + 1) * BLK)
                        sp.dma_start(e_scr[b, k].rearrange("h t i j -> i (h t) j"),
                                     rows_first(e_nat[own, :, :, own])).then_inc(s["e_stored"], 16)
                    sp.wait_ge(s["e_stored"], 16 * BLKS * (b + 1))
                    sp.dma_start(e_blk[:, :, :, :], e_scr[b].rearrange("k h t i j -> (k h) t i j")).then_inc(s["e_loaded"], 16)
                    sp.wait_ge(s["blk_step"], (b + 1) * (BLK_STEPS + 2))
                    sp.dma_start(x_scr[b].rearrange("k h t c i -> (k h) t c i"), xz_blk[:, :, :, :]).then_inc(s["x_stored"], 16)
                    sp.wait_ge(s["x_stored"], 16 * (b + 1))
                    for k in range(BLKS):
                        own = slice(k * BLK, (k + 1) * BLK)
                        sp.dma_start(rows_first(xT[own, :, :, own]),
                                     x_scr[b, k].rearrange("h t c i -> c (h t) i")).then_inc(s["x_loaded"], 16)

                parts_to_dram(0)
                sp.wait_ge(s["prod_out"], 1)
                q_operand(0)
                k_operand(0)
                with sp.Fori(0, B - 1) as b:
                    blocks(b)
                    parts_to_dram(b + 1)
                    sp.wait_ge(s["prod_out"], b + 2)
                    k_operand(b + 1)
                    sp.wait_ge(s["mt_ps"], NH * (b + 1))
                    q_operand(b + 1)
                blocks(B - 1)

            @block.scalar
            def _(act):
                act.sem_inc(s["e_out"], FREE_SCORES)

                def normed(b):
                    act.wait_ge(s["hT_ps"], b + 1)
                    nc.scalar.copy(hT[:, :], ps[:, MISC, :]).then_inc(s["hT_sb"], 1)

                def queries_keys(b):
                    act.wait_ge(s["qk_ps"], b + 1)
                    for i, n in enumerate(("dbq", "dbk")):
                        nc.scalar.activation(qk[:, i, :], ps[:, WIDE[i], :], ACT.Identity,
                                             bias=vec(core, n)).then_inc(s["qk_sb"], 1)

                def exponentials(b):
                    act.wait_ge(s["diff_out"], b + 1)
                    nc.scalar.activation(eii[:, :, :], sii[:, :, :], ACT.Exp, scale=SCALE).then_inc(s["eii_out"], 1)

                    def sums(g):
                        act.wait_ge(s["zo_ps"], b * GROUPS + g + 1)
                        if g >= 2:
                            act.wait_ge(s["zoT_ps"], b * GROUPS + g - 1)
                        nc.scalar.copy(z_off[:, g % 2, :], ps[:, Z_BANK[g % 2], 0:3 * P]).then_inc(s["zo_sb"], 1)

                    for hd in range(NH):
                        e_of = (e_off[:, hd, 0:OFF[1]], e_off[:, hd, OFF[1]:OFF_COLS],
                                e_nat[:, hd, :, :].rearrange("p t j -> p (t j)"))
                        for k, out in enumerate(e_of):
                            i = hd * len(e_of) + k
                            act.wait_ge(s["s_ps"], b * SCORES + i + 1)
                            nc.scalar.activation(out, ps[:, SCORE[i % FREE_SCORES], 0:out.shape[1]], ACT.Exp,
                                                 scale=SCALE).then_inc(s["e_out"], 1)
                        if hd % GROUP == GROUP - 1 and hd > GROUP:
                            sums(hd // GROUP - 1)
                    sums(GROUPS - 1)
                    act.wait_ge(s["zT_ps"], b + 1)
                    nc.scalar.copy(zT[:, :], ps[0:TPB * NH, MISC, 0:P]).then_inc(s["zT_sb"], 1)
                    act.wait_ge(s["zT_sb"], b + 1)
                    for t in range(TPB):
                        act.dma_start(z_scr[b, :, :, t, :].rearrange("k h i -> h k i"),
                                     zT[t * NH:(t + 1) * NH, :].rearrange("h (k i) -> h k i", i=BLK)).then_inc(s["z_stored"], 16)
                    act.wait_ge(s["z_stored"], 16 * TPB * (b + 1))
                    act.dma_start(z_blk[:, :, :], z_scr[b].rearrange("k h t i -> (k h) t i")).then_inc(s["z_loaded"], 16)

                def solve(b):
                    for hd in range(NH):
                        act.wait_ge(s["mt_ps"], b * NH + hd + 1)
                        nc.scalar.copy(mT[:, :, hd, :], ps[:, MT_BANK[hd % 2], :].rearrange(
                            "p (t i) -> p t i", t=TPB)).then_inc(s["mt_sb"], 1)
                    for t in range(TPB):
                        first = (b * TPB + t) * BLKS

                        def turned(k, half, out):
                            act.wait_ge(s["an_ps"], 2 * (first + k) + half + 1)
                            nc.scalar.copy(of_half(out, half), turn_bank(half)).then_inc(s["an_sb"], 1)

                        turned(0, 0, a_nat)
                        with act.Fori(1, TURNS) as k:
                            turned(k - 1, 1, a_nat)
                            turned(k, 0, a_nat)
                        turned(TURNS - 1, 1, a_nat)
                        turned(TURNS, 0, a_all[:, t, :, :])
                        turned(TURNS, 1, a_all[:, t, :, :])

                normed(0)
                queries_keys(0)
                with act.Fori(0, B - 1) as b:
                    exponentials(b)
                    normed(b + 1)
                    act.wait_ge(s["x_stored"], 16 * (b + 1))
                    queries_keys(b + 1)
                    solve(b)
                exponentials(B - 1)
                solve(B - 1)

            @block.vector
            def _(dve):
                nc.vector.memset(xT_blk[:, :, :, :], 0.0).then_inc(s["set"], 1)
                nc.vector.memset(g_nat[:, :, :], 0.0).then_inc(s["set"], 1)
                dve.wait_ge(s["set"], 3)
                for c in range(BLK):
                    last = nc.vector.memset(xT_blk[:, :, c, c:c + 1], 1.0)
                last.then_inc(s["set"], 1)
                dve.wait_ge(s["set"], 4)
                dve.sem_inc(s["max_out"], len(FIRST_MAXQ))
                swap_pairs = [i ^ 1 if i % HD < 2 else i for i in range(32)]

                def normed(b):
                    layer_norm_stats(nc, dve, None, lambda t: x_sb[:, b * TPB + t, :], TPB, ln, s, "ln", b + 1)

                def rotated(b):
                    dve.wait_ge(s["qk_sb"], 2 * b + 2)
                    dve.sem_inc(s["passed"], 1)
                    nc.vector.stream_shuffle(swap[:, :, :], qk[:, :, :], swap_pairs).then_inc(s["swapped"], 1)
                    dve.wait_ge(s["swapped"], b + 1)
                    nc.vector.tensor_tensor(qk[:, :, :], qk[:, :, :], w["cos"].unsqueeze(1).to_broadcast([P, 2, S]),
                                            ALU.mult).then_inc(s["rot1"], 1)
                    nc.vector.tensor_tensor(swap[:, :, :], swap[:, :, :], w["sin"].unsqueeze(1).to_broadcast([P, 2, S]),
                                            ALU.mult).then_inc(s["rot2"], 1)
                    dve.wait_ge(s["rot1"], b + 1)
                    dve.wait_ge(s["rot2"], b + 1)
                    nc.vector.tensor_tensor(qk[:, :, :], qk[:, :, :], swap[:, :, :], ALU.add).then_inc(s["rot3"], 1)
                    dve.wait_ge(s["rot3"], b + 1)
                    nc.vector.tensor_tensor(swap[:, 0, :], qk[:, 0, :], qk[:, 1, :], ALU.mult).then_inc(s["prod_out"], 1)

                def maximum(b, hd, t, banks=MAXQ):
                    dve.wait_ge(s["max_ps"], b * HEADS_Q + hd * TPB + t + 1)
                    dve.sem_inc(s["passed"], 1)
                    nc.vector.tensor_reduce(row_max[:, hd, t:t + 1], ps[:, banks[t % len(banks)], 0:(t + 1) * P], AX.X,
                                            ALU.max).then_inc(s["max_out"], 1)

                def values(b):
                    dve.wait_ge(s["v_ps"], b + 1)
                    nc.vector.tensor_tensor(v_raw[:, :, :, :],
                                            ps[:, MISC, :].rearrange("p (t h d) -> p t h d", t=TPB, d=HD),
                                            row(core, "d_bv").rearrange("p (h d) -> p h d", d=HD).unsqueeze(1)
                                            .to_broadcast([P, TPB, NH, HD]), ALU.add).then_inc(s["v_sb"], 1)

                def own_scores(b):
                    dve.wait_ge(s["sii_ps"], b + 1)
                    nc.vector.tensor_copy(sii[:, :, :], ps[:, MISC, 0:TPB * NH].rearrange("p (t h) -> p t h", t=TPB)).then_inc(
                        s["sii_sb"], 1)

                def shift(b):
                    dve.wait_ge(s["max_out"], (b + 1) * HEADS_Q + len(FIRST_MAXQ))
                    dve.wait_ge(s["sii_sb"], b + 1)
                    nc.vector.tensor_tensor(sii[:, :, :], sii[:, :, :], row_max[:, :, :].rearrange("p h t -> p t h"),
                                            ALU.subtract).then_inc(s["diff_out"], 1)
                    dve.wait_ge(s["mT_ps"], b + 1)
                    minus = ps[0:HEADS_Q, MAX_T, 0:P]
                    nc.vector.tensor_scalar(max_part[:, 0, :], minus, -1.0, None, ALU.mult).then_inc(s["m_split"], 1)
                    dve.wait_ge(s["m_split"], 5 * b + 1)
                    nc.vector.scalar_tensor_tensor(out=max_rest[:, 0, :], in0=minus, scalar=-1.0, in1=max_part[:, 0, :],
                                                   op0=ALU.mult, op1=ALU.subtract).then_inc(s["m_split"], 1)

                def shift_rest(b):
                    dve.wait_ge(s["m_split"], 5 * b + 2)
                    nc.vector.tensor_copy(max_part[:, 1, :], max_rest[:, 0, :]).then_inc(s["m_split"], 1)
                    dve.wait_ge(s["m_split"], 5 * b + 3)
                    nc.vector.tensor_tensor(max_rest[:, 1, :], max_rest[:, 0, :], max_part[:, 1, :],
                                            ALU.subtract).then_inc(s["m_split"], 1)
                    dve.wait_ge(s["m_split"], 5 * b + 4)
                    nc.vector.tensor_copy(max_part[:, 2, :], max_rest[:, 1, :]).then_inc(s["m_split"], 1)

                def blocks(b, ahead):
                    dve.wait_ge(s["eii_out"], b + 1)
                    dve.wait_ge(s["v_sb"], b + 1)
                    nc.vector.tensor_tensor(vn[:, :, :, :], v_raw[:, :, :, :],
                                            eii[:, :, :].unsqueeze(3).to_broadcast([P, TPB, NH, HD]),
                                            ALU.mult).then_inc(s["v_out"], 1)
                    for hd in range(NH):
                        dve.wait_ge(s["e_out"], b * SCORES + 3 * (hd + 1) + FREE_SCORES)
                        nc.vector.tensor_reduce(z_col[:, :, hd], e_nat[:, hd, :, :], AX.X, ALU.add).then_inc(s["sums_out"], 1)
                    dve.wait_ge(s["sums_out"], (b + 1) * NH)
                    nc.vector.tensor_tensor(z_col[:, :, :], z_col[:, :, :], eii[:, :, :], ALU.add).then_inc(s["z_out"], 1)
                    dve.wait_ge(s["z_out"], b * (GROUPS + 1) + 1)
                    for g in range(GROUPS):
                        dve.wait_ge(s["zoT_ps"], b * GROUPS + g + 1)
                        heads = slice(g * GROUP, (g + 1) * GROUP)
                        nc.vector.tensor_tensor(
                            z_col[:, 1:TPB, heads], z_col[:, 1:TPB, heads],
                            ps[:, ZT_BANK[g % 2], 0:3 * P].rearrange("p (t h c) -> p t h c", t=TPB - 1, c=HEAD_COLS)[:, :, :, 0],
                            ALU.add).then_inc(s["z_out"], 1)
                    if ahead:
                        normed(b + 1)
                    done = b * (BLK_STEPS + 2)
                    dve.wait_ge(s["z_loaded"], 16 * (b + 1))
                    nc.vector.reciprocal(zi_blk[:, :, :], z_blk[:, :, :]).then_inc(s["zi_out"], 1)
                    dve.wait_ge(s["zi_out"], b + 1)
                    dve.wait_ge(s["e_loaded"], 16 * (b + 1))
                    nc.vector.tensor_tensor(m_blk[:, :, :, :], e_blk[:, :, :, :],
                                            zi_blk[:, :, :].unsqueeze(3).to_broadcast([P, TPB, BLK, BLK]),
                                            ALU.mult).then_inc(s["blk_step"], 1)
                    for i in range(1, BLK):
                        dve.wait_ge(s["blk_step"], done + 2 * i - 1)
                        nc.vector.tensor_tensor(prod[:, :, 0:i, 0:i], xT_blk[:, :, 0:i, 0:i],
                                                m_blk[:, :, i, 0:i].unsqueeze(2).to_broadcast([P, TPB, i, i]),
                                                ALU.mult).then_inc(s["blk_step"], 1)
                        dve.wait_ge(s["blk_step"], done + 2 * i)
                        nc.vector.tensor_reduce(xT_blk[:, :, 0:i, i], prod[:, :, 0:i, 0:i], AX.X,
                                                ALU.add).then_inc(s["blk_step"], 1)
                    dve.wait_ge(s["blk_step"], done + BLK_STEPS + 1)
                    nc.vector.tensor_tensor(xz_blk[:, :, :, :], xT_blk[:, :, :, :],
                                            zi_blk[:, :, :].unsqueeze(3).to_broadcast([P, TPB, BLK, BLK]),
                                            ALU.mult).then_inc(s["blk_step"], 1)

                def solve(b, ahead):
                    tiles = bass.ds(b * TPB, TPB)
                    dve.wait_ge(s["ln_done"], b + 1)
                    nc.vector.tensor_tensor(x_sb[:, tiles, :], x_sb[:, tiles, :],
                                            row(core, "d_bd").unsqueeze(1).to_broadcast([P, TPB, H]),
                                            ALU.add).then_inc(s["bias_out"], 1)

                    def add_output(t):
                        dve.wait_ge(s["o_ps"], b * TPB + t + 1)
                        dve.wait_ge(s["bias_out"], b + 1)
                        nc.vector.tensor_tensor(x_sb[:, b * TPB + t, :], x_sb[:, b * TPB + t, :], ps[:, WIDE[0], 0:H],
                                                ALU.add).then_inc(s["x_out"], 1)

                    for t in range(TPB):
                        first = (b * TPB + t) * BLKS
                        earlier = 2 * (b * (TPB - 1) + t - 1)
                        heads = [slice(half * NH // 2, (half + 1) * NH // 2) for half in range(2)]
                        if t == 0:
                            dve.wait_ge(s["v_out"], b + 1)
                            nc.vector.tensor_copy(g_nat[:, :, 0:HD], vn[:, t, :, :]).then_inc(s["gn_sb"], 2)
                            if ahead:
                                own_scores(b + 1)
                        else:
                            for half in range(2):
                                dve.wait_ge(s["g_ps"], earlier + half + 1)
                                nc.vector.tensor_copy(of_half(gT, half), step_bank(half)).then_inc(s["gT_sb"], 1)
                            for half in range(2):
                                dve.wait_ge(s["gn_ps"], earlier + half + 1)
                                nc.vector.tensor_tensor(
                                    g_nat[:, heads[half], 0:HD], vn[:, t, heads[half], :],
                                    turn_bank(half).rearrange("p (h c) -> p h c", c=HEAD_COLS)[:, :, 0:HD],
                                    ALU.add).then_inc(s["gn_sb"], 1)
                            add_output(t - 1)
                        for half in range(2):
                            dve.wait_ge(s["at_ps"], 2 * first + half + 1)
                            nc.vector.tensor_copy(of_half(xg, half), step_bank(half)).then_inc(s["at_sb"], 1)
                        dve.wait_ge(s["at_sb"], 2 * first + 2)
                        dve.sem_inc(s["passed"], 1)

                        def added(half, k):
                            dve.wait_ge(s["at_ps"], 2 * (first + k) + half + 1)
                            nc.vector.tensor_tensor(of_half(aT, half), step_bank(half), of_half(xg, half),
                                                    ALU.add).then_inc(s["at_sb"], 1)

                        added(0, 1)
                        added(1, 1)
                        head, heads_beside = BESIDE[t] if ahead else (0, 0)
                        if heads_beside:
                            with dve.Fori(2, 2 + heads_beside) as k:
                                added(0, k)
                                maximum(b + 1, head + k - 2, 0)
                                maximum(b + 1, head + k - 2, 1)
                                added(1, k)
                                maximum(b + 1, head + k - 2, 2)
                                maximum(b + 1, head + k - 2, 3)
                        first_alone = 2 + heads_beside
                        if ahead and t == TPB - 1:
                            added(0, first_alone)
                            shift(b + 1)
                            added(1, first_alone)
                            shift_rest(b + 1)
                            first_alone += 1
                        if first_alone < BLKS:
                            with dve.Fori(first_alone, BLKS) as k:
                                added(0, k)
                                added(1, k)
                    add_output(TPB - 1)

                normed(0)
                values(0)
                rotated(0)
                split_parts(dve, nc.vector, qk, part, (rest, rest), s, 0)
                own_scores(0)
                for i in range(HEADS_Q):
                    maximum(0, i // TPB, i % TPB, FIRST_MAXQ)
                shift(0)
                shift_rest(0)
                with dve.Fori(0, B - 1) as b:
                    blocks(b, True)
                    values(b + 1)
                    rotated(b + 1)
                    solve(b, True)
                blocks(B - 1, False)
                solve(B - 1, False)

            @block.tensor
            def _(pe):
                pe.wait_ge(s["set"], 4)

                def turn(src, done, n=TPB, bank=MISC):
                    for t in range(n):
                        last = nc.tensor.transpose(ps[:, bank, t * P:(t + 1) * P], src(t), core.ident[:, :])
                    last.then_inc(done, 1)

                def early(b):
                    pe.wait_ge(s["ln_done"], b + 1)
                    turn(lambda t: ln["out"][:, t, :], s["hT_ps"])
                    pe.wait_ge(s["hT_sb"], b + 1)
                    for t in range(TPB):
                        last = nc.tensor.matmul(ps[:, MISC, t * H:(t + 1) * H], hT[:, t * P:(t + 1) * P],
                                                w["d_wqkv"][:, 2 * H:3 * H], start=True, stop=True)
                    last.then_inc(s["v_ps"], 1)
                    for i in range(2):
                        last = nc.tensor.matmul(ps[:, WIDE[i], :], w["d_wqkv"][:, i * H:(i + 1) * H], hT[:, :],
                                                start=True, stop=True)
                    last.then_inc(s["qk_ps"], 1)

                def own_scores(b):
                    pe.wait_ge(s["prod_out"], b + 1)
                    pe.wait_ge(s["v_sb"], b + 1)
                    for t in range(TPB):
                        last = nc.tensor.matmul(ps[:, MISC, t * NH:(t + 1) * NH], swap[:, 0, t * P:(t + 1) * P],
                                                w["head_sum"], start=True, stop=True)
                    last.then_inc(s["sii_ps"], 1)

                def operands_in(b):
                    pe.wait_ge(s["q_loaded"], 16 * PARTS * (b + 1))
                    pe.wait_ge(s["k_loaded"], 16 * (PARTS + 1) * (b + 1))

                def for_maximum(b, hd, t, banks=MAXQ):
                    n, bank = (t + 1) * P, banks[t % len(banks)]
                    pe.wait_ge(s["max_out"], b * HEADS_Q + hd * TPB + t + 1 + len(FIRST_MAXQ) - len(banks))
                    pe.sem_inc(s["passed"], 1)
                    nc.tensor.matmul(ps[:, bank, 0:n], q_op[0:QK_ROWS, hd, t * P:(t + 1) * P],
                                     k_op[0:QK_ROWS, hd, 0:n], start=True, stop=False)
                    nc.tensor.matmul(ps[:, bank, t * P:n], w["ident_b"], w["mask_up"],
                                     start=False, stop=True).then_inc(s["max_ps"], 1)

                def turn_maxima(b):
                    pe.wait_ge(s["max_out"], (b + 1) * HEADS_Q + len(FIRST_MAXQ))
                    pe.sem_inc(s["passed"], 1)
                    nc.tensor.transpose(ps[0:HEADS_Q, MAX_T, 0:P], row_max[:, :, :].rearrange("p h t -> p (h t)"),
                                        core.ident[:, :]).then_inc(s["mT_ps"], 1)

                def scores(b):
                    pe.wait_ge(s["m_loaded"], 16 * (b + 1))

                    def of_head(hd):
                        q, k = q_op[0:SHIFT_ROWS, hd, :], k_op[0:SHIFT_ROWS, hd, :]
                        i = b * SCORES + 3 * hd
                        pe.wait_ge(s["e_out"], i + 1)
                        nc.tensor.matmul(ps[:, SCORE[3 * hd % FREE_SCORES], 0:3 * P], k[:, 0:P], q[:, P:S],
                                         start=True, stop=True).then_inc(s["s_ps"], 1)
                        pe.wait_ge(s["e_out"], i + 2)
                        bank = SCORE[(3 * hd + 1) % FREE_SCORES]
                        nc.tensor.matmul(ps[:, bank, 0:2 * P], k[:, P:2 * P], q[:, 2 * P:S], start=True, stop=True)
                        nc.tensor.matmul(ps[:, bank, 2 * P:3 * P], k[:, 2 * P:3 * P], q[:, 3 * P:S],
                                         start=True, stop=True).then_inc(s["s_ps"], 1)
                        pe.wait_ge(s["e_out"], i + 3)
                        bank = SCORE[(3 * hd + 2) % FREE_SCORES]
                        nc.tensor.matmul(ps[:, bank, :], w["ident_b"], w["mask_diag4"], start=True, stop=False)
                        for t in range(TPB):
                            own = slice(t * P, (t + 1) * P)
                            last = nc.tensor.matmul(ps[:, bank, own], q[:, own], k[:, own],
                                                    start=False, stop=(t == TPB - 1))
                        last.then_inc(s["s_ps"], 1)

                    def sums(g, key_tiles):
                        if key_tiles[0] == 0:
                            pe.wait_ge(s["e_out"], b * SCORES + 3 * GROUP * (g + 1) + FREE_SCORES)
                            if g >= 2:
                                pe.wait_ge(s["zo_sb"], b * GROUPS + g - 1)
                        for j in key_tiles:
                            for hh in range(GROUP):
                                last = nc.tensor.matmul(
                                    ps[hh * HEAD_COLS:(hh + 1) * HEAD_COLS, Z_BANK[g % 2], j * P:3 * P], w["ones_f"],
                                    e_off[:, g * GROUP + hh, OFF[j]:OFF[j] + (3 - j) * P], start=(j == 0), stop=(j == 2))
                        if key_tiles[-1] == 2:
                            last.then_inc(s["zo_ps"], 1)

                    def turn_sums(g):
                        pe.wait_ge(s["zo_sb"], b * GROUPS + g + 1)
                        if g >= 2:
                            pe.wait_ge(s["z_out"], b * (GROUPS + 1) + g)
                        turn(lambda t: z_off[:, g % 2, t * P:(t + 1) * P], s["zoT_ps"], TPB - 1, ZT_BANK[g % 2])

                    for g in range(GROUPS):
                        for hh in range(GROUP):
                            of_head(g * GROUP + hh)
                            if g >= 1 and hh >= 1:
                                sums(g - 1, [hh - 1])
                        if g >= 2:
                            turn_sums(g - 2)
                    sums(GROUPS - 1, [0, 1, 2])
                    turn_sums(GROUPS - 2)
                    turn_sums(GROUPS - 1)
                    pe.wait_ge(s["z_out"], (b + 1) * (GROUPS + 1))
                    pe.sem_inc(s["passed"], 1)
                    nc.tensor.transpose(ps[0:TPB * NH, MISC, 0:P], z_col[:, :, :].rearrange("p t h -> p (t h)"),
                                        core.ident[:, :]).then_inc(s["zT_ps"], 1)
                    pe.wait_ge(s["zT_sb"], b + 1)

                def solve(b, ahead):
                    pe.wait_ge(s["x_loaded"], 16 * BLKS * (b + 1))
                    for hd in range(NH):
                        pe.wait_ge(s["masked"], b * NH + hd + 1)
                        if hd >= 2:
                            pe.wait_ge(s["mt_sb"], b * NH + hd - 1)
                        for t in range(TPB):
                            last = nc.tensor.matmul(ps[:, MT_BANK[hd % 2], t * P:(t + 1) * P], e_nat[:, hd, t, :],
                                                    xT[:, hd, t, :], start=True, stop=True)
                        last.then_inc(s["mt_ps"], 1)
                        if ahead and hd == NH // 2:
                            own_scores(b + 1)
                    pe.wait_ge(s["mt_sb"], (b + 1) * NH)
                    if ahead:
                        pe.wait_ge(s["sii_sb"], b + 2)

                    def groups_of(half):
                        return range(half * GROUPS // 2, (half + 1) * GROUPS // 2)

                    def side_by_side(half, lhs, rhs, done):
                        for j, g in enumerate(groups_of(half)):
                            for hh in range(GROUP):
                                hd = g * GROUP + hh
                                last = nc.tensor.matmul(
                                    ps[hh * HEAD_COLS:(hh + 1) * HEAD_COLS, STEP[half], j * P:(j + 1) * P],
                                    lhs(hd), rhs(hd), start=True, stop=True)
                        last.then_inc(done, 1)

                    def turn_half(half, src, done):
                        for j, g in enumerate(groups_of(half)):
                            last = nc.tensor.transpose(ps[:, TURN[half], j * P:(j + 1) * P], src[:, g, :], core.ident[:, :])
                        last.then_inc(done, 1)

                    def output(t):
                        for g in range(GROUPS):
                            last = nc.tensor.matmul(ps[:, WIDE[0], 0:H], aT[:, g, :], w["d_wd"][:, g, :],
                                                    start=(g == 0), stop=(g == GROUPS - 1))
                        last.then_inc(s["o_ps"], 1)

                    for t in range(TPB):
                        first = (b * TPB + t) * BLKS
                        if t > 0:
                            earlier = 2 * (b * (TPB - 1) + t - 1)
                            for half in range(2):
                                pe.wait_ge(s["an_sb"], 2 * first - 1 + half)
                                for n, g in enumerate(groups_of(half)):
                                    for j in range(t):
                                        c = OFF[j] + (t - 1 - j) * P
                                        for hh in range(GROUP):
                                            hd = g * GROUP + hh
                                            last = nc.tensor.matmul(
                                                ps[hh * HEAD_COLS:(hh + 1) * HEAD_COLS, STEP[half], n * P:(n + 1) * P],
                                                a_all[:, j, hd, :], e_off[:, hd, c:c + P], start=(j == 0), stop=(j == t - 1))
                                last.then_inc(s["g_ps"], 1)
                            if t > 1:
                                pe.wait_ge(s["x_out"], b * TPB + t - 1)
                            output(t - 1)
                            for half in range(2):
                                pe.wait_ge(s["gT_sb"], earlier + half + 1)
                                turn_half(half, gT, s["gn_ps"])

                        def inverse(half):
                            pe.wait_ge(s["gn_sb"], 2 * (b * TPB + t) + half + 1)
                            side_by_side(half, lambda hd: g_nat[:, hd, :], lambda hd: xT[:, hd, t, :], s["at_ps"])

                        def product(half, k):
                            pe.wait_ge(s["an_sb"], 2 * (first + k - 1) + half + 1)
                            side_by_side(half, lambda hd: a_nat[:, hd, :], lambda hd: mT[:, t, hd, :], s["at_ps"])

                        def turned(half, k, src):
                            pe.wait_ge(s["at_sb"], 2 * (first + k) + half + 1)
                            turn_half(half, src, s["an_ps"])

                        inverse(0)
                        inverse(1)
                        turned(0, 0, xg)
                        turned(1, 0, xg)
                        product(0, 1)
                        turned(0, 1, aT)
                        product(1, 1)
                        head, heads_beside = BESIDE[t] if ahead else (0, 0)
                        if heads_beside:
                            if head == 0:
                                operands_in(b + 1)
                                pe.sem_inc(s["passed"], 1)
                            with pe.Fori(2, 2 + heads_beside) as k:
                                product(0, k)
                                for_maximum(b + 1, head + k - 2, 0)
                                turned(1, k - 1, aT)
                                for_maximum(b + 1, head + k - 2, 1)
                                turned(0, k, aT)
                                product(1, k)
                                for_maximum(b + 1, head + k - 2, 2)
                                for_maximum(b + 1, head + k - 2, 3)
                        first_alone = 2 + heads_beside
                        if ahead and t == TPB - 1:
                            product(0, first_alone)
                            turn_maxima(b + 1)
                            turned(1, first_alone - 1, aT)
                            turned(0, first_alone, aT)
                            product(1, first_alone)
                            first_alone += 1
                        if first_alone < BLKS:
                            with pe.Fori(first_alone, BLKS) as k:
                                product(0, k)
                                turned(1, k - 1, aT)
                                turned(0, k, aT)
                                product(1, k)
                        turned(1, BLKS - 1, aT)
                    pe.wait_ge(s["x_out"], b * TPB + TPB - 1)
                    output(TPB - 1)
                    pe.wait_ge(s["an_sb"], 2 * BLKS * TPB * (b + 1))
                    pe.wait_ge(s["x_out"], b * TPB + TPB)

                early(0)
                own_scores(0)
                operands_in(0)
                for i in range(HEADS_Q):
                    for_maximum(0, i // TPB, i % TPB, FIRST_MAXQ)
                turn_maxima(0)
                with pe.Fori(0, B - 1) as b:
                    scores(b)
                    early(b + 1)
                    solve(b, True)
                scores(B - 1)
                solve(B - 1, False)



def store_phase(core, nc):
    stored = core.sem("stored")
    with nc.Block() as block:
        @block.sync
        def _(sp):
            sp.dma_start(core.out.rearrange("b (n p) h -> p (b n) h", p=P), core.x[:, :, :]).then_inc(stored, 16)
            sp.wait_ge(stored, 16)


@contextmanager
def semaphores_of_phase(core, nc):
    handles = []

    def allocate(name):
        handles.append(nc.alloc_semaphore(name))
        return handles[-1]

    core.sem = allocate
    yield
    core.sem = nc.alloc_semaphore
    nc.clear_and_free_semaphores(handles)
    nc.all_engine_barrier()


def build(nc, arrays, layers=(0, 1, 2, 3)):
    core = Core()
    with ExitStack() as ctx:
        core.sem = nc.alloc_semaphore
        core.dram = {}
        for name, a in arrays.items():
            core.dram[name] = nc.dram_tensor(name, a.shape, mybir.dt.from_np(a.dtype), kind="ExternalInput").ap()
        core.out = nc.dram_tensor("out_0", [B, S, H], F32, kind="ExternalOutput").ap()

        def keep(name, shape, dt=F32):
            return ctx.enter_context(nc.sbuf_tensor(name, shape, dt))

        core.x = keep("x", [P, TILES, H])[:, :, :]
        core.minus_half = keep("minus_half", [P, TPB])[:, :]
        core.w = {}
        mamba_weights = ExitStack()
        later = ("in_L0_attn_a_x", "ones", "f_w1", "f_w2")
        for name, a in sorted(arrays.items(), key=lambda item: item[0].startswith("m_")):
            if name not in later:
                core.w[name] = (mamba_weights if name.startswith("m_") else ctx).enter_context(nc.sbuf_tensor("sb_" + name, list(a.shape), mybir.dt.from_np(a.dtype)))[
                    tuple(slice(None) for _ in a.shape)]
        core.vec, core.rows, core.ident = core.w["vec"], core.w["rows"], core.w["ident"]
        core.pick = core.w["pick"]
        core.q_scr, core.k_scr = (nc.dram_tensor(n, [B, PARTS, HD, NH, S], BF16, kind="Internal").ap() for n in ("q_scr", "k_scr"))
        core.xs_scr, core.ys_scr = (nc.dram_tensor(n, [SLOTS * P, H], F32, kind="Internal").ap() for n in ("xs_scr", "ys_scr"))
        core.m_scr = nc.dram_tensor("m_scr", [B, PARTS, NH * TPB, P], BF16, kind="Internal").ap()
        core.e_scr = nc.dram_tensor("e_scr", [B, BLKS, NH, TPB, BLK, BLK], F32, kind="Internal").ap()
        core.x_scr = nc.dram_tensor("x_scr", [B, BLKS, NH, TPB, BLK, BLK], F32, kind="Internal").ap()
        core.z_scr = nc.dram_tensor("z_scr", [B, BLKS, NH, TPB, BLK], F32, kind="Internal").ap()
        load_phase(core, nc)
        if 0 in layers:
            with semaphores_of_phase(core, nc):
                mamba_phase(core, nc)
        mamba_weights.close()
        if 1 in layers:
            with semaphores_of_phase(core, nc):
                ffn_phase(core, nc, "f1_")
        if 2 in layers:
            with semaphores_of_phase(core, nc):
                delta_phase(core, nc)
        if 3 in layers:
            with semaphores_of_phase(core, nc):
                ffn_phase(core, nc, "f3_")
        store_phase(core, nc)


def kernel(**inputs):
    from concourse import bacc
    from concourse.bass_utils import run_bass_kernel_spmd

    nc = bacc.Bacc("TRN2", target_bir_lowering=False, num_devices=1)
    arrays = lay_out(inputs)
    build(nc, arrays)
    r = run_bass_kernel_spmd(nc, [arrays], core_ids=[0])
    return r.results[0]["out_0"]
```
